# Optimizing a Trainium2 kernel written in Bass

```python
import numpy as np
import jax
import jax.numpy as jnp

def _softmax(x, axis=-1):
    return jax.nn.softmax(x, axis=axis)

def _gelu(x):
    return jax.nn.gelu(x, approximate=True)

def _silu(x):
    return jax.nn.silu(x)

def _sigmoid(x):
    return jax.nn.sigmoid(x)

def _layernorm(x, axis=-1, eps=1e-05):
    m = jnp.mean(x, axis=axis, keepdims=True)
    v = jnp.var(x, axis=axis, keepdims=True)
    return (x - m) / jnp.sqrt(v + eps)

def _scatter_add(tgt, idx, src, axis=0):
    return tgt.at[idx].add(src)

def _segment_sum(src, seg, n):
    return jax.ops.segment_sum(src, seg, n)
kernel_name = 'mk_vit_tower_cls_d2_tok_img1024_r4_bbec98'

def setup_inputs(seed: int=0):
    np.random.seed(seed)
    _w = jnp.asarray

    def _rec_inputs():
        import jax
        import jax.numpy as jnp
        _rk = jax.random.key(seed)
        x = -7.10856e-05 + 0.999911 * jax.random.normal(jax.random.fold_in(_rk, 1), (4, 512, 256, 4), jnp.float32)
        cls_tok = 0.02 * jax.random.normal(jax.random.fold_in(_rk, 5), (1, 1, 256), jnp.float32)
        return (x, cls_tok)
    x, cls_tok = _rec_inputs()

    def _L0_tok_setup():
        import jax, jax.numpy as jnp
        import numpy as np
        B, S, D, E = (8, 512, 256, 4)
        DE = 512
        key = jax.random.key(seed)
        k1, k2, k3, k4 = jax.random.split(key, 4)
        scale = 1.0 / np.sqrt(D)
        return {'expert_id': 0, 'freq_features': jax.random.normal(k1, (B, S, D, E), dtype=jnp.float32), 'W0': jax.random.normal(k2, (DE, D), dtype=jnp.float32) * scale, 'W1': jax.random.normal(k3, (DE, D), dtype=jnp.float32) * scale, 'Wo': jax.random.normal(k4, (D, DE), dtype=jnp.float32) * (1.0 / np.sqrt(DE))}
    _L0_tok_all = _L0_tok_setup()
    _L0_tok_in = {k: v for k, v in _L0_tok_all.items() if k in ('W0', 'W1', 'Wo')}
    del _L0_tok_all

    def _L0_attn_setup():
        import jax, jax.numpy as jnp
        import numpy as np
        D = 256
        H = 16
        S = 512
        B = 2
        LN_EPS = 1e-05
        key = jax.random.key(seed)
        ks = jax.random.split(key, 8)
        x = jax.random.normal(ks[0], (B, S, D), dtype=jnp.float32)
        W_w = jax.random.normal(ks[1], (3 * D, D), dtype=jnp.float32) * 0.02
        W_b = jnp.zeros((3 * D,), dtype=jnp.float32)
        proj_w = jax.random.normal(ks[2], (D, D), dtype=jnp.float32) * 0.02
        proj_b = jnp.zeros((D,), dtype=jnp.float32)
        ln_g = jnp.ones((D,), dtype=jnp.float32)
        ln_b = jnp.zeros((D,), dtype=jnp.float32)
        rpb = jax.random.normal(ks[3], (2 * S - 1, H), dtype=jnp.float32)
        return {'x': x, 'W_w': W_w, 'W_b': W_b, 'proj_w': proj_w, 'proj_b': proj_b, 'ln_g': ln_g, 'ln_b': ln_b, 'rpb': rpb}
    _L0_attn_all = _L0_attn_setup()
    _L0_attn_in = {k: v for k, v in _L0_attn_all.items() if k in ('W_w', 'W_b', 'proj_w', 'proj_b', 'ln_g', 'ln_b', 'rpb')}
    del _L0_attn_all

    def _L0_ffn_setup():
        import jax, jax.numpy as jnp
        import numpy as np
        DIM = 256
        HID = 704
        N_ROUTED = 7
        TOPK = 2
        B, S = (4, 512)

        def _expert(x, wg, wu, wd):
            return jax.nn.silu(x @ wg) * (x @ wu) @ wd
        key = jax.random.key(seed)
        ks = jax.random.split(key, 9)
        s = 0.02
        x = jax.random.normal(ks[0], (B, S, DIM), jnp.float32)
        shared_gate = jax.random.normal(ks[1], (DIM, HID), jnp.float32) * s
        shared_up = jax.random.normal(ks[2], (DIM, HID), jnp.float32) * s
        shared_down = jax.random.normal(ks[3], (HID, DIM), jnp.float32) * s
        routed_gate = jax.random.normal(ks[4], (N_ROUTED, DIM, HID), jnp.float32) * s
        routed_up = jax.random.normal(ks[5], (N_ROUTED, DIM, HID), jnp.float32) * s
        routed_down = jax.random.normal(ks[6], (N_ROUTED, HID, DIM), jnp.float32) * s
        Wr = jax.random.normal(ks[7], (DIM, N_ROUTED), jnp.float32) * s
        routing_bias = jax.random.normal(ks[8], (N_ROUTED,), jnp.float32)
        return dict(x=x, shared_gate=shared_gate, shared_up=shared_up, shared_down=shared_down, routed_gate=routed_gate, routed_up=routed_up, routed_down=routed_down, Wr=Wr, routing_bias=routing_bias)
    _L0_ffn_all = _L0_ffn_setup()
    _L0_ffn_in = {k: v for k, v in _L0_ffn_all.items() if k in ('shared_gate', 'shared_up', 'shared_down', 'routed_gate', 'routed_up', 'routed_down', 'Wr', 'routing_bias')}
    del _L0_ffn_all

    def _L1_attn_setup():
        import jax, jax.numpy as jnp
        import numpy as np
        D_MODEL = 256
        N_HEADS = 16
        HEAD_DIM = D_MODEL // N_HEADS
        KV_LATENT = 64
        LN_EPS = 1e-05

        def apply_rope(x):
            b, h, t, d = x.shape
            half = d // 2
            pos = jnp.arange(t, dtype=x.dtype)[:, None]
            inv_freq = 1.0 / 10000.0 ** (jnp.arange(half, dtype=x.dtype) / half)
            angles = pos * inv_freq[None, :]
            sin = jnp.sin(angles)[None, None]
            cos = jnp.cos(angles)[None, None]
            x1, x2 = (x[..., :half], x[..., half:])
            return jnp.concatenate([x1 * cos - x2 * sin, x1 * sin + x2 * cos], axis=-1)
        key = jax.random.key(seed)
        ks = jax.random.split(key, 6)
        d, L = (D_MODEL, KV_LATENT)
        s = 1.0 / np.sqrt(d)
        sl = 1.0 / np.sqrt(L)
        return {'x': jax.random.normal(ks[0], (2, 512, d), dtype=jnp.float32), 'W_q': jax.random.uniform(ks[1], (d, d), jnp.float32, -s, s), 'W_dkv': jax.random.uniform(ks[2], (d, L), jnp.float32, -s, s), 'W_uk': jax.random.uniform(ks[3], (L, d), jnp.float32, -sl, sl), 'W_uv': jax.random.uniform(ks[4], (L, d), jnp.float32, -sl, sl), 'W_o': jax.random.uniform(ks[5], (d, d), jnp.float32, -s, s), 'ln_gamma': jnp.ones((L,), jnp.float32), 'ln_beta': jnp.zeros((L,), jnp.float32)}
    _L1_attn_all = _L1_attn_setup()
    _L1_attn_in = {k: v for k, v in _L1_attn_all.items() if k in ('W_q', 'W_dkv', 'W_uk', 'W_uv', 'W_o', 'ln_gamma', 'ln_beta')}
    del _L1_attn_all

    def _L1_ffn_setup():
        import jax, jax.numpy as jnp
        import numpy as np
        NUM_EXPERTS = 8
        TOP_K = 2
        key = jax.random.key(seed)
        ks = jax.random.split(key, 4)
        B, S, H, F = (4, 1024, 256, 1024)
        x = jax.random.normal(ks[0], (B, S, H), dtype=jnp.float32)
        router_w = jax.random.normal(ks[1], (H, NUM_EXPERTS), dtype=jnp.float32) * 0.02
        w1 = jax.random.normal(ks[2], (H, F), dtype=jnp.float32) * 0.02
        b1 = jnp.zeros((F,), dtype=jnp.float32)
        w2 = jax.random.normal(ks[3], (F, H), dtype=jnp.float32) * 0.02
        b2 = jnp.zeros((H,), dtype=jnp.float32)
        return {'x': x, 'router_w': router_w, 'w1': w1, 'b1': b1, 'w2': w2, 'b2': b2}
    _L1_ffn_all = _L1_ffn_setup()
    _L1_ffn_in = {k: v for k, v in _L1_ffn_all.items() if k in ('router_w', 'w1', 'b1', 'w2', 'b2')}
    del _L1_ffn_all
    return {'x': x, 'cls_tok': cls_tok, 'L0_tok_W0': _L0_tok_in['W0'], 'L0_tok_W1': _L0_tok_in['W1'], 'L0_tok_Wo': _L0_tok_in['Wo'], 'L0_attn_W_w': _L0_attn_in['W_w'], 'L0_attn_W_b': _L0_attn_in['W_b'], 'L0_attn_proj_w': _L0_attn_in['proj_w'], 'L0_attn_proj_b': _L0_attn_in['proj_b'], 'L0_attn_ln_g': _L0_attn_in['ln_g'], 'L0_attn_ln_b': _L0_attn_in['ln_b'], 'L0_attn_rpb': _L0_attn_in['rpb'], 'L0_ffn_shared_gate': _L0_ffn_in['shared_gate'], 'L0_ffn_shared_up': _L0_ffn_in['shared_up'], 'L0_ffn_shared_down': _L0_ffn_in['shared_down'], 'L0_ffn_routed_gate': _L0_ffn_in['routed_gate'], 'L0_ffn_routed_up': _L0_ffn_in['routed_up'], 'L0_ffn_routed_down': _L0_ffn_in['routed_down'], 'L0_ffn_Wr': _L0_ffn_in['Wr'], 'L0_ffn_routing_bias': _L0_ffn_in['routing_bias'], 'L1_attn_W_q': _L1_attn_in['W_q'], 'L1_attn_W_dkv': _L1_attn_in['W_dkv'], 'L1_attn_W_uk': _L1_attn_in['W_uk'], 'L1_attn_W_uv': _L1_attn_in['W_uv'], 'L1_attn_W_o': _L1_attn_in['W_o'], 'L1_attn_ln_gamma': _L1_attn_in['ln_gamma'], 'L1_attn_ln_beta': _L1_attn_in['ln_beta'], 'L1_ffn_router_w': _L1_ffn_in['router_w'], 'L1_ffn_w1': _L1_ffn_in['w1'], 'L1_ffn_b1': _L1_ffn_in['b1'], 'L1_ffn_w2': _L1_ffn_in['w2'], 'L1_ffn_b2': _L1_ffn_in['b2']}

def reference(x, cls_tok, L0_tok_W0, L0_tok_W1, L0_tok_Wo, L0_attn_W_w, L0_attn_W_b, L0_attn_proj_w, L0_attn_proj_b, L0_attn_ln_g, L0_attn_ln_b, L0_attn_rpb, L0_ffn_shared_gate, L0_ffn_shared_up, L0_ffn_shared_down, L0_ffn_routed_gate, L0_ffn_routed_up, L0_ffn_routed_down, L0_ffn_Wr, L0_ffn_routing_bias, L1_attn_W_q, L1_attn_W_dkv, L1_attn_W_uk, L1_attn_W_uv, L1_attn_W_o, L1_attn_ln_gamma, L1_attn_ln_beta, L1_ffn_router_w, L1_ffn_w1, L1_ffn_b1, L1_ffn_w2, L1_ffn_b2):
    import jax
    import jax.numpy as jnp

    def _L0_tok_ref(expert_id, freq_features, W0, W1, Wo):
        import jax, jax.numpy as jnp
        import numpy as np
        B, S, D, E = (8, 512, 256, 4)
        DE = 512
        x = freq_features[:, :, :, expert_id]
        gate = jax.nn.relu(jnp.einsum('bsd,ed->bse', x, W0))
        up = jnp.einsum('bsd,ed->bse', x, W1)
        hidden = gate * up
        out = jnp.einsum('bse,de->bsd', hidden, Wo)
        return out

    def _L0_attn_ref(x, W_w, W_b, proj_w, proj_b, ln_g, ln_b, rpb):
        import jax, jax.numpy as jnp
        import numpy as np
        D = 256
        H = 16
        S = 512
        B = 2
        LN_EPS = 1e-05
        b, s, d = x.shape
        hd = d // H
        qkv = x @ W_w.T + W_b
        q, k, v = jnp.split(qkv, 3, axis=-1)
        q, k, v = (z.reshape(b, s, H, hd).transpose(0, 2, 1, 3) for z in (q, k, v))
        attn = jnp.einsum('bhqd,bhkd->bhqk', q, k) / jnp.sqrt(jnp.float32(d))
        causal = jnp.triu(jnp.ones((s, s), dtype=bool), k=1)
        attn = jnp.where(causal[None, None], -jnp.inf, attn)
        rel_idx = jnp.arange(s)[None, :] - jnp.arange(s)[:, None] + (s - 1)
        bias = rpb[rel_idx].transpose(2, 0, 1)
        attn = attn + bias[None]
        w = jax.nn.softmax(attn, axis=-1)
        o = jnp.einsum('bhqk,bhkd->bhqd', w, v)
        o = o.transpose(0, 2, 1, 3).reshape(b, s, d)
        out = o @ proj_w.T + proj_b
        y = x + out
        mu = jnp.mean(y, axis=-1, keepdims=True)
        var = jnp.var(y, axis=-1, keepdims=True)
        return (y - mu) / jnp.sqrt(var + LN_EPS) * ln_g + ln_b

    def _L0_ffn_ref(x, shared_gate, shared_up, shared_down, routed_gate, routed_up, routed_down, Wr, routing_bias):
        import jax, jax.numpy as jnp
        import numpy as np
        DIM = 256
        HID = 704
        N_ROUTED = 7
        TOPK = 2
        B, S = (4, 512)

        def _expert(x, wg, wu, wd):
            return jax.nn.silu(x @ wg) * (x @ wu) @ wd
        b, s, d = x.shape
        n_exp = routed_gate.shape[0]
        shared_out = _expert(x, shared_gate, shared_up, shared_down)
        logits = x @ Wr * routing_bias
        probs = jax.nn.sigmoid(logits)
        scores, idx = jax.lax.top_k(probs, TOPK)
        scores = scores / scores.sum(-1, keepdims=True)
        t = b * s
        xf = x.reshape(t, d)
        weights = jnp.zeros((t, n_exp), x.dtype).at[jnp.arange(t)[:, None], idx.reshape(t, TOPK)].add(scores.reshape(t, TOPK))
        combined = jnp.zeros_like(xf)
        for e in range(n_exp):
            combined = combined + _expert(xf, routed_gate[e], routed_up[e], routed_down[e]) * weights[:, e:e + 1]
        return shared_out + combined.reshape(b, s, d)

    def _L1_attn_ref(x, W_q, W_dkv, W_uk, W_uv, W_o, ln_gamma, ln_beta):
        import jax, jax.numpy as jnp
        import numpy as np
        D_MODEL = 256
        N_HEADS = 16
        HEAD_DIM = D_MODEL // N_HEADS
        KV_LATENT = 64
        LN_EPS = 1e-05

        def apply_rope(x):
            b, h, t, d = x.shape
            half = d // 2
            pos = jnp.arange(t, dtype=x.dtype)[:, None]
            inv_freq = 1.0 / 10000.0 ** (jnp.arange(half, dtype=x.dtype) / half)
            angles = pos * inv_freq[None, :]
            sin = jnp.sin(angles)[None, None]
            cos = jnp.cos(angles)[None, None]
            x1, x2 = (x[..., :half], x[..., half:])
            return jnp.concatenate([x1 * cos - x2 * sin, x1 * sin + x2 * cos], axis=-1)
        b, t, _ = x.shape
        q = (x @ W_q).reshape(b, t, N_HEADS, HEAD_DIM).transpose(0, 2, 1, 3)
        lat = x @ W_dkv
        mu = jnp.mean(lat, axis=-1, keepdims=True)
        var = jnp.mean(jnp.square(lat - mu), axis=-1, keepdims=True)
        lat = (lat - mu) * jax.lax.rsqrt(var + LN_EPS) * ln_gamma + ln_beta
        k = (lat @ W_uk).reshape(b, t, N_HEADS, HEAD_DIM).transpose(0, 2, 1, 3)
        v = (lat @ W_uv).reshape(b, t, N_HEADS, HEAD_DIM).transpose(0, 2, 1, 3)
        q = apply_rope(q)
        k = apply_rope(k)
        scores = jnp.einsum('bhqd,bhkd->bhqk', q, k) / jnp.sqrt(jnp.float32(HEAD_DIM))
        causal = jnp.tril(jnp.ones((t, t), dtype=bool))
        scores = jnp.where(causal[None, None], scores, -jnp.inf)
        attn = jax.nn.softmax(scores, axis=-1)
        out = jnp.einsum('bhqk,bhkd->bhqd', attn, v)
        out = out.transpose(0, 2, 1, 3).reshape(b, t, D_MODEL)
        return out @ W_o

    def _L1_ffn_ref(x, router_w, w1, b1, w2, b2):
        import jax, jax.numpy as jnp
        import numpy as np
        NUM_EXPERTS = 8
        TOP_K = 2
        B, S, H = x.shape
        xt = x.reshape(-1, H)
        router_logits = jnp.matmul(xt, router_w)
        router_probs = jax.nn.softmax(router_logits, axis=-1)
        top_k_probs, top_k_indices = jax.lax.top_k(router_probs, TOP_K)
        top_k_probs = top_k_probs / jnp.sum(top_k_probs, axis=-1, keepdims=True)
        one_hot = jax.nn.one_hot(top_k_indices, NUM_EXPERTS, dtype=xt.dtype)
        combine = jnp.einsum('tk,tke->te', top_k_probs, one_hot)
        expert_out = jnp.matmul(jax.nn.gelu(jnp.matmul(xt, w1) + b1), w2) + b2
        out = expert_out * jnp.sum(combine, axis=-1, keepdims=True)
        return out.reshape(B, S, H)
    h = _L0_tok_ref(0, x, L0_tok_W0, L0_tok_W1, L0_tok_Wo)
    h = jnp.concatenate([jnp.broadcast_to(cls_tok, (h.shape[0], 1, h.shape[2])), h], axis=1)
    h = h + _L0_attn_ref(_layernorm(h, axis=-1), L0_attn_W_w, L0_attn_W_b, L0_attn_proj_w, L0_attn_proj_b, L0_attn_ln_g, L0_attn_ln_b, L0_attn_rpb)
    h = h + _L0_ffn_ref(_layernorm(h, axis=-1), L0_ffn_shared_gate, L0_ffn_shared_up, L0_ffn_shared_down, L0_ffn_routed_gate, L0_ffn_routed_up, L0_ffn_routed_down, L0_ffn_Wr, L0_ffn_routing_bias)
    h = h + _L1_attn_ref(_layernorm(h, axis=-1), L1_attn_W_q, L1_attn_W_dkv, L1_attn_W_uk, L1_attn_W_uv, L1_attn_W_o, L1_attn_ln_gamma, L1_attn_ln_beta)
    h = h + _L1_ffn_ref(_layernorm(h, axis=-1), L1_ffn_router_w, L1_ffn_w1, L1_ffn_b1, L1_ffn_w2, L1_ffn_b2)
    return h

_drawn_inputs = setup_inputs


def setup_inputs(seed=0):
    import zlib

    import numpy as np

    out = dict(_drawn_inputs(seed))
    spreads = {'L0_attn_W_b': (0.0, 0.357),
     'L0_attn_proj_b': (0.0, 0.1),
     'L0_attn_ln_g': (1.0, 0.2),
     'L0_attn_ln_b': (0.0, 0.1),
     'L1_attn_ln_gamma': (1.0, 0.6),
     'L1_attn_ln_beta': (0.0, 0.4),
     'L1_ffn_b1': (0.0, 0.369),
     'L1_ffn_b2': (0.0, 0.291)}
    factors = {'L0_attn_W_w': 5.537,
     'L0_attn_rpb': 8.0,
     'L0_ffn_shared_gate': 3.583,
     'L0_ffn_shared_up': 3.55,
     'L0_ffn_shared_down': 3.542,
     'L0_ffn_routed_gate': 5.007,
     'L0_ffn_routed_up': 4.96,
     'L0_ffn_routed_down': 4.952,
     'L0_ffn_Wr': 5.987,
     'L0_ffn_routing_bias': 6.951,
     'L1_attn_W_q': 6.085,
     'L1_attn_W_uk': 6.056,
     'L1_ffn_router_w': 64.0}
    for name, (base, spread) in spreads.items():
        noise = np.random.default_rng([zlib.crc32(name.encode()), seed]).standard_normal(out[name].shape)
        drawn = base * np.exp(spread * noise) if base else spread * noise
        out[name] = jnp.asarray(drawn.astype(out[name].dtype))
    for name, factor in factors.items():
        out[name] = (out[name] * factor).astype(out[name].dtype)
    return out
```

```python
import concourse.bass as bass
from concourse import mybir
from contextlib import ExitStack

F32 = mybir.dt.float32
F32R = mybir.dt.float32r
ALU = mybir.AluOpType
ACT = mybir.ActivationFunctionType
AX = mybir.AxisListType

B = 4
SX = 512
SEQ = SX + 1
SP = 516
T = B * SP
D = 256
KT = D // 128
P = 128
CH = 344
NCH = T // CH
QC = SP // 2
NQC = T // QC
H, HD = 16, 16
HG = 4
NT = (T + P - 1) // P
NEG = -1.0e30
EPS = 1e-5
HID0, NEXP0 = 704, 7
NEXP1 = 8
FF1 = 1024


def tile_start(i):
    return min(i * P, T - P)


def split_product(pe, out, w_hi, w_lo, x_hi, x_lo, start=True, stop=True, ):
    pe.matmul(out, w_hi, x_hi, start=start, stop=False, skip_group_check=True)
    pe.matmul(out, w_hi, x_lo, start=False, stop=False, skip_group_check=True)
    return pe.matmul(out, w_lo, x_hi, start=False, stop=stop, skip_group_check=True)


class Chain:

    def __init__(self, eng, sem):
        self.eng, self.sem, self.n = eng, sem, 0

    def __call__(self, ins):
        self.n += 1
        ins.then_inc(self.sem, 1)
        self.eng.wait_ge(self.sem, self.n)


class Phase:

    def __init__(self, nc, name):
        self.nc, self.name, self.stack = nc, name, ExitStack()

    def __enter__(self):
        self.stack.__enter__()
        return self

    def __exit__(self, *a):
        return self.stack.__exit__(*a)

    def sb(self, name, shape, dt=F32):
        return self.stack.enter_context(self.nc.sbuf_tensor(f"{self.name}_{name}", shape, dt))

    def ps(self, name, shape):
        return self.stack.enter_context(self.nc.psum_tensor(f"{self.name}_{name}", shape, F32))

    def sem(self, name):
        s = self.stack.enter_context(self.nc.semaphore(f"{self.name}_{name}"))
        self.used.append(s.num)
        return s

    used = []


def clear_semaphores(nc):
    with nc.Block() as block:
        @block.sync
        def _(sp):
            sp.sem_clear(range(min(Phase.used), max(Phase.used) + 1))


def layer_norm(nc, name, x, mean_w, eps, xn=None, hi=None, lo=None, gain=None, shift=None, add_to=None,
               spill=None, x_add=None, x_bias=None, width=KT):
    with Phase(nc, name) as ph:
        xc = [ph.sb(f"xc{i}", [P, width, CH]) for i in range(2)]
        sq = [ph.sb(f"sq{i}", [P, width, CH]) for i in range(2)]
        std = [ph.sb(f"std{i}", [P, CH]) for i in range(2)]
        rstd = [ph.sb(f"rstd{i}", [P, CH]) for i in range(2)]
        mean_ps = [ph.ps(f"mean{i}", [P, 512]) for i in range(2)]
        var_ps = [ph.ps(f"var{i}", [P, 512]) for i in range(2)]
        mean_done, centred, squared, var_done, std_done, normed, hi_done, own, own2, stored = (
            ph.sem(n) for n in ("mean", "centred", "squared", "var", "stdd", "normed", "hid", "own", "own2", "st"))

        def cols(t, c):
            return t[:, :, c * CH:(c + 1) * CH]

        def spread(t):
            return t.unsqueeze(1).to_broadcast([P, width, CH])

        with nc.Block() as block:
            @block.tensor
            def _(pe):
                def mean(c):
                    if c >= 2:
                        pe.wait_ge(centred, c - 1)
                    for k in range(width):
                        mm = pe.matmul(mean_ps[c % 2][:, 0:CH], mean_w, cols(x, c)[:, k, :],
                                       start=(k == 0), stop=(k == width - 1))
                    mm.then_inc(mean_done, 1)

                def var(c):
                    pe.wait_ge(squared, c + 1)
                    for k in range(width):
                        mm = pe.matmul(var_ps[c % 2][:, 0:CH], mean_w, sq[c % 2][:, k, :],
                                       start=(k == 0), stop=(k == width - 1))
                    mm.then_inc(var_done, 1)

                mean(0)
                for c in range(NCH):
                    if c + 1 < NCH:
                        mean(c + 1)
                    var(c)

            @block.scalar
            def _(act):
                for c in range(NCH):
                    act.wait_ge(centred, c + 1)
                    if c >= 2:
                        act.wait_ge(var_done, c - 1)
                    act.activation(sq[c % 2][:, :, :], xc[c % 2][:, :, :], ACT.Square).then_inc(squared, 1)
                    act.wait_ge(var_done, c + 1)
                    if c >= 2:
                        act.wait_ge(normed, c - 1)
                    act.activation(std[c % 2][:, :], var_ps[c % 2][:, 0:CH], ACT.Sqrt, bias=eps)\
                       .then_inc(std_done, 1)
                    if hi is not None:
                        act.wait_ge(normed, c + 1)
                        act.activation(cols(hi, c), cols(xn, c), ACT.Copy).then_inc(hi_done, 1)

            @block.vector
            def _(dve):
                step = Chain(dve, own)

                def centre(c):
                    dve.wait_ge(mean_done, c + 1)
                    if c >= 2:
                        dve.wait_ge(squared, c - 1)
                    dve.tensor_tensor(xc[c % 2][:, :, :], cols(x, c), spread(mean_ps[c % 2][:, 0:CH]),
                                      ALU.subtract).then_inc(centred, 1)

                centre(0)
                for c in range(NCH):
                    if c + 1 < NCH:
                        centre(c + 1)
                    dve.wait_ge(std_done, c + 1)
                    dve.reciprocal(rstd[c % 2][:, :], std[c % 2][:, :]).then_inc(own2, 1)
                    dve.wait_ge(own2, c + 1)
                    dve.wait_ge(centred, c + 1)
                    last = dve.tensor_tensor(cols(xn, c), xc[c % 2][:, :, :], spread(rstd[c % 2][:, :]), ALU.mult)
                    if gain is not None:
                        step(last)
                        for k in range(width):
                            last = dve.tensor_scalar(cols(xn, c)[:, k, :], cols(xn, c)[:, k, :], gain[:, k:k + 1],
                                                     shift[:, k:k + 1], ALU.mult, ALU.add)
                            if k < width - 1:
                                step(last)
                    last.then_inc(normed, 1)
                    if add_to is not None:
                        dve.wait_ge(normed, c + 1)
                        dve.tensor_tensor(cols(add_to, c), cols(add_to, c), cols(xn, c), ALU.add)
                    if hi is not None:
                        dve.wait_ge(hi_done, c + 1)
                        dve.tensor_tensor(cols(lo, c), cols(xn, c), cols(hi, c).bitcast(F32), ALU.subtract)

            if spill is not None:
                @block.sync
                def _(sp):
                    for c in range(NCH):
                        sp.wait_ge(normed, c + 1)
                        sp.dma_start(spill[:, :, c * CH:(c + 1) * CH], cols(xn, c)).then_inc(stored, 16)
                    sp.wait_ge(stored, 16 * NCH)


def split_weights(nc, name, loads):
    with Phase(nc, name) as ph:
        got = [ph.sem(f"got{i}") for i in range(len(loads))]
        hi_done = ph.sem("hid")
        with nc.Block() as block:
            @block.sync
            def _(sp):
                for s, (raw, src, _, _) in zip(got, loads):
                    sp.dma_start(raw, src).then_inc(s, 16)

            @block.scalar
            def _(act):
                for s, (raw, _, hi, _) in zip(got, loads):
                    act.wait_ge(s, 16)
                    if hi is not None:
                        act.activation(hi, raw, ACT.Copy).then_inc(hi_done, 1)

            @block.vector
            def _(dve):
                n = 0
                for s, (raw, _, hi, lo) in zip(got, loads):
                    dve.wait_ge(s, 16)
                    if hi is not None:
                        n += 1
                        dve.wait_ge(hi_done, n)
                        dve.tensor_tensor(lo, raw, hi.bitcast(F32), ALU.subtract)


def gated_ffn(nc, name, *, x_hi, x_lo, chunks, J, half, gated, func, experts, load, w_mult, finish,
              lag, up_bias=None, out_bias=None, store=None):
    NC = len(chunks)
    N = chunks[0][1]
    GU = 2 * J if gated else J
    if half:
        GU -= 1
    FULL = J - 1 if half else J
    PASSES = 2 if experts > 1 else 1
    S = PASSES * NC * J
    with Phase(nc, name) as ph:
        raw1 = ph.sb("raw1", [P, KT, GU * P])
        raw2 = ph.sb("raw2", [P, J, D])
        w1 = [[ph.sb(f"w1{p}{q}", [P, KT, GU * P], F32R) for q in "hl"] for p in range(PASSES)]
        w2 = [[ph.sb(f"w2{p}{q}", [P, J, D], F32R) for q in "hl"] for p in range(PASSES)]
        hid_hi = ph.sb("hidhi", [P, J, N], F32R)
        hid_lo = ph.sb("hidlo", [P, J, N], F32R)
        gate_sb = [ph.sb(f"gate{i}", [P, N]) for i in range(2)]
        up_half = ph.sb("uphalf", [64, N]) if half else None
        hidden = [ph.sb(f"hidden{i}", [P, N]) for i in range(2)]
        out_sb = [ph.sb(f"out{i}", [P, KT, N]) for i in range(2)]
        factor = [ph.sb(f"factor{p}", [P, T]) for p in range(PASSES)] if w_mult is not None else None
        gu_ps = [ph.ps(f"gu{i}", [P, 2, 512]) for i in range(3)]
        out_ps = ph.ps("outps", [P, KT, 512])
        raw_in, raw2_in, split_done, cleared, own = (ph.sem(n) for n in ("raw", "raw2", "split", "clear", "own"))
        gu_done, gate_done, hid_made, hi_done, lo_done, down_done, out_done, evacuated, added, up_done = (
            ph.sem(n) for n in ("gu", "gated", "hid", "hi", "lo", "down", "outd", "evac", "added", "updone"))
        factor_in = [ph.sem(f"factor{p}") for p in range(PASSES)] if factor else None
        stored = ph.sem("stored")

        def turns(eng, body):
            if experts > 1:
                with eng.Fori(0, experts // PASSES) as it:
                    body(it)
            else:
                body(0)

        def where(s):
            return s // (NC * J), s // J % NC, s % J

        def is_half(s):
            return half and s % J == J - 1

        with nc.Block() as block:
            @block.sync
            def _(sp):
                for e in range(experts):
                    if e >= 1:
                        sp.wait_ge(split_done, e)
                    n = 0
                    for dst, src in load(e, raw1, raw2):
                        sp.dma_start(dst, src).then_inc(raw_in, 16)
                        n += 1
                    if factor:
                        if e >= PASSES:
                            sp.wait_ge(evacuated, (e - PASSES + 1) * NC)
                        sp.dma_start(factor[e % PASSES][:, :], w_mult(e)).then_inc(factor_in[e % PASSES], 16)

            @block.gpsimd
            def _(pool):
                step = Chain(pool, own)
                if half:
                    step(pool.memset(hid_hi[64:P, J - 1, :].bitcast(F32), 0.0))
                    step(pool.memset(hid_lo[64:P, J - 1, :].bitcast(F32), 0.0))
                    pool.memset(raw2[64:P, J - 1, :], 0.0).then_inc(cleared, 1)
                    pool.wait_ge(cleared, 1)

                n_raw = len(load(0, raw1, raw2))

                def pieces(e):
                    p = e % PASSES
                    W = GU * P // 4
                    out = [(raw1[:, :, i * W:(i + 1) * W], w1[p][0][:, :, i * W:(i + 1) * W],
                            w1[p][1][:, :, i * W:(i + 1) * W]) for i in range(4)]
                    J2 = J // 2
                    out += [(raw2[:, a:b, :], w2[p][0][:, a:b, :], w2[p][1][:, a:b, :])
                            for a, b in ((0, J2), (J2, J))]
                    return out

                def split(e, i):
                    if i == 0:
                        pool.wait_ge(raw_in, 16 * n_raw * (e + 1))
                        if e >= PASSES:
                            pool.wait_ge(out_done, (e - PASSES + 1) * NC)
                    raw, hi, lo = pieces(e)[i]
                    step(pool.tensor_copy(hi, raw))
                    last = pool.tensor_tensor(lo, raw, hi.bitcast(F32), ALU.subtract)
                    if i == 5:
                        last.then_inc(split_done, 1)

                for i in range(6):
                    split(0, i)
                for e in range(experts):
                    for c in range(NC):
                        if e + 1 < experts:
                            split(e + 1, c)
                        pool.wait_ge(evacuated, e * NC + c + 1)
                        dst = finish(c)
                        if store is None:
                            ins = pool.tensor_tensor(dst, dst, out_sb[c % 2][:, :, :], ALU.add)
                        else:
                            ins = pool.tensor_copy(dst, out_sb[c % 2][:, :, :])
                        ins.then_inc(added, 1)

            @block.tensor
            def _(pe):
                def first(it, s):
                    p, c, j = where(s)
                    if c == 0 and j == 0:
                        pe.wait_ge(split_done, it * PASSES + p + 1)
                    if s >= 3:
                        pe.wait_ge(hid_made, it * S + s - 2)
                    a, n = chunks[c]
                    tiles = [(0, j)]
                    if gated and not is_half(s):
                        tiles.append((1, FULL + j))
                    if is_half(s):
                        tiles = [(0, 2 * FULL)]
                    for g, m in tiles:
                        for k in range(KT):
                            w = [w1[p][q][:, k, m * P:(m + 1) * P] for q in range(2)]
                            mm = split_product(pe, gu_ps[s % 3][:, g, 0:N], w[0], w[1], x_hi[:, k, a:a + n],
                                               x_lo[:, k, a:a + n], k == 0, k == KT - 1)
                    mm.then_inc(gu_done, 1)

                def down(it, s):
                    p, c, j = where(s)
                    pe.wait_ge(lo_done, it * S + s + 1)
                    if j == 0:
                        pe.wait_ge(evacuated, it * PASSES * NC + s // J)
                    for m in range(KT):
                        w = [w2[p][q][:, j, m * P:(m + 1) * P] for q in range(2)]
                        mm = split_product(pe, out_ps[:, m, 0:N], w[0], w[1], hid_hi[:, j, :],
                                           hid_lo[:, j, :], j == 0, j == J - 1)
                    if j == J - 1:
                        mm.then_inc(out_done, 1)
                    else:
                        mm.then_inc(down_done, 1)

                def body(it):
                    for s in range(S + lag):
                        if s < S:
                            first(it, s)
                        if s >= lag:
                            down(it, s - lag)

                if half:
                    pe.wait_ge(cleared, 1)
                turns(pe, body)

            def slot_free(eng, it, s):
                if s >= J:
                    q = s - J
                    if q % J == J - 1:
                        eng.wait_ge(out_done, it * (S // J) + q // J + 1)
                    else:
                        eng.wait_ge(down_done, it * (S // J) * (J - 1) + q // J * (J - 1) + q % J + 1)

            @block.scalar
            def _(act):
                def body(it):
                    for s in range(S + 1):
                        if s < S:
                            act.wait_ge(gu_done, it * S + s + 1)
                            r = 64 if is_half(s) else P
                            src = gu_ps[s % 3][0:r, 0, 0:N]
                            if gated:
                                if s >= 2:
                                    act.wait_ge(hid_made, it * S + s - 1)
                                ins = act.activation(gate_sb[s % 2][0:r, :], src, func)
                                ins.then_inc(gate_done, 1)
                                if is_half(s):
                                    act.activation(up_half[:, :], gu_ps[s % 3][64:P, 0, 0:N], ACT.Copy)\
                                       .then_inc(up_done, 1)
                            else:
                                if s >= 2:
                                    act.wait_ge(lo_done, it * S + s - 1)
                                act.activation(hidden[s % 2][:, :], src, func, bias=up_bias[:, s % J:s % J + 1])\
                                   .then_inc(hid_made, 1)
                        if gated and s >= 1:
                            q = s - 1
                            r = 64 if is_half(q) else P
                            act.wait_ge(hid_made, it * S + q + 1)
                            slot_free(act, it, q)
                            act.activation(hid_hi[0:r, q % J, :], hidden[q % 2][0:r, :], ACT.Copy)\
                               .then_inc(hi_done, 1)
                turns(act, body)

            @block.vector
            def _(dve):
                def low(it, q):
                    r = 64 if is_half(q) else P
                    if not gated:
                        dve.wait_ge(hid_made, it * S + q + 1)
                        slot_free(dve, it, q)
                        dve.tensor_copy(hid_hi[:, q % J, :], hidden[q % 2][:, :]).then_inc(hi_done, 1)
                    dve.wait_ge(hi_done, it * S + q + 1)
                    dve.tensor_tensor(hid_lo[0:r, q % J, :], hidden[q % 2][0:r, :],
                                      hid_hi[0:r, q % J, :].bitcast(F32), ALU.subtract).then_inc(lo_done, 1)

                def evacuate(it, n):
                    p, c = n // NC, n % NC
                    a, _ = chunks[c]
                    dve.wait_ge(out_done, it * PASSES * NC + n + 1)
                    if n >= 2:
                        dve.wait_ge(added, it * PASSES * NC + n - 1)
                    elif experts > 1:
                        dve.wait_ge(added, it * PASSES * NC)
                    if factor and c == 0:
                        dve.wait_ge(factor_in[p], 16 * it + 16)
                    dst = out_sb[n % 2]
                    if out_bias is not None:
                        for m in range(KT):
                            ins = dve.scalar_tensor_tensor(out=dst[:, m, :], in0=out_ps[:, m, 0:N],
                                                           scalar=out_bias[:, m:m + 1],
                                                           in1=factor[p][:, a:a + N], op0=ALU.add, op1=ALU.mult)
                    elif factor:
                        f = factor[p][:, a:a + N].unsqueeze(1).to_broadcast([P, KT, N])
                        ins = dve.tensor_tensor(dst[:, :, :], out_ps[:, :, 0:N], f, ALU.mult)
                    else:
                        ins = dve.tensor_copy(dst[:, :, :], out_ps[:, :, 0:N])
                    ins.then_inc(evacuated, 1)

                def body(it):
                    if gated:
                        for s in range(S + 1):
                            if s < S:
                                dve.wait_ge(gate_done, it * S + s + 1)
                                if s >= 2:
                                    dve.wait_ge(lo_done, it * S + s - 1)
                                    dve.wait_ge(hi_done, it * S + s - 1)
                                if is_half(s):
                                    dve.wait_ge(up_done, it * PASSES * NC + s // J + 1)
                                    dve.tensor_tensor(hidden[s % 2][0:64, :], up_half[:, :], gate_sb[s % 2][0:64, :],
                                                      ALU.mult).then_inc(hid_made, 1)
                                else:
                                    dve.tensor_tensor(hidden[s % 2][:, :], gu_ps[s % 3][:, 1, 0:N],
                                                      gate_sb[s % 2][:, :], ALU.mult).then_inc(hid_made, 1)
                            if s >= 1:
                                low(it, s - 1)
                            done = s + 1 - J - lag
                            if done >= 0 and done % J == 0:
                                evacuate(it, done // J)
                        for n in range(PASSES * NC):
                            if n * J + J + lag - 1 > S:
                                evacuate(it, n)
                    else:
                        n = 0
                        for s in range(S):
                            low(it, s)
                            done = s + 1 - J - lag
                            if done >= 0 and done % J == 0:
                                evacuate(it, done // J)
                                n += 1
                        for m in range(n, PASSES * NC):
                            evacuate(it, m)

                turns(dve, body)


def attention(nc, name, *, q_scr, k_scr, v_scr, o_scr, m_scr, scale, toeplitz, consts, v_bias):
    NB = 4
    UNITS = 8
    QA = 256
    QB = SP - QA
    PW = QA + 128 + 3 * QB + (SP - 384) + 4
    with Phase(nc, name) as ph:
        qst = [ph.sb(f"q{i}", [P, HG, SP], F32R) for i in range(NB)]
        kst = [ph.sb(f"k{i}", [P, HG, SP], F32R) for i in range(NB)]
        vst = [ph.sb(f"v{i}", [P, 5, HG, 32]) for i in range(NB)]
        prob = [ph.sb(f"prob{i}", [P, HG, PW]) for i in range(2)]
        mx = [ph.sb(f"mx{i}", [P, 32]) for i in range(2)]
        mneg = [ph.sb(f"mneg{i}", [P, 32], F32R) for i in range(2)]
        mxt = [ph.sb(f"mxt{i}", [P, 32], F32R) for i in range(2)]
        o_sb = ph.sb("osb", [P, SP])
        rec = ph.sb("rec", [P, SP])
        o_n = [ph.sb(f"on{i}", [P, SP]) for i in range(2)]
        max_ps = ph.ps("max", [P, 2, 512])
        s_ps = ph.ps("s", [P, 4, 512])
        o_ps = ph.ps("o", [P, 2, 512])
        ident, flip, sums, diag, tail, mask2, row48 = (
            consts[n] for n in ("ident", "flip", "sums", "diag", "tail", "mask2", "row48"))
        q_in = [ph.sem(f"qin{i}") for i in range(NB)]
        ready, max_mm, max_read, m_made, m_in0, m_in1, m_out, s_mm, exp_done, pv_done, o_copied, sum_mm, rec_done, o_done, o_out0, o_out1, own, pown = (
            ph.sem(n) for n in ("ready", "maxmm", "maxrd", "mmade", "min0", "min1", "mout", "smm", "exp", "pv", "ocp",
                                "summ", "recd", "odone", "oout0", "oout1", "own", "pown"))
        m_in = [m_in0, m_in1]
        o_out = [o_out0, o_out1]
        LOADS = 4
        ML = 2
        NU = B * H // HG

        def unit(u):
            return u // B, u % B

        MAXES = 4
        with nc.Block() as block:
            @block.gpsimd
            def _(pool):
                step = Chain(pool, pown)
                step(pool.memset(o_sb[:, :], 0.0))
                for i in range(NB):
                    step(pool.memset(qst[i][:, :, :].bitcast(F32), 0.0))
                    step(pool.memset(kst[i][:, :, :].bitcast(F32), 0.0))
                for i in range(2):
                    step(pool.memset(mx[i][:, :], 0.0))
                for i in range(NB):
                    for h in range(HG):
                        ins = pool.tensor_scalar(kst[i][32:64, h, :], o_sb[32:64, :], row48[32:64, :], None, ALU.add)
                        if (i, h) != (NB - 1, HG - 1):
                            step(ins)
                ins.then_inc(ready, 1)

                for u in range(NU):
                    hg, b = unit(u)
                    pool.wait_ge(rec_done, u + 1)
                    if u >= 2:
                        pool.wait_ge(o_out[u % 2], 16 * (u // 2))
                    ins = pool.tensor_tensor(o_n[u % 2][:, :], o_sb[:, :], rec[:, :], ALU.mult)
                    if v_bias is not None:
                        step(ins)
                        ins = pool.tensor_scalar(o_n[u % 2][:, :], o_n[u % 2][:, :], v_bias[:, hg:hg + 1], None, ALU.add)
                    ins.then_inc(o_done, 1)

            @block.sync
            def _(sp):
                sp.wait_ge(ready, 1)

                def load(u):
                    hg, b = unit(u)
                    i = u % NB
                    if u >= NB:
                        sp.wait_ge(pv_done, u - NB + 1)
                    for scr, tiles, r, n in ((q_scr, qst, 3 * HD + 1, SEQ), (k_scr, kst, 3 * HD, SP)):
                        sp.dma_start(tiles[i][0:r, :, 0:n].bitcast(F32),
                                     scr[hg * HG:(hg + 1) * HG, :, b * SP:b * SP + n].rearrange("h r t -> r h t"))\
                          .then_inc(q_in[i], 16)
                    cols = slice(hg * HG * 32, (hg + 1) * HG * 32)
                    sp.dma_start(vst[i][:, 0:4, :, :].rearrange("p n h c -> p n (h c)"),
                                 v_scr[b * SP:b * SP + 512, cols].rearrange("(n p) c -> p n c", p=P))\
                      .then_inc(q_in[i], 16)
                    sp.dma_start(vst[i][:, 4, :, :].rearrange("p h c -> p (h c)"),
                                 v_scr[(b + 1) * SP - P:(b + 1) * SP, cols]).then_inc(q_in[i], 16)

                def maxima(u):
                    i, scr = u % NB, m_scr[u % 2]
                    sp.wait_ge(m_made, u + 1)
                    sp.dma_start(scr.rearrange("(r k) f -> k r f", k=4), mxt[u % 2][:, :].bitcast(F32)).then_inc(m_out, 16)
                    sp.wait_ge(m_out, 16 * (u + 1))
                    row = qst[i][3 * HD:3 * HD + 1, :, :].bitcast(F32)
                    sp.dma_start(row[:, :, 1:SEQ], scr[0:64].rearrange("(o h n) f -> o h (n f)", o=1, h=HG))\
                      .then_inc(m_in[u % 2], 16)
                    sp.dma_start(row[:, :, 0:1], scr.rearrange("(o r k) f -> o r k f", k=4, o=1)[:, 16:16 + HG, 0, 0:1],
                                 allow_slow_non_contiguous=True).then_inc(m_in[u % 2], 16)

                def store(u):
                    hg, b = unit(u)
                    sp.wait_ge(o_done, u + 1)
                    sp.dma_start(o_scr[hg * P:(hg + 1) * P, b * SP:b * SP + SEQ], o_n[u % 2][:, 0:SEQ])\
                      .then_inc(o_out[u % 2], 16)

                for u in range(min(3, NU)):
                    load(u)
                for u in range(NU + 1):
                    if u + 3 < NU:
                        load(u + 3)
                    if u >= 1:
                        store(u - 1)
                    if toeplitz is not None and u == B + 1:
                        sp.wait_ge(s_mm, 2 * HG * B)
                        sp.wait_ge(max_read, 4 * HG * B)
                        toeplitz["load"](sp, 2)
                    if toeplitz is not None and u == 2 * B:
                        toeplitz["load"](sp, 3)
                    if u % UNITS == 0 and u < NU:
                        maxima(u)
                        maxima(u + 1)
                    if u < NU and u % UNITS + 2 < UNITS:
                        maxima(u + 2)
                for i in range(2):
                    sp.wait_ge(o_out[i], 16 * (NU // 2))

            @block.tensor
            def _(pe):
                def maxima_mm(it, u, h):
                    i = u % NB
                    if h == 0:
                        pe.wait_ge(q_in[i], it * (UNITS // NB) * 16 * LOADS + (u // NB + 1) * 16 * LOADS)
                    n = (u * HG + h) * MAXES
                    base = it * UNITS * HG * MAXES
                    pe.wait_ge(max_read, base + n)
                    pe.matmul(max_ps[:, 0, 508:510], qst[i][:, h, 0:P], kst[i][:, h, 0:2], start=True, stop=True)
                    pe.matmul(max_ps[:, 0, 0:130], qst[i][:, h, 1:1 + P], kst[i][:, h, 0:130], start=True, stop=True)
                    pe.matmul(max_ps[:, 0, 130:388], qst[i][:, h, 129:129 + P], kst[i][:, h, 0:258],
                              start=True, stop=True).then_inc(max_mm, 1)
                    pe.matmul(max_ps[:, 1, 0:386], qst[i][:, h, 257:257 + P], kst[i][:, h, 0:386],
                              start=True, stop=True).then_inc(max_mm, 1)
                    pe.wait_ge(max_read, base + n + 2)
                    pe.matmul(max_ps[:, 0, 0:QC], qst[i][:, h, 385:385 + P], kst[i][:, h, 0:QC],
                              start=True, stop=True)
                    pe.wait_ge(max_read, base + n + 3)
                    pe.matmul(max_ps[:, 1, 0:QC], qst[i][:, h, 385:385 + P], kst[i][:, h, QC:SP],
                              start=True, stop=True).then_inc(max_mm, 1)

                def scores(it, u, h):
                    i = u % NB
                    n = it * UNITS * HG + u * HG + h
                    slot = (u // B) % 2
                    if h == 0:
                        pe.wait_ge(m_in[u % 2], it * (UNITS // 2) * 16 * ML + (u // 2 + 1) * 16 * ML)
                        if toeplitz is not None and u % B == 0:
                            pe.wait_ge(toeplitz["loaded"][slot], 16 * toeplitz["n"] * (it + 1))

                    def piece(out, k0, q0, nq):
                        diagonal = q0 <= k0 + P - 1
                        more = toeplitz is not None or diagonal
                        mm = pe.matmul(out, kst[i][:, h, k0:k0 + P], qst[i][:, h, q0:q0 + nq],
                                       start=True, stop=not more, skip_group_check=True)
                        if k0 % P:
                            if toeplitz is not None:
                                for part in ("hi", "lo"):
                                    pe.matmul(out, flip, toeplitz["tail_" + part][slot][:, h, :], start=False,
                                              stop=False, skip_group_check=True)
                            mm = pe.matmul(out, ident, tail, start=False, stop=True, skip_group_check=True)
                        elif toeplitz is not None:
                            for part in ("hi", "lo"):
                                a = q0 - k0
                                mm = pe.matmul(out, flip, toeplitz[part][slot][:, h, a:a + nq], start=False,
                                               stop=(part == "lo"), skip_group_check=True)
                        elif diagonal:
                            mm = pe.matmul(out[:, 0:P], ident, diag, start=False, stop=True, skip_group_check=True)
                        return mm

                    if (u, h) == (0, 0):
                        pe.wait_ge(exp_done, 2 * n)
                    else:
                        pe.wait_ge(exp_done, 2 * n - 1)
                    piece(s_ps[:, 0, 0:QA], 0, 0, QA)
                    piece(s_ps[:, 0, QA:QA + P], P, P, P).then_inc(s_mm, 1)
                    pe.wait_ge(exp_done, 2 * n)
                    piece(s_ps[:, 1, 0:QB], 0, QA, QB)
                    piece(s_ps[:, 2, 0:QB], P, QA, QB)
                    piece(s_ps[:, 3, 0:QB], 2 * P, QA, QB)
                    piece(s_ps[:, 1, QB:QB + SP - 384], 3 * P, 384, SP - 384)
                    piece(s_ps[:, 2, QB:QB + 4], SP - P, 512, 4).then_inc(s_mm, 1)

                def values(it, u):
                    i = u % NB
                    pr = prob[u % 2]
                    n = it * UNITS + u
                    pe.wait_ge(exp_done, it * UNITS * HG * 2 + (u + 1) * HG * 2)
                    pe.wait_ge(rec_done, n)
                    at = QA + P
                    plan = [(0, 0, 0, QA, 0), (0, 1, P, P, QA)]
                    plan += [(1, t, 0, QB, at + t * QB) for t in range(3)]
                    plan += [(1, 3, P, QB - P, at + 3 * QB), (1, 4, QA, 4, at + 3 * QB + SP - 384)]
                    for bank, t, c0, w, src in plan:
                        for h in range(HG):
                            mm = pe.matmul(o_ps[32 * h:32 * h + 32, bank, c0:c0 + w], vst[i][:, t, h, :],
                                           pr[:, h, src:src + w], start=(t == 0), stop=(t == (1 if bank == 0 else 4)),
                                           skip_group_check=True)
                    mm.then_inc(pv_done, 1)

                def spread_sums(it, u):
                    n = it * UNITS + u
                    pe.wait_ge(o_copied, n + 1)
                    pe.matmul(o_ps[:, 0, 0:QC], sums, o_sb[:, 0:QC], start=True, stop=True)
                    pe.matmul(o_ps[:, 1, 0:QC], sums, o_sb[:, QC:SP], start=True, stop=True).then_inc(sum_mm, 1)

                with pe.Fori(0, NU // UNITS) as it:
                    for u in range(2):
                        for h in range(HG):
                            maxima_mm(it, u, h)
                    for u in range(UNITS + 1):
                        for h in range(HG):
                            if u < UNITS:
                                scores(it, u, h)
                            if h == 0 and u >= 1:
                                values(it, u - 1)
                            if h == 2 and u >= 1:
                                spread_sums(it, u - 1)
                            if u + 2 < UNITS:
                                maxima_mm(it, u + 2, h)

            @block.scalar
            def _(act):
                def exps(it, u, h):
                    n = it * UNITS * HG + u * HG + h
                    pr = prob[u % 2]
                    at = QA + P
                    if h == 0 and u >= 2:
                        act.wait_ge(pv_done, it * UNITS + u - 1)
                    act.wait_ge(s_mm, 2 * n + 1)
                    act.activation(pr[:, h, 0:at], s_ps[:, 0, 0:at], ACT.Exp, scale=scale).then_inc(exp_done, 1)
                    act.wait_ge(s_mm, 2 * n + 2)
                    act.activation(pr[:, h, at:at + 3 * QB].rearrange("p (t q) -> p t q", t=3), s_ps[:, 1:4, 0:QB],
                                   ACT.Exp, scale=scale)
                    at += 3 * QB
                    act.activation(pr[:, h, at:at + SP - 384], s_ps[:, 1, QB:QB + SP - 384], ACT.Exp, scale=scale)
                    at += SP - 384
                    act.activation(pr[:, h, at:at + 4], s_ps[:, 2, QB:QB + 4], ACT.Exp, scale=scale)\
                       .then_inc(exp_done, 1)

                def copy_out(it, u):
                    n = it * UNITS + u
                    act.wait_ge(pv_done, n + 1)
                    act.wait_ge(o_done, n)
                    act.activation(o_sb[:, 0:QA], o_ps[:, 0, 0:QA], ACT.Copy)
                    act.activation(o_sb[:, QA:SP], o_ps[:, 1, 0:QB], ACT.Copy).then_inc(o_copied, 1)

                with act.Fori(0, NU // UNITS) as it:
                    for u in range(UNITS + 1):
                        for h in range(HG):
                            if u < UNITS:
                                exps(it, u, h)
                            if h == 0 and u >= 1:
                                copy_out(it, u - 1)

            @block.vector
            def _(dve):
                def bias2(slot, h):
                    return toeplitz["max"][slot][:, h, :] if toeplitz is not None else mask2

                def maxima(it, u, h):
                    slot = (u // B) % 2
                    m = mx[u % 2]
                    base = it * UNITS * HG * 3 + (u * HG + h) * 3
                    t2 = bias2(slot, h)
                    if h == 0:
                        dve.wait_ge(ready, 1)
                        if toeplitz is not None and u % B == 0:
                            dve.wait_ge(toeplitz["loaded"][slot], 16 * toeplitz["n"] * (it + 1))
                        if u >= 2:
                            dve.wait_ge(m_in[u % 2], it * (UNITS // 2) * 16 * ML + (u // 2) * 16 * ML)
                        else:
                            dve.wait_ge(m_in[u % 2], it * (UNITS // 2) * 16 * ML)
                    dve.wait_ge(max_mm, base + 2)
                    dve.tensor_tensor(m[0:1, 16 + h:17 + h], max_ps[0:1, 0, 508:509], t2[0:1, 385:386], ALU.add)\
                       .then_inc(max_read, 1)

                    def piece(i, src):
                        w = src.shape[-1] * (2 if len(src.shape) == 3 else 1)
                        a = 384 - 128 * i
                        b2 = t2[:, a:a + w]
                        if len(src.shape) == 3:
                            b2 = b2.rearrange("p (a c) -> p a c", a=2)
                        return dve.tensor_tensor_reduce(src, src, b2, 1.0, 3.0 * NEG, ALU.add, ALU.max,
                                                        m[:, 4 * h + i:4 * h + i + 1])

                    piece(0, max_ps[:, 0, 0:130])
                    piece(1, max_ps[:, 0, 130:388]).then_inc(max_read, 1)
                    piece(2, max_ps[:, 1, 0:386])\
                        .then_inc(max_read, 1)
                    dve.wait_ge(max_mm, base + 3)
                    dve.memset(m[:, 31:32], 0.0)
                    piece(3, max_ps[:, :, 0:QC]).then_inc(max_read, 1)

                def turn_maxima(it, u):
                    done = it * UNITS * HG * MAXES + (u + 1) * HG * MAXES
                    dve.wait_ge(max_read, done)
                    dve.tensor_scalar(mneg[u % 2][:, :], mx[u % 2][:, :], -1.0, None, ALU.mult).then_inc(own, 1)
                    dve.wait_ge(own, it * UNITS + u + 1)
                    dve.transpose(mxt[u % 2][:, :].bitcast(F32), mneg[u % 2][:, :].bitcast(F32)).then_inc(m_made, 1)

                def invert(it, u):
                    n = it * UNITS + u
                    dve.wait_ge(sum_mm, n + 1)
                    dve.wait_ge(o_done, n)
                    dve.reciprocal(rec[:, :].rearrange("p (a c) -> p a c", a=2), o_ps[:, :, 0:QC]).then_inc(rec_done, 1)

                with dve.Fori(0, NU // UNITS) as it:
                    for u in range(2):
                        for h in range(HG):
                            maxima(it, u, h)
                        turn_maxima(it, u)
                    for u in range(UNITS + 1):
                        for h in range(HG):
                            if u + 2 < UNITS:
                                maxima(it, u + 2, h)
                            if h == 2 and u >= 1:
                                invert(it, u - 1)
                        if u + 2 < UNITS:
                            turn_maxima(it, u + 2)


def project(nc, name, *, x_hi, x_lo, kv_hi, kv_lo, w, w_swap, rope, bias, w_v, q_scr, k_scr, v_scr, before=None):
    STEPS = B * 4 * 2
    with Phase(nc, name) as ph:
        val = [ph.sb(f"val{i}", [P, QC]) for i in range(3)]
        t1 = [ph.sb(f"t1{i}", [P, QC]) for i in range(2)] if rope else None
        t2 = [ph.sb(f"t2{i}", [P, QC]) for i in range(2)] if rope else None
        hi = [ph.sb(f"hi{i}", [P, 2, QC], F32R) for i in range(3)]
        lo = [ph.sb(f"lo{i}", [P, 2, QC], F32R) for i in range(3)]
        v_sb = [ph.sb(f"v{i}", [P, H, 32]) for i in range(2)]
        ps = [ph.ps(f"qk{i}", [P, 2, 512]) for i in range(3)]
        ps_v = [ph.ps(f"vps{i}", [P, 512]) for i in range(2)]
        mm_done, val_done, half_done, hi_done, lo_done, v_mm, v_ready, v_copied, own = (
            ph.sem(n) for n in ("mm", "val", "half", "hi", "lo", "vmm", "vready", "vcopied", "own"))
        out_qk = [ph.sem(f"outqk{i}") for i in range(3)]
        out_v = [ph.sem(f"outv{i}") for i in range(2)]

        def tokens(s):
            return slice(s // 8 * SP + s % 2 * QC, s // 8 * SP + s % 2 * QC + QC)

        with nc.Block() as block:
            @block.tensor
            def _(pe):
                def qk(s):
                    m = s // 2 % 4
                    if s >= 3:
                        pe.wait_ge(val_done if not rope else half_done, s - 2)
                    for g, ww in enumerate((w, w_swap) if rope else (w,)):
                        kt, w_hi, w_lo, xh, xl = ww[m]
                        for k in range(kt):
                            mm = split_product(pe, ps[s % 3][:, g, 0:QC], w_hi(k), w_lo(k), xh[:, k, tokens(s)],
                                               xl[:, k, tokens(s)], k == 0, k == kt - 1)
                    mm.then_inc(mm_done, 1)

                def v(i):
                    kt, w_hi, w_lo, xh, xl = w_v
                    a = tile_start(i)
                    if i >= 2:
                        pe.wait_ge(v_copied, i - 1)
                    for k in range(kt):
                        mm = split_product(pe, ps_v[i % 2][:, 0:D], xh[:, k, a:a + P], xl[:, k, a:a + P], w_hi(k),
                                           w_lo(k), k == 0, k == kt - 1)
                    mm.then_inc(v_mm, 1)

                for s in range(STEPS):
                    qk(s)
                    if s % 2:
                        v(s // 2)
                v(NT - 1)

            @block.scalar
            def _(act):
                for s in range(STEPS):
                    m = s // 2 % 4
                    if not rope:
                        act.wait_ge(mm_done, s + 1)
                        if s >= 3:
                            act.wait_ge(lo_done, s - 2)
                        act.activation(val[s % 3][:, :], ps[s % 3][:, 0, 0:QC], ACT.Identity, bias=bias[:, m:m + 1])\
                           .then_inc(val_done, 1)
                    act.wait_ge(val_done, s + 1)
                    if s >= 6:
                        act.wait_ge(out_qk[s // 2 % 3], 48 * (s // 6))
                    act.activation(hi[s // 2 % 3][:, s % 2, :], val[s % 3][:, :], ACT.Copy).then_inc(hi_done, 1)

            @block.vector
            def _(dve):
                def low(s):
                    dve.wait_ge(hi_done, s + 1)
                    dve.tensor_tensor(lo[s // 2 % 3][:, s % 2, :], val[s % 3][:, :],
                                      hi[s // 2 % 3][:, s % 2, :].bitcast(F32), ALU.subtract).then_inc(lo_done, 1)

                def v(i):
                    dve.wait_ge(v_mm, i + 1)
                    dve.wait_ge(v_ready, 4)
                    if i >= 2:
                        dve.wait_ge(out_v[i % 2], 16 * (i // 2))
                    dve.tensor_copy(v_sb[i % 2][:, :, 0:HD], ps_v[i % 2][:, 0:D].rearrange("p (h d) -> p h d", d=HD))\
                       .then_inc(v_copied, 1)

                for s in range(STEPS + 1):
                    if rope and s < STEPS:
                        cos, sin = (t[:, s % 2 * QC:(s % 2 + 1) * QC] for t in rope)
                        dve.wait_ge(mm_done, s + 1)
                        if s >= 2:
                            dve.wait_ge(val_done, s - 1)
                        dve.tensor_tensor(t1[s % 2][:, :], ps[s % 3][:, 0, 0:QC], cos, ALU.mult)
                        dve.tensor_tensor(t2[s % 2][:, :], ps[s % 3][:, 1, 0:QC], sin, ALU.mult).then_inc(half_done, 1)
                    if s >= 1:
                        low(s - 1)
                        if (s - 1) % 2:
                            v((s - 1) // 2)
                v(NT - 1)

            @block.gpsimd
            def _(pool):
                step = Chain(pool, own)
                for i in range(2):
                    step(pool.memset(v_sb[i][:, :, :], 0.0))
                for i in range(2):
                    pool.memset(v_sb[i][:, :, HD:HD + 1], 1.0).then_inc(v_ready, 2)
                if rope:
                    for s in range(STEPS):
                        pool.wait_ge(half_done, s + 1)
                        if s >= 3:
                            pool.wait_ge(lo_done, s - 2)
                        pool.tensor_tensor(val[s % 3][:, :], t1[s % 2][:, :], t2[s % 2][:, :], ALU.add)\
                            .then_inc(val_done, 1)

            @block.sync
            def _(sp):
                if before is not None:
                    before(sp)
                for n in range(STEPS // 2):
                    b, m = n // 4, n % 4
                    sp.wait_ge(lo_done, 2 * n + 2)
                    heads = slice(m % 2 * 8, m % 2 * 8 + 8)
                    scr, parts = (q_scr, (hi, lo, hi)) if m < 2 else (k_scr, (hi, hi, lo))
                    for r, part in enumerate(parts):
                        sp.dma_start(scr[heads, r * HD:(r + 1) * HD, b * SP:(b + 1) * SP],
                                     part[n % 3][:, :, :].rearrange("p a t -> p (a t)").bitcast(F32))\
                          .then_inc(out_qk[n % 3], 16)
                    for i in ([n] if n < STEPS // 2 - 1 else [n, NT - 1]):
                        sp.wait_ge(v_copied, i + 1)
                        skip = i * P - tile_start(i)
                        sp.dma_start(v_scr[i * P:tile_start(i) + P, :],
                                     v_sb[i % 2][skip:P, :, :].rearrange("p h c -> p (h c)")).then_inc(out_v[i % 2], 16)
                for i in range(3):
                    sp.wait_ge(out_qk[i], 48 * ((STEPS // 2 - i + 2) // 3))
                for i in range(2):
                    sp.wait_ge(out_v[i], 16 * ((NT - i + 1) // 2))


def project_out(nc, name, *, o_scr, w, hT, xn=None, xn_scr=None, bias=None):
    with Phase(nc, name) as ph:
        o = ph.sb("o", [P, KT, T])
        o_hi = ph.sb("ohi", [P, KT, T], F32R)
        o_lo = ph.sb("olo", [P, KT, T], F32R)
        ps = [ph.ps(f"y{i}", [P, 512]) for i in range(4)]
        loaded = [ph.sem(f"in{b}") for b in range(B)]
        cleared, xn_in, hi_done, lo_done, y_mm, y_done = (ph.sem(n) for n in ("clear", "xn", "hi", "lo", "mm", "y"))
        with nc.Block() as block:
            @block.sync
            def _(sp):
                for b in range(B):
                    for k in range(KT):
                        sp.dma_start(o[:, k, b * SP:b * SP + SEQ],
                                     o_scr.rearrange("(h r) t -> h r t", r=32)[k * 8:(k + 1) * 8, 0:HD, b * SP:b * SP + SEQ])\
                          .then_inc(loaded[b], 16)
                if xn is not None:
                    sp.dma_start(xn[:, :, :], xn_scr).then_inc(xn_in, 16)

            @block.gpsimd
            def _(pool):
                for b in range(B):
                    ins = pool.memset(o[:, :, b * SP + SEQ:(b + 1) * SP], 0.0)
                ins.then_inc(cleared, 1)

            @block.scalar
            def _(act):
                act.wait_ge(cleared, 1)
                for b in range(B):
                    act.wait_ge(loaded[b], 16 * KT)
                    t = slice(b * SP, (b + 1) * SP)
                    act.activation(o_hi[:, :, t], o[:, :, t], ACT.Copy).then_inc(hi_done, 1)

            @block.tensor
            def _(pe):
                for n in range(KT * NQC):
                    b, c, m = n // (2 * KT), n // KT, n % KT
                    if c % 2 == 0 and m == 0:
                        pe.wait_ge(lo_done, b + 1)
                    if n >= 4:
                        pe.wait_ge(y_done, n - 3)
                    for k in range(KT):
                        t = slice(c * QC, (c + 1) * QC)
                        mm = split_product(pe, ps[n % 4][:, 0:QC], w[0][:, k, m * P:(m + 1) * P],
                                           w[1][:, k, m * P:(m + 1) * P], o_hi[:, k, t], o_lo[:, k, t],
                                           k == 0, k == KT - 1)
                    mm.then_inc(y_mm, 1)

            @block.vector
            def _(dve):
                def low(b):
                    dve.wait_ge(hi_done, b + 1)
                    t = slice(b * SP, (b + 1) * SP)
                    dve.tensor_tensor(o_lo[:, :, t], o[:, :, t], o_hi[:, :, t].bitcast(F32), ALU.subtract)\
                       .then_inc(lo_done, 1)

                low(0)
                if xn is not None:
                    dve.wait_ge(xn_in, 16)
                for n in range(KT * NQC):
                    if n % (2 * KT) == 0 and n // (2 * KT) + 1 < B:
                        low(n // (2 * KT) + 1)
                    c, m = n // KT, n % KT
                    t = slice(c * QC, (c + 1) * QC)
                    dve.wait_ge(y_mm, n + 1)
                    if xn is not None:
                        ins = dve.scalar_tensor_tensor(out=xn[:, m, t], in0=ps[n % 4][:, 0:QC], scalar=bias[:, m:m + 1],
                                                       in1=xn[:, m, t], op0=ALU.add, op1=ALU.add)
                    else:
                        ins = dve.tensor_tensor(hT[:, m, t], ps[n % 4][:, 0:QC], hT[:, m, t], ALU.add)
                    ins.then_inc(y_done, 1)


def latent(nc, name, x_hi, x_lo, w, lat):
    with Phase(nc, name) as ph:
        ps = [ph.ps(f"l{i}", [P, 512]) for i in range(2)]
        mm_done, read = ph.sem("mm"), ph.sem("read")
        with nc.Block() as block:
            @block.tensor
            def _(pe):
                for c in range(NCH):
                    if c >= 2:
                        pe.wait_ge(read, c - 1)
                    t = slice(c * CH, (c + 1) * CH)
                    for k in range(KT):
                        mm = split_product(pe, ps[c % 2][:, 0:CH], w[0][:, k, :], w[1][:, k, :], x_hi[:, k, t],
                                           x_lo[:, k, t], k == 0, k == KT - 1)
                    mm.then_inc(mm_done, 1)

            @block.scalar
            def _(act):
                for c in range(NCH):
                    act.wait_ge(mm_done, c + 1)
                    act.activation(lat[:, 0, c * CH:(c + 1) * CH], ps[c % 2][:, 0:CH], ACT.Copy).then_inc(read, 1)


def router(nc, name, *, xn, w, ne, identity, scr, gain=None, before=None):
    with Phase(nc, name) as ph:
        ps = ph.ps("logits", [P, 512])
        ps_t = ph.ps("turned", [P, 2, 512])
        logit = ph.sb("logit", [P, NT, ne])
        prob = ph.sb("prob", [P, NT, ne])
        beats = ph.sb("beats", [P, NT, ne, ne])
        tied = ph.sb("tied", [P, NT, ne, ne])
        rank = ph.sb("rank", [P, NT, ne])
        one = ph.sb("one", [P, NT])
        two = ph.sb("two", [P, NT])
        best = ph.sb("best", [P, NT, 8])
        fac = ph.sb("fac", [P, 256])
        fac_t = ph.sb("fact", [P, 2, P])
        mm_done, scaled, e_done, own, fac_done, turned, copied, out = (
            ph.sem(n) for n in ("mm", "scaled", "exp", "own", "fac", "turned", "copied", "out"))

        with nc.Block() as block:
            @block.tensor
            def _(pe):
                for i in range(NT):
                    a = tile_start(i)
                    for k in range(KT):
                        mm = pe.matmul(ps[:, i * 8:i * 8 + ne], xn[:, k, a:a + P], w[:, k, :],
                                       start=(k == 0), stop=(k == KT - 1))
                mm.then_inc(mm_done, 1)
                pe.wait_ge(fac_done, 1)
                for g in range(2):
                    mm = pe.transpose(ps_t[:, g, 0:P], fac[:, g * P:(g + 1) * P], identity)
                mm.then_inc(turned, 1)

            @block.scalar
            def _(act):
                act.wait_ge(scaled, 1)
                act.activation(prob[:, :, :], logit[:, :, :], ACT.Exp, scale=(-1.0 if gain is not None else 1.0))\
                   .then_inc(e_done, 1)

            @block.vector
            def _(dve):
                step = Chain(dve, own)
                each = [P, NT, ne]
                step(dve.memset(fac[:, :], 0.0))
                dve.wait_ge(mm_done, 1)
                raw = ps[:, 0:NT * 8].rearrange("p (n e) -> p n e", e=8)[:, :, 0:ne]
                if gain is not None:
                    step(dve.tensor_tensor(rank[:, :, :], raw, gain.unsqueeze(1).to_broadcast(each), ALU.mult))
                    dve.tensor_scalar(logit[:, :, :], rank[:, :, :], -87.0, None, ALU.max).then_inc(scaled, 1)
                    dve.wait_ge(e_done, 1)
                    step(dve.tensor_scalar(rank[:, :, :], prob[:, :, :], 1.0, None, ALU.add))
                    step(dve.reciprocal(prob[:, :, :], rank[:, :, :]))
                    other = prob[:, :, :].unsqueeze(2).to_broadcast([P, NT, ne, ne])
                    this = prob[:, :, :].unsqueeze(3).to_broadcast([P, NT, ne, ne])
                    step(dve.tensor_tensor(tied[:, :, :, :], other, this, ALU.is_equal))
                    for n in range(ne):
                        ins = dve.memset(tied[:, :, n, n:ne], 0.0)
                    step(ins)
                    step(dve.tensor_tensor(beats[:, :, :, :], other, this, ALU.is_gt))
                    step(dve.tensor_tensor(beats[:, :, :, :], beats[:, :, :, :], tied[:, :, :, :], ALU.add))
                    step(dve.tensor_reduce(rank[:, :, :], beats[:, :, :, :], AX.X, ALU.add))
                    step(dve.tensor_scalar(rank[:, :, :], rank[:, :, :], 1.5, None, ALU.is_lt))
                    step(dve.tensor_tensor(rank[:, :, :], rank[:, :, :], prob[:, :, :], ALU.mult))
                    step(dve.tensor_reduce(one[:, :], rank[:, :, :], AX.X, ALU.add))
                    step(dve.reciprocal(two[:, :], one[:, :]))
                    f = fac[:, 0:NT * 8].rearrange("p (n e) -> p n e", e=8)
                    dve.memset(f[:, :, ne:8], 1.0)
                    dve.tensor_tensor(f[:, :, 0:ne], rank[:, :, :], two[:, :].unsqueeze(2).to_broadcast(each), ALU.mult)\
                       .then_inc(fac_done, 1)
                else:
                    step(dve.tensor_reduce(one[:, :], raw, AX.X, ALU.max))
                    dve.tensor_tensor(logit[:, :, :], raw, one[:, :].unsqueeze(2).to_broadcast(each), ALU.subtract)\
                       .then_inc(scaled, 1)
                    dve.wait_ge(e_done, 1)
                    step(dve.tensor_reduce(one[:, :], prob[:, :, :], AX.X, ALU.add))
                    step(dve.reciprocal(two[:, :], one[:, :]))
                    step(dve.tensor_tensor(rank[:, :, :], prob[:, :, :], two[:, :].unsqueeze(2).to_broadcast(each), ALU.mult))
                    for i in range(NT):
                        ins = dve.max(best[:, i, :], rank[:, i, :])
                    step(ins)
                    step(dve.tensor_tensor(one[:, :], best[:, :, 0], best[:, :, 1], ALU.add))
                    step(dve.reciprocal(two[:, :], one[:, :]))
                    step(dve.tensor_tensor(best[:, :, 0:2], best[:, :, 0:2], two[:, :].unsqueeze(2).to_broadcast([P, NT, 2]),
                                           ALU.mult))
                    dve.tensor_tensor(fac[:, 0:NT], best[:, :, 0], best[:, :, 1], ALU.add).then_inc(fac_done, 1)
                dve.wait_ge(turned, 1)
                dve.tensor_copy(fac_t[:, :, :], ps_t[:, :, 0:P]).then_inc(copied, 1)

            @block.sync
            def _(sp):
                if before is not None:
                    before(sp)
                sp.wait_ge(copied, 1)
                whole = T // P * P
                if gain is not None:
                    sp.dma_start(scr[:, 0:whole].rearrange("e (n t) -> n e t", t=P), fac_t[:, 0, :]).then_inc(out, 16)
                    sp.dma_start(scr[:, whole:T], fac_t[0:8, 1, P - (T - whole):P]).then_inc(out, 16)
                else:
                    sp.dma_start(scr[:, 0:whole].rearrange("e (n t) -> (e n) t", t=P), fac_t[0:NT - 1, 0, :]).then_inc(out, 16)
                    sp.dma_start(scr[:, whole:T], fac_t[NT - 1:NT, 0, P - (T - whole):P]).then_inc(out, 16)
                sp.wait_ge(out, 32)


RL = 648
RZ = 4


def bias_rows(nc, name, fwd_in, rev_in, scale, row_scr, fwd_scr, copied, rev_hi_scr, rev_lo_scr):
    with Phase(nc, name) as ph:
        fwd, rev = ph.sb("fwd", [H, RL]), ph.sb("rev", [H, RL])
        hi, lo = ph.sb("hi", [H, RL], F32R), ph.sb("lo", [H, RL], F32R)
        loaded, cleared, scaled, hi_done, lo_done, out = (ph.sem(n) for n in ("in", "clear", "scaled", "hi", "lo", "out"))
        with nc.Block() as block:
            @block.vector
            def _(dve):
                dve.memset(fwd[:, 0:RZ], 0.0)
                dve.memset(fwd[:, RZ + SEQ:RL], NEG)
                dve.memset(rev[:, 0:RL - RZ - SEQ], NEG)
                dve.memset(rev[:, RL - RZ:RL], 0.0).then_inc(cleared, 1)
                dve.wait_ge(loaded, 32)
                a = RL - RZ - SEQ
                dve.tensor_scalar(fwd[:, RZ:RZ + SEQ], fwd[:, RZ:RZ + SEQ], 1.0 / scale, None, ALU.mult)
                dve.tensor_scalar(rev[:, a:a + SEQ], rev[:, a:a + SEQ], 1.0 / scale, None, ALU.mult).then_inc(scaled, 1)
                dve.wait_ge(scaled, 1)
                dve.tensor_copy(hi[:, :], rev[:, :]).then_inc(hi_done, 1)
                dve.wait_ge(hi_done, 1)
                dve.tensor_tensor(lo[:, :], rev[:, :], hi[:, :].bitcast(F32), ALU.subtract).then_inc(lo_done, 1)

            @block.sync
            def _(sp):
                sp.dma_start(fwd[:, RZ:RZ + SEQ], fwd_in[:, 0:SEQ]).then_inc(loaded, 16)
                sp.dma_start(rev[:, RL - RZ - SEQ:RL - RZ], rev_in[:, 2 * SX - 1 - SEQ:2 * SX - 1]).then_inc(loaded, 16)
                sp.wait_ge(lo_done, 1)
                sp.dma_start(row_scr, fwd[:, :]).then_inc(out, 16)
                sp.dma_start(rev_hi_scr, hi[:, :].bitcast(F32)).then_inc(out, 16)
                sp.dma_start(rev_lo_scr, lo[:, :].bitcast(F32)).then_inc(out, 16)
                sp.wait_ge(out, 48)
                sp.dma_start(fwd_scr.rearrange("p h n -> p (h n)"),
                             bass.AP(tensor=row_scr.tensor, offset=row_scr.offset, ap=[[0, P], [1, H * RL]]))\
                  .then_inc(copied, 16)


def vit_tower(nc, A):
    def scratch(name, shape):
        return nc.dram_tensor(name, shape, F32).ap()

    q_scr, k_scr = scratch("q_scr", [H, 3 * HD + 1, T]), scratch("k_scr", [H, 3 * HD, T])
    v_scr, o_scr = scratch("v_scr", [T, H * 32]), scratch("o_scr", [H * 32, T])
    m_scr = [scratch(f"m_scr{i}", [P, 32]) for i in range(2)]
    xn_scr = scratch("xn_scr", [P, KT, T])
    row_scr, rev_hi_scr, rev_lo_scr = (scratch(n, [H, RL]) for n in ("row_scr", "rev_hi_scr", "rev_lo_scr"))
    fwd_scr = scratch("fwd_scr", [P, H, RL])
    fac0_scr, fac1_scr = scratch("fac0_scr", [8, T]), scratch("fac1_scr", [1, T])

    def rows(ap):
        return ap.rearrange("(k p) n -> p k n", p=P)

    Phase.used.clear()
    with Phase(nc, "all") as top:
        hT = top.sb("hT", [P, KT, T])
        one_c = top.sb("mean", [P, P])
        one64 = top.sb("mean64", [P, P])
        identf = top.sb("identf", [P, P])
        eps = top.sb("eps", [P, 1])
        got, copied = top.sem("got"), top.sem("copied")

        with Phase(nc, "init") as ph, nc.Block() as block:
            zeros, cleared = ph.sb("zeros", [H, T]), ph.sem("cleared")

            @block.sync
            def _(sp):
                sp.dma_start(identf[:, :], A["c_ident"]).then_inc(got, 16)
                sp.wait_ge(cleared, 1)
                sp.dma_start(q_scr[:, 3 * HD, :], zeros[:, :]).then_inc(got, 16)
                for b in range(B):
                    sp.dma_start(hT[:, :, b * SP:b * SP + 1], A["cls"].unsqueeze(2), allow_slow_non_contiguous=True)\
                      .then_inc(got, 16)
                sp.wait_ge(got, 16 * (B + 2))

            @block.vector
            def _(dve):
                dve.memset(zeros[:, :], 0.0).then_inc(cleared, 1)
                for b in range(B):
                    dve.memset(hT[:, :, b * SP + SEQ:(b + 1) * SP], 0.0)
                dve.memset(one_c[:, :], 1.0 / D)
                dve.memset(one64[0:64, :], 1.0 / 64)
                dve.memset(one64[64:P, :], 0.0)
                dve.memset(eps[:, :], EPS)

        bias_rows(nc, "rows", A["rpb_fwd"], A["rpb_rev"], 1.0 / 16, row_scr, fwd_scr, copied, rev_hi_scr, rev_lo_scr)

        with Phase(nc, "tok") as ph:
            raw = ph.sb("raw", [P, KT, B * SX])
            hi, lo = ph.sb("hi", [P, KT, B * SX], F32R), ph.sb("lo", [P, KT, B * SX], F32R)
            x = A["x0"].rearrange("(k p) n -> p k n", p=P)
            split_weights(nc, "toks", [(raw[:, :, b * SX:(b + 1) * SX], x[:, :, b * SX:(b + 1) * SX],
                                        hi[:, :, b * SX:(b + 1) * SX], lo[:, :, b * SX:(b + 1) * SX]) for b in range(B)])
            gated_ffn(nc, "tokf", x_hi=hi, x_lo=lo, chunks=[(b * SX, SX) for b in range(B)], J=4, half=False, gated=True,
                      func=ACT.Relu, experts=1, w_mult=None, lag=2,
                      load=lambda e, r1, r2: [(r1[:, :, 0:512], rows(A["w0"])), (r1[:, :, 512:1024], rows(A["w1"])),
                                              (r2[:, :, :], rows(A["wo"]))],
                      finish=lambda c: hT[:, :, c * SP + 1:c * SP + 1 + SX], store=True)

        with Phase(nc, "L0") as l0:
            t_hi, t_lo, t_max = ([l0.sb(f"t{n}{i}", [P, HG, SP], dt) for i in range(2)]
                                 for n, dt in (("hi", F32R), ("lo", F32R), ("mx", F32)))
            tail_hi, tail_lo = ([l0.sb(f"tail{n}{i}", [P, HG, 4], F32R) for i in range(2)] for n in "hl")
            t_sem = [l0.sem(f"t{i}") for i in range(2)]
            vb = l0.sb("vb", [P, H // HG])
            b_in, b_clear = l0.sem("b"), l0.sem("bc")

            def load_bias(sp, hg):
                i = hg % 2

                def window(scr, first, n, step=1):
                    return bass.AP(tensor=scr.tensor, offset=scr.offset + hg * HG * RL + first,
                                   ap=[[step, P], [RL, HG], [1, n]])

                own = RL - 1 - RZ - SX - (P - 1)
                for dst, src in ((t_hi[i][:, :, :].bitcast(F32), window(rev_hi_scr, own, SP)),
                                 (t_lo[i][:, :, :].bitcast(F32), window(rev_lo_scr, own, SP)),
                                 (t_max[i][:, :, :], window(fwd_scr, RZ + P - 1, SP, H * RL - 1)),
                                 (tail_hi[i][:, :, :].bitcast(F32), window(rev_hi_scr, own + P - 4, 4)),
                                 (tail_lo[i][:, :, :].bitcast(F32), window(rev_lo_scr, own + P - 4, 4))):
                    sp.dma_start(dst, src).then_inc(t_sem[i], 16)

            with Phase(nc, "L0p") as ph:
                xn = ph.sb("xn", [P, KT, T])
                hi, lo = ph.sb("hi", [P, KT, T], F32R), ph.sb("lo", [P, KT, T], F32R)
                wr = ph.sb("wraw", [P, KT, 3 * D])
                wh, wl = ph.sb("wh", [P, KT, 3 * D], F32R), ph.sb("wl", [P, KT, 3 * D], F32R)
                bias = ph.sb("bias", [P, 4])
                split_weights(nc, "L0w", [(wr[:, :, :], rows(A["wqkv"]), wh[:, :, :], wl[:, :, :]),
                                          (bias[:, :], A["bqk"], None, None)])
                layer_norm(nc, "L0n", hT, one_c[:, :], eps[:, 0:1], xn=xn, hi=hi, lo=lo, spill=xn_scr)

                def part(t, m, n=P):
                    return lambda k: t[:, k, m:m + n]

                def before(sp):
                    sp.wait_ge(copied, 16)
                    load_bias(sp, 0)
                    load_bias(sp, 1)

                w = [(KT, part(wh, m * P), part(wl, m * P), hi, lo) for m in range(4)]
                project(nc, "L0q", x_hi=hi, x_lo=lo, kv_hi=hi, kv_lo=lo, w=w, w_swap=None, rope=None, bias=bias,
                        w_v=(KT, part(wh, 2 * D, D), part(wl, 2 * D, D), hi, lo), q_scr=q_scr, k_scr=k_scr, v_scr=v_scr,
                        before=before)

            with Phase(nc, "L0a") as ph:
                consts = attention_consts(nc, ph, A, identf, toeplitz=True)
                with nc.Block() as block:
                    @block.gpsimd
                    def _(pool):
                        pool.memset(vb[:, :], 0.0).then_inc(b_clear, 1)

                    @block.sync
                    def _(sp):
                        sp.wait_ge(b_clear, 1)
                        for h in range(HG):
                            sp.dma_start(vb[32 * h:32 * h + HD, :], A["bv"][h]).then_inc(b_in, 16)
                        sp.wait_ge(b_in, 16 * HG)
                attention(nc, "L0t", q_scr=q_scr, k_scr=k_scr, v_scr=v_scr, o_scr=o_scr, m_scr=m_scr, scale=1.0 / 16,
                          toeplitz={"hi": t_hi, "lo": t_lo, "max": t_max, "tail_hi": tail_hi, "tail_lo": tail_lo,
                                    "loaded": t_sem, "n": 5, "load": load_bias}, consts=consts, v_bias=vb)

        with Phase(nc, "L0o") as ph:
            xn = ph.sb("xn", [P, KT, T])
            wr = ph.sb("wraw", [P, KT, D])
            w = [ph.sb(f"w{q}", [P, KT, D], F32R) for q in "hl"]
            vec = ph.sb("vec", [P, 3, KT])
            split_weights(nc, "L0ow", [(wr[:, :, :], rows(A["wproj"]), w[0][:, :, :], w[1][:, :, :]),
                                       (vec[:, :, :], A["vec0"], None, None)])
            project_out(nc, "L0oo", o_scr=o_scr, w=w, hT=hT, xn=xn, xn_scr=xn_scr, bias=vec[:, 0, :])
            layer_norm(nc, "L0on", xn, one_c[:, :], eps[:, 0:1], xn=xn, gain=vec[:, 1, :], shift=vec[:, 2, :], add_to=hT)

        with Phase(nc, "E") as ph:
            hi, lo = ph.sb("hi", [P, KT, T], F32R), ph.sb("lo", [P, KT, T], F32R)
            with Phase(nc, "E1") as p2:
                xn = p2.sb("xn", [P, KT, T])
                wr = p2.sb("wr", [P, KT, NEXP0])
                gain = p2.sb("gain", [P, NEXP0])
                split_weights(nc, "E1w", [(wr[:, :, :], rows(A["wr0"]), None, None),
                                          (gain[:, :], A["rb"].to_broadcast([P, NEXP0]), None, None)])
                layer_norm(nc, "E1n", hT, one_c[:, :], eps[:, 0:1], xn=xn, hi=hi, lo=lo)
                router(nc, "E1r", xn=xn, w=wr, ne=NEXP0, identity=identf[:, :], scr=fac0_scr, gain=gain[:, :])

            def load_expert(e, r1, r2):
                return [(r1[:, :, :], rows(A["gu"][e])), (r2[:, 0:5, :], rows(A["down"][e, 0:640, :])),
                        (r2[0:64, 5, :], A["down"][e, 640:HID0, :])]

            gated_ffn(nc, "Ef", x_hi=hi, x_lo=lo, chunks=[(c * CH, CH) for c in range(NCH)], J=6, half=True, gated=True,
                      func=ACT.Silu, experts=NEXP0 + 1, w_mult=lambda e: fac0_scr[e:e + 1, :].to_broadcast([P, T]), lag=3,
                      load=load_expert, finish=lambda c: hT[:, :, c * CH:(c + 1) * CH])

        clear_semaphores(nc)

        with Phase(nc, "L1p") as ph:
            xn = ph.sb("xn", [P, KT, T])
            hi, lo = ph.sb("hi", [P, KT, T], F32R), ph.sb("lo", [P, KT, T], F32R)
            lat, lat_hi, lat_lo = (ph.sb(f"lat{i}", [P, 1, T], dt) for i, dt in enumerate((F32, F32R, F32R)))
            wqr, wq = ph.sb("wqr", [P, KT, 2 * D]), [ph.sb(f"wq{q}", [P, KT, 2 * D], F32R) for q in "hl"]
            wlr, wl = ph.sb("wlr", [P, KT, P]), [ph.sb(f"wl{q}", [P, KT, P], F32R) for q in "hl"]
            wkr, wk = ph.sb("wkr", [P, 1, 3 * D]), [ph.sb(f"wk{q}", [P, 1, 3 * D], F32R) for q in "hl"]
            vec = ph.sb("vec", [P, 2])
            cos, sin = ph.sb("cos", [P, SP]), ph.sb("sin", [P, SP])
            with nc.Block() as block:
                @block.vector
                def _(dve):
                    dve.memset(wlr[:, :, 64:P], 0.0)
                    dve.memset(wkr[64:P, :, :], 0.0)
                    dve.memset(vec[:, :], 0.0)
            split_weights(nc, "L1w1", [(wqr[:, :, :], rows(A["wq1"]), None, None),
                                       (wlr[:, :, 0:64], rows(A["wdkv"]), None, None),
                                       (wkr[0:64, 0, :], A["wkv1"], None, None),
                                       (vec[0:64, :], A["vec1"], None, None),
                                       (cos[:, :], A["c_cos"], None, None), (sin[:, :], A["c_sin"], None, None)])
            with nc.Block() as block:
                w_hi = ph.sem("whi")

                @block.scalar
                def _(act):
                    for r, w in ((wqr, wq), (wlr, wl), (wkr, wk)):
                        act.activation(w[0][:, :, :], r[:, :, :], ACT.Copy).then_inc(w_hi, 1)

                @block.vector
                def _(dve):
                    for n, (r, w) in enumerate(((wqr, wq), (wlr, wl), (wkr, wk))):
                        dve.wait_ge(w_hi, n + 1)
                        dve.tensor_tensor(w[1][:, :, :], r[:, :, :], w[0][:, :, :].bitcast(F32), ALU.subtract)

            layer_norm(nc, "L1n", hT, one_c[:, :], eps[:, 0:1], xn=xn, hi=hi, lo=lo)
            latent(nc, "L1l", hi, lo, wl, lat)
            layer_norm(nc, "L1ln", lat, one64[:, :], eps[:, 0:1], xn=lat, hi=lat_hi, lo=lat_lo, gain=vec[:, 0:1],
                       shift=vec[:, 1:2], width=1)

            def part(t, m, n=P):
                return lambda k: t[:, k, m:m + n]

            def four(q0, k0):
                return ([(KT, part(wq[0], q0 + m * P), part(wq[1], q0 + m * P), hi, lo) for m in range(2)]
                        + [(1, part(wk[0], k0 + m * P), part(wk[1], k0 + m * P), lat_hi, lat_lo) for m in range(2)])

            project(nc, "L1q", x_hi=hi, x_lo=lo, kv_hi=lat_hi, kv_lo=lat_lo, w=four(0, 0), w_swap=four(D, D),
                    rope=(cos, sin), bias=None, w_v=(1, part(wk[0], 2 * D, D), part(wk[1], 2 * D, D), lat_hi, lat_lo),
                    q_scr=q_scr, k_scr=k_scr, v_scr=v_scr)

        with Phase(nc, "L1a") as ph:
            consts = attention_consts(nc, ph, A, identf, toeplitz=False)
            attention(nc, "L1t", q_scr=q_scr, k_scr=k_scr, v_scr=v_scr, o_scr=o_scr, m_scr=m_scr, scale=1.0 / 4,
                      toeplitz=None, consts=consts, v_bias=None)

        with Phase(nc, "L1o") as ph:
            wr = ph.sb("wraw", [P, KT, D])
            w = [ph.sb(f"w{q}", [P, KT, D], F32R) for q in "hl"]
            split_weights(nc, "L1ow", [(wr[:, :, :], rows(A["wo1"]), w[0][:, :, :], w[1][:, :, :])])
            project_out(nc, "L1oo", o_scr=o_scr, w=w, hT=hT)

        with Phase(nc, "F") as ph:
            hi, lo = ph.sb("hi", [P, KT, T], F32R), ph.sb("lo", [P, KT, T], F32R)
            b1, b2 = ph.sb("b1", [P, FF1 // P]), ph.sb("b2", [P, KT])
            with Phase(nc, "F1") as p2:
                xn = p2.sb("xn", [P, KT, T])
                wr = p2.sb("wr", [P, KT, NEXP1])
                split_weights(nc, "F1w", [(wr[:, :, :], rows(A["wr1"]), None, None), (b1[:, :], A["b1"], None, None),
                                          (b2[:, :], A["b2"], None, None)])
                layer_norm(nc, "F1n", hT, one_c[:, :], eps[:, 0:1], xn=xn, hi=hi, lo=lo)
                router(nc, "F1r", xn=xn, w=wr, ne=NEXP1, identity=identf[:, :], scr=fac1_scr)
            gated_ffn(nc, "Ff", x_hi=hi, x_lo=lo, chunks=[(c * CH, CH) for c in range(NCH)], J=FF1 // P, half=False,
                      gated=False, func=ACT.Gelu_apprx_tanh, experts=1,
                      w_mult=lambda e: fac1_scr.to_broadcast([P, T]), lag=3,
                      load=lambda e, r1, r2: [(r1[:, :, :], rows(A["ff1"])), (r2[:, :, :], rows(A["ff2"]))],
                      finish=lambda c: hT[:, :, c * CH:(c + 1) * CH], up_bias=b1, out_bias=b2)

        with nc.Block() as block:
            done = top.sem("done")

            @block.sync
            def _(sp):
                sp.dma_start(A["out"].rearrange("(k p) t -> p k t", p=P), hT[:, :, :]).then_inc(done, 16)
                sp.wait_ge(done, 16)


def attention_consts(nc, ph, A, identf, toeplitz):
    ident, turn, tail = ph.sb("ident", [P, P], F32R), ph.sb("turn", [P, P], F32R), ph.sb("tail", [P, 4], F32R)
    raw = ph.sb("craw", [P, 2 * P + 4])
    sums, row48 = ph.sb("sums", [P, P]), ph.sb("row48", [P, 1])
    mask2 = None if toeplitz else ph.sb("mask2", [P, SP])
    got = ph.sem("cgot")
    loads = [(raw[:, :], A["c_masks"]), (sums[:, :], A["c_sums"]), (row48[:, :], A["c_row48"])]
    if mask2 is not None:
        loads.append((mask2[:, :], A["c_mask2"]))
    with nc.Block() as block:
        @block.sync
        def _(sp):
            for dst, src in loads:
                sp.dma_start(dst, src).then_inc(got, 16)

        @block.vector
        def _(dve):
            dve.wait_ge(got, 16 * len(loads))
            dve.tensor_copy(ident[:, :], identf[:, :])
            dve.tensor_copy(turn[:, :], raw[:, P:2 * P] if toeplitz else raw[:, 0:P])
            dve.tensor_copy(tail[:, :], raw[:, 2 * P:])
    return {"ident": ident[:, :], "flip": turn[:, :] if toeplitz else None, "diag": None if toeplitz else turn[:, :],
            "tail": tail[:, :], "sums": sums[:, :], "row48": row48[:, :],
            "mask2": None if mask2 is None else mask2[:, :]}


def constants():
    import numpy as np
    p = np.arange(P)
    half = HD // 2
    inv = (1.0 / 10000.0 ** (np.arange(half, dtype=np.float32) / np.float32(half))).astype(np.float32)
    ang = np.arange(SP, dtype=np.float32)[None, :] * inv[:, None]
    row = p % HD
    sign = np.where(row < half, -1.0, 1.0)[:, None]
    diag = np.where(p[:, None] > p[None, :], NEG, 0.0)
    j = np.arange(4)[None, :]
    tail = np.where((p[:, None] < P - 4) | (p[:, None] - (P - 4) > j), NEG, 0.0)
    return {
        "c_ident": np.eye(P, dtype=np.float32),
        "c_cos": np.cos(ang.astype(np.float64))[row % half].astype(np.float32),
        "c_sin": (np.sin(ang.astype(np.float64))[row % half] * sign).astype(np.float32),
        "c_masks": np.concatenate([diag, np.eye(P)[::-1], tail], 1).astype(np.float32),
        "c_mask2": np.where(np.arange(SP)[None, :] > 385 + p[:, None], NEG, 0.0).astype(np.float32),
        "c_sums": (p[:, None] == p[None, :] // 32 * 32 + HD).astype(np.float32),
        "c_row48": (p == 3 * HD).astype(np.float32)[:, None],
    }


def kernel(**inputs):
    import numpy as np
    import concourse.bacc as bacc
    from concourse.bass_utils import run_bass_kernel_spmd as run

    a = {k: np.asarray(v) for k, v in inputs.items()}
    n0, nh = HID0 // P * P, H

    def gate_up(g, u):
        return np.concatenate([g[..., :n0], u[..., :n0], g[..., n0:], u[..., n0:]], -1)

    def swapped(w):
        return w.reshape(-1, nh, 2, HD // 2)[:, :, ::-1].reshape(-1, D)

    qkv, wb = a["L0_attn_W_w"], a["L0_attn_W_b"]
    wq, wuk = a["L1_attn_W_q"], a["L1_attn_W_uk"]
    arrays = {
        "x0": a["x"][..., 0].transpose(2, 0, 1).reshape(D, B * SX),
        "cls": a["cls_tok"].reshape(KT, P).T,
        "w0": a["L0_tok_W0"].T, "w1": a["L0_tok_W1"].T, "wo": a["L0_tok_Wo"].T,
        "wqkv": qkv.T, "bqk": wb[:2 * D].reshape(4, P).T,
        "bv": wb[2 * D:].reshape(H // HG, HG, HD).transpose(1, 2, 0),
        "rpb_fwd": a["L0_attn_rpb"].T, "rpb_rev": a["L0_attn_rpb"][::-1].T,
        "wproj": a["L0_attn_proj_w"].T,
        "vec0": np.stack([a[f"L0_attn_{n}"].reshape(KT, P).T for n in ("proj_b", "ln_g", "ln_b")], 1),
        "wr0": a["L0_ffn_Wr"], "rb": a["L0_ffn_routing_bias"][None],
        "gu": np.concatenate([gate_up(a["L0_ffn_routed_gate"], a["L0_ffn_routed_up"]),
                              gate_up(a["L0_ffn_shared_gate"], a["L0_ffn_shared_up"])[None]]),
        "down": np.concatenate([a["L0_ffn_routed_down"], a["L0_ffn_shared_down"][None]]),
        "wq1": np.concatenate([wq, swapped(wq)], 1), "wdkv": a["L1_attn_W_dkv"],
        "wkv1": np.concatenate([wuk, swapped(wuk), a["L1_attn_W_uv"]], 1),
        "vec1": np.stack([a["L1_attn_ln_gamma"], a["L1_attn_ln_beta"]], 1),
        "wo1": a["L1_attn_W_o"], "wr1": a["L1_ffn_router_w"], "ff1": a["L1_ffn_w1"], "ff2": a["L1_ffn_w2"],
        "b1": a["L1_ffn_b1"].reshape(FF1 // P, P).T, "b2": a["L1_ffn_b2"].reshape(KT, P).T,
        **constants(),
    }
    arrays = {f"in_{k}": np.ascontiguousarray(v) for k, v in arrays.items()}
    nc = bacc.Bacc("TRN2", target_bir_lowering=False, num_devices=1)
    aps = {k[3:]: nc.dram_tensor(k, v.shape, F32, kind="ExternalInput").ap() for k, v in arrays.items()}
    aps["out"] = nc.dram_tensor("out_dram", [D, T], F32, kind="ExternalOutput").ap()
    vit_tower(nc, aps)
    got = run(nc, [arrays], core_ids=[0]).results[0]["out_dram"]
    return np.ascontiguousarray(got.reshape(D, B, SP)[:, :, :SEQ].transpose(1, 2, 0))
```

```python
import concourse.bass as bass
from concourse import mybir
from contextlib import ExitStack

F32 = mybir.dt.float32
F32R = mybir.dt.float32r
ALU = mybir.AluOpType
ACT = mybir.ActivationFunctionType
AX = mybir.AxisListType

B = 4
SX = 512
SEQ = SX + 1
SP = 516
T = B * SP
D = 256
KT = D // 128
P = 128
CH = 344
NCH = T // CH
QC = SP // 2
NQC = T // QC
H, HD = 16, 16
HG = 4
NT = (T + P - 1) // P
NEG = -1.0e30
EPS = 1e-5
HID0, NEXP0 = 704, 7
NEXP1 = 8
FF1 = 1024


def tile_start(i):
    return min(i * P, T - P)


def split_product(pe, out, w_hi, w_lo, x_hi, x_lo, start=True, stop=True, ):
    pe.matmul(out, w_hi, x_hi, start=start, stop=False, skip_group_check=True)
    pe.matmul(out, w_hi, x_lo, start=False, stop=False, skip_group_check=True)
    return pe.matmul(out, w_lo, x_hi, start=False, stop=stop, skip_group_check=True)


class Chain:

    def __init__(self, eng, sem):
        self.eng, self.sem, self.n = eng, sem, 0

    def __call__(self, ins):
        self.n += 1
        ins.then_inc(self.sem, 1)
        self.eng.wait_ge(self.sem, self.n)


class Phase:

    def __init__(self, nc, name):
        self.nc, self.name, self.stack = nc, name, ExitStack()

    def __enter__(self):
        self.stack.__enter__()
        return self

    def __exit__(self, *a):
        return self.stack.__exit__(*a)

    def sb(self, name, shape, dt=F32):
        return self.stack.enter_context(self.nc.sbuf_tensor(f"{self.name}_{name}", shape, dt))

    def ps(self, name, shape):
        return self.stack.enter_context(self.nc.psum_tensor(f"{self.name}_{name}", shape, F32))

    def sem(self, name):
        s = self.stack.enter_context(self.nc.semaphore(f"{self.name}_{name}"))
        self.used.append(s.num)
        return s

    used = []


def clear_semaphores(nc):
    with nc.Block() as block:
        @block.sync
        def _(sp):
            sp.sem_clear(range(min(Phase.used), max(Phase.used) + 1))


def layer_norm(nc, name, x, consts, xn=None, hi=None, lo=None, gain=None, shift=None, add_to=None, spill=None,
               width=KT, beside=None):
    mean_w, ones, identity, eps = consts
    SUB = CH // 4
    XB, SB = 4, 3
    with Phase(nc, name) as ph:
        xc = [ph.sb(f"xc{i}", [P, width, CH]) for i in range(XB)]
        sq = [ph.sb(f"sq{i}", [P, width, CH]) for i in range(SB)]
        std = [ph.sb(f"std{i}", [SUB, 4]) for i in range(2)]
        rstd = [ph.sb(f"rstd{i}", [SUB, 4]) for i in range(2)]
        diag = [ph.sb(f"diag{i}", [SUB, 4, SUB]) for i in range(2)]
        mean_ps = [ph.ps(f"mean{i}", [P, 512]) for i in range(2)]
        var_ps = [ph.ps(f"var{i}", [SUB, 512]) for i in range(2)]
        rstd_ps = [ph.ps(f"rstdps{i}", [P, 512]) for i in range(2)]
        mean_done, centred, squared, var_done, std_done, inverted, diag_done, spread_done, scaled, normed, hi_done, stored = (
            ph.sem(n) for n in ("mean", "centred", "squared", "var", "stdd", "inv", "diag", "spread", "scaled", "normed",
                                "hid", "st"))
        if gain is None:
            normed = scaled

        def cols(t, c):
            return t[:, :, c * CH:(c + 1) * CH]

        def spread(t):
            return t.unsqueeze(1).to_broadcast([P, width, CH])

        with nc.Block() as block:
            @block.tensor
            def _(pe):
                def mean(c):
                    if c >= 2:
                        pe.wait_ge(centred, c - 1)
                    for k in range(width):
                        mm = pe.matmul(mean_ps[c % 2][:, 0:CH], mean_w, cols(x, c)[:, k, :],
                                       start=(k == 0), stop=(k == width - 1))
                    mm.then_inc(mean_done, 1)

                def var(c):
                    pe.wait_ge(squared, c + 1)
                    if c >= 2:
                        pe.wait_ge(std_done, c - 1)
                    for j in range(4):
                        for k in range(width):
                            mm = pe.matmul(var_ps[c % 2][:, j:j + 1], sq[c % SB][:, k, j * SUB:(j + 1) * SUB],
                                           mean_w[:, 0:1], start=(k == 0), stop=(k == width - 1))
                    mm.then_inc(var_done, 1)

                def spread_inverse(c):
                    pe.wait_ge(diag_done, c + 1)
                    if c >= 2:
                        pe.wait_ge(scaled, c - 1)
                    for j in range(4):
                        mm = pe.matmul(rstd_ps[c % 2][:, j * SUB:(j + 1) * SUB], ones[0:SUB, :], diag[c % 2][:, j, :],
                                       start=True, stop=True)
                    mm.then_inc(spread_done, 1)

                mean(0)
                mean(1)
                for s in range(NCH + 1):
                    if s + 2 < NCH:
                        mean(s + 2)
                    if s < NCH:
                        var(s)
                    if s >= 1:
                        spread_inverse(s - 1)

            @block.scalar
            def _(act):
                def square(c):
                    act.wait_ge(centred, c + 1)
                    if c >= SB:
                        act.wait_ge(var_done, c - SB + 1)
                    act.activation(sq[c % SB][:, :, :], xc[c % XB][:, :, :], ACT.Square).then_inc(squared, 1)

                square(0)
                square(1)
                for s in range(NCH + 1):
                    if s < NCH:
                        act.wait_ge(var_done, s + 1)
                        if s >= 2:
                            act.wait_ge(inverted, s - 1)
                        act.activation(std[s % 2][:, :], var_ps[s % 2][:, 0:4], ACT.Sqrt, bias=eps[0:SUB, :])\
                           .then_inc(std_done, 1)
                    if s + 2 < NCH:
                        square(s + 2)
                    if s >= 1:
                        c = s - 1
                        if gain is not None:
                            act.wait_ge(scaled, c + 1)
                            for k in range(width):
                                ins = act.activation(cols(xn, c)[:, k, :], xc[c % XB][:, k, :], ACT.Identity,
                                                     bias=shift[:, k:k + 1], scale=gain[:, k:k + 1])
                            ins.then_inc(normed, 1)
                        if hi is not None:
                            act.wait_ge(normed, c + 1)
                            act.activation(cols(hi, c), cols(xn, c), ACT.Copy).then_inc(hi_done, 1)

            @block.vector
            def _(dve):
                def centre(c):
                    dve.wait_ge(mean_done, c + 1)
                    if c >= XB:
                        dve.wait_ge(squared, c - XB + 1)
                        dve.wait_ge(normed, c - XB + 1)
                    dve.tensor_tensor(xc[c % XB][:, :, :], cols(x, c), spread(mean_ps[c % 2][:, 0:CH]),
                                      ALU.subtract).then_inc(centred, 1)

                centre(0)
                centre(1)
                for s in range(NCH + 2):
                    if s < NCH:
                        dve.wait_ge(std_done, s + 1)
                        if s >= 2:
                            dve.wait_ge(diag_done, s - 1)
                        dve.reciprocal(rstd[s % 2][:, :], std[s % 2][:, :]).then_inc(inverted, 1)
                    if s + 2 < NCH:
                        centre(s + 2)
                    if s < NCH:
                        dve.wait_ge(inverted, s + 1)
                        if s >= 2:
                            dve.wait_ge(spread_done, s - 1)
                        dve.tensor_tensor(diag[s % 2][:, :, :],
                                          identity[0:SUB, 0:SUB].unsqueeze(1).to_broadcast([SUB, 4, SUB]),
                                          rstd[s % 2][:, :].unsqueeze(2).to_broadcast([SUB, 4, SUB]), ALU.mult)\
                           .then_inc(diag_done, 1)
                    if 1 <= s <= NCH:
                        c = s - 1
                        dve.wait_ge(spread_done, c + 1)
                        dve.wait_ge(centred, c + 1)
                        dst = cols(xn, c) if gain is None else xc[c % XB][:, :, :]
                        dve.tensor_tensor(dst, xc[c % XB][:, :, :], spread(rstd_ps[c % 2][:, 0:CH]), ALU.mult)\
                           .then_inc(scaled, 1)
                    if s >= 2:
                        c = s - 2
                        dve.wait_ge(normed, c + 1)
                        if add_to is not None:
                            dve.tensor_tensor(cols(add_to, c), cols(add_to, c), cols(xn, c), ALU.add)
                        if hi is not None:
                            dve.wait_ge(hi_done, c + 1)
                            dve.tensor_tensor(cols(lo, c), cols(xn, c), cols(hi, c).bitcast(F32), ALU.subtract)

            if beside is not None:
                @block.gpsimd
                def _(pool):
                    beside[1](pool)

            if spill is not None or beside is not None:
                @block.sync
                def _(sp):
                    if beside is not None:
                        beside[0](sp)
                    if spill is not None:
                        for c in range(NCH):
                            sp.wait_ge(normed, c + 1)
                            sp.dma_start(spill[:, :, c * CH:(c + 1) * CH], cols(xn, c)).then_inc(stored, 16)
                        sp.wait_ge(stored, 16 * NCH)


def preload(ph, name, loads, clear=()):
    got, own = ph.sem(name + "got"), ph.sem(name + "own")

    moved = [(raw, src) for raw, src, _, _ in loads if src is not None]

    def start(sp):
        for raw, src in moved:
            sp.dma_start(raw, src).then_inc(got, 16)

    def program(pool):
        step = Chain(pool, own)
        for raw in clear:
            step(pool.memset(raw, 0.0))
        pool.wait_ge(got, 16 * len(moved))
        last = None
        for raw, _, hi, lo in loads:
            if hi is not None:
                step(pool.tensor_copy(hi, raw))
                last = pool.tensor_tensor(lo, raw, hi.bitcast(F32), ALU.subtract)
        return last

    return start, program


def split_loads(nc, name, loads, init):
    with Phase(nc, name) as ph:
        got = [ph.sem(f"got{i}") for i in range(len(loads))]
        hi_done = ph.sem("hid")
        with nc.Block() as block:
            @block.sync
            def _(sp):
                for s, (raw, src, _, _) in zip(got, loads):
                    sp.dma_start(raw, src).then_inc(s, 16)
                init[0](sp)

            @block.scalar
            def _(act):
                for s, (raw, _, hi, _) in zip(got, loads):
                    act.wait_ge(s, 16)
                    act.activation(hi, raw, ACT.Copy).then_inc(hi_done, 1)

            @block.vector
            def _(dve):
                init[1](dve)
                for n, (raw, _, hi, lo) in enumerate(loads):
                    dve.wait_ge(hi_done, n + 1)
                    dve.tensor_tensor(lo, raw, hi.bitcast(F32), ALU.subtract)


class FfnWeights:

    def __init__(self, ph, J, half, gated, experts):
        GU = 2 * J if gated else J
        if half:
            GU -= 1
        self.GU, self.J = GU, J
        self.passes = 2 if experts > 1 else 1
        self.raw1, self.raw2 = ph.sb("raw1", [P, KT, GU * P]), ph.sb("raw2", [P, J, D])
        self.w1 = [[ph.sb(f"w1{p}{q}", [P, KT, GU * P], F32R) for q in "hl"] for p in range(self.passes)]
        self.w2 = [[ph.sb(f"w2{p}{q}", [P, J, D], F32R) for q in "hl"] for p in range(self.passes)]

    def first(self, ph, load, half=False, more=()):
        clear = [self.raw2[64:P, self.J - 1, :]] if half else []
        start, get = preload(ph, "ffn", [(dst, src, None, None) for dst, src in load(0, self.raw1, self.raw2)]
                      + list(more), clear)
        own = ph.sem("ffnsplit")

        def program(pool):
            get(pool)
            step = Chain(pool, own)
            for raw, parts in ((self.raw1, self.w1[0]), (self.raw2, self.w2[0])):
                step(pool.tensor_copy(parts[0][:, :, :], raw[:, :, :]))
                pool.tensor_tensor(parts[1][:, :, :], raw[:, :, :], parts[0][:, :, :].bitcast(F32), ALU.subtract)

        return start, program


def gated_ffn(nc, name, *, weights, x_hi, x_lo, chunks, J, half, gated, func, experts, load, w_mult, finish,
              lag, up_bias=None, out_bias=None, store=None, output=None):
    NC = len(chunks)
    N = chunks[0][1]
    GU, PASSES = weights.GU, weights.passes
    FULL = J - 1 if half else J
    S = PASSES * NC * J
    with Phase(nc, name) as ph:
        raw1, raw2, w1, w2 = weights.raw1, weights.raw2, weights.w1, weights.w2
        hid_hi = ph.sb("hidhi", [P, J, N], F32R)
        hid_lo = ph.sb("hidlo", [P, J, N], F32R)
        gate_sb = [ph.sb(f"gate{i}", [P, N]) for i in range(2)]
        up_half = ph.sb("uphalf", [64, N]) if half else None
        hidden = [ph.sb(f"hidden{i}", [P, N]) for i in range(2)]
        out_sb = [ph.sb(f"out{i}", [P, KT, N]) for i in range(2)]
        factor = [ph.sb(f"factor{p}", [P, T]) for p in range(PASSES)] if w_mult is not None else None
        gu_ps = [ph.ps(f"gu{i}", [P, 2, 512]) for i in range(3)]
        out_ps = ph.ps("outps", [P, KT, 512])
        raw_in, split_done, own = (ph.sem(n) for n in ("raw", "split", "own"))
        gu_done, gate_done, hid_made, hi_done, lo_done, down_done, out_done, evacuated, added, up_done = (
            ph.sem(n) for n in ("gu", "gated", "hid", "hi", "lo", "down", "outd", "evac", "added", "updone"))
        factor_in = [ph.sem(f"factor{p}") for p in range(PASSES)] if factor else None
        stored = ph.sem("stored")
        start = ph.sb("start", [P, 1])
        CREDIT = 1 if experts > 1 else 0

        def turns(eng, body):
            if experts > 1:
                with eng.Fori(0, experts // PASSES) as it:
                    body(it)
            else:
                body(0)

        def where(s):
            return s // (NC * J), s // J % NC, s % J

        def is_half(s):
            return half and s % J == J - 1

        with nc.Block() as block:
            @block.sync
            def _(sp):
                for e in range(experts):
                    if e >= 1:
                        if e >= 2:
                            sp.wait_ge(split_done, e)
                        for dst, src in load(e, raw1, raw2):
                            sp.dma_start(dst, src).then_inc(raw_in, 16)
                    if factor:
                        if e >= PASSES:
                            sp.wait_ge(evacuated, (e - PASSES + 1) * NC + CREDIT)
                        sp.dma_start(factor[e % PASSES][:, :], w_mult(e)).then_inc(factor_in[e % PASSES], 16)
                if output is not None:
                    for c in range(NC):
                        sp.wait_ge(added, c + 1)
                        sp.dma_start(output(c), finish(c)).then_inc(stored, 16)
                    sp.wait_ge(stored, 16 * NC)

            @block.gpsimd
            def _(pool):
                step = Chain(pool, own)
                if half:
                    pool.memset(hid_hi[64:P, J - 1, :].bitcast(F32), 0.0).then_inc(added, CREDIT)
                    pool.wait_ge(added, CREDIT)
                    pool.memset(hid_lo[64:P, J - 1, :].bitcast(F32), 0.0).then_inc(split_done, 1)
                    pool.wait_ge(split_done, 1)

                n_raw = len(load(0, raw1, raw2)) if experts > 1 else 0

                def pieces(e):
                    p = e % PASSES
                    W = GU * P // 4
                    out = [(raw1[:, :, i * W:(i + 1) * W], w1[p][0][:, :, i * W:(i + 1) * W],
                            w1[p][1][:, :, i * W:(i + 1) * W]) for i in range(4)]
                    J2 = J // 2
                    out += [(raw2[:, a:b, :], w2[p][0][:, a:b, :], w2[p][1][:, a:b, :])
                            for a, b in ((0, J2), (J2, J))]
                    return out

                def split(e, i):
                    if i == 0:
                        pool.wait_ge(raw_in, 16 * n_raw * e)
                        if e >= PASSES:
                            pool.wait_ge(out_done, (e - PASSES + 1) * NC)
                    raw, hi, lo = pieces(e)[i]
                    step(pool.tensor_copy(hi, raw))
                    last = pool.tensor_tensor(lo, raw, hi.bitcast(F32), ALU.subtract)
                    if i == 5:
                        last.then_inc(split_done, 1)

                for e in range(experts):
                    for c in range(NC):
                        if e + 1 < experts:
                            split(e + 1, c)
                        pool.wait_ge(evacuated, e * NC + c + 1 + CREDIT)
                        dst = finish(c)
                        if store is None:
                            ins = pool.tensor_tensor(dst, dst, out_sb[c % 2][:, :, :], ALU.add)
                        else:
                            ins = pool.tensor_copy(dst, out_sb[c % 2][:, :, :])
                        ins.then_inc(added, 1)

            @block.tensor
            def _(pe):
                def first(it, s):
                    p, c, j = where(s)
                    if experts > 1 and c == 0 and j == 0:
                        pe.wait_ge(split_done, it * PASSES + p + 1)
                    if s >= 3:
                        pe.wait_ge(hid_made, it * S + s - 2)
                    a, n = chunks[c]
                    tiles = [(0, j)]
                    if gated and not is_half(s):
                        tiles.append((1, FULL + j))
                    if is_half(s):
                        tiles = [(0, 2 * FULL)]
                    for g, m in tiles:
                        for k in range(KT):
                            w = [w1[p][q][:, k, m * P:(m + 1) * P] for q in range(2)]
                            mm = split_product(pe, gu_ps[s % 3][:, g, 0:N], w[0], w[1], x_hi[:, k, a:a + n],
                                               x_lo[:, k, a:a + n], k == 0, k == KT - 1)
                    mm.then_inc(gu_done, 1)

                def down(it, s):
                    p, c, j = where(s)
                    pe.wait_ge(lo_done, it * S + s + 1)
                    if j == 0 and (experts > 1 or s > 0):
                        pe.wait_ge(evacuated, it * PASSES * NC + s // J + CREDIT)
                    for m in range(KT):
                        w = [w2[p][q][:, j, m * P:(m + 1) * P] for q in range(2)]
                        mm = split_product(pe, out_ps[:, m, 0:N], w[0], w[1], hid_hi[:, j, :],
                                           hid_lo[:, j, :], j == 0, j == J - 1)
                    if j == J - 1:
                        mm.then_inc(out_done, 1)
                    else:
                        mm.then_inc(down_done, 1)

                def body(it):
                    for s in range(S + lag):
                        if s < S:
                            first(it, s)
                        if s >= lag:
                            down(it, s - lag)

                turns(pe, body)

            def slot_free(eng, it, s):
                if s >= J:
                    q = s - J
                    if q % J == J - 1:
                        eng.wait_ge(out_done, it * (S // J) + q // J + 1)
                    else:
                        eng.wait_ge(down_done, it * (S // J) * (J - 1) + q // J * (J - 1) + q % J + 1)

            @block.scalar
            def _(act):
                def body(it):
                    for s in range(S + 1):
                        if s < S:
                            act.wait_ge(gu_done, it * S + s + 1)
                            r = 64 if is_half(s) else P
                            src = gu_ps[s % 3][0:r, 0, 0:N]
                            if gated:
                                if s >= 2:
                                    act.wait_ge(hid_made, it * S + s - 1)
                                ins = act.activation(gate_sb[s % 2][0:r, :], src, func)
                                ins.then_inc(gate_done, 1)
                                if is_half(s):
                                    act.activation(up_half[:, :], gu_ps[s % 3][64:P, 0, 0:N], ACT.Copy)\
                                       .then_inc(up_done, 1)
                            else:
                                if s >= 2:
                                    act.wait_ge(lo_done, it * S + s - 1)
                                act.activation(hidden[s % 2][:, :], src, func, bias=up_bias[:, s % J:s % J + 1])\
                                   .then_inc(hid_made, 1)
                        if gated and s >= 1:
                            q = s - 1
                            r = 64 if is_half(q) else P
                            act.wait_ge(hid_made, it * S + q + 1)
                            slot_free(act, it, q)
                            act.activation(hid_hi[0:r, q % J, :], hidden[q % 2][0:r, :], ACT.Copy)\
                               .then_inc(hi_done, 1)
                turns(act, body)

            @block.vector
            def _(dve):
                def low(it, q):
                    r = 64 if is_half(q) else P
                    if not gated:
                        dve.wait_ge(hid_made, it * S + q + 1)
                        slot_free(dve, it, q)
                        dve.tensor_copy(hid_hi[:, q % J, :], hidden[q % 2][:, :]).then_inc(hi_done, 1)
                    dve.wait_ge(hi_done, it * S + q + 1)
                    dve.tensor_tensor(hid_lo[0:r, q % J, :], hidden[q % 2][0:r, :],
                                      hid_hi[0:r, q % J, :].bitcast(F32), ALU.subtract).then_inc(lo_done, 1)

                def evacuate(it, n):
                    p, c = n // NC, n % NC
                    a, _ = chunks[c]
                    dve.wait_ge(out_done, it * PASSES * NC + n + 1)
                    if n >= 2:
                        dve.wait_ge(added, it * PASSES * NC + n - 1 + CREDIT)
                    elif experts > 1:
                        dve.wait_ge(added, it * PASSES * NC + CREDIT)
                    if factor and c == 0:
                        dve.wait_ge(factor_in[p], 16 * it + 16)
                    dst = out_sb[n % 2]
                    if out_bias is not None:
                        for m in range(KT):
                            ins = dve.scalar_tensor_tensor(out=dst[:, m, :], in0=out_ps[:, m, 0:N],
                                                           scalar=out_bias[:, m:m + 1],
                                                           in1=factor[p][:, a:a + N], op0=ALU.add, op1=ALU.mult)
                    elif factor:
                        f = factor[p][:, a:a + N].unsqueeze(1).to_broadcast([P, KT, N])
                        ins = dve.tensor_tensor(dst[:, :, :], out_ps[:, :, 0:N], f, ALU.mult)
                    else:
                        ins = dve.tensor_copy(dst[:, :, :], out_ps[:, :, 0:N])
                    ins.then_inc(evacuated, 1)

                def body(it):
                    if gated:
                        for s in range(S + 1):
                            if s < S:
                                dve.wait_ge(gate_done, it * S + s + 1)
                                if s >= 2:
                                    dve.wait_ge(lo_done, it * S + s - 1)
                                    dve.wait_ge(hi_done, it * S + s - 1)
                                if is_half(s):
                                    dve.wait_ge(up_done, it * PASSES * NC + s // J + 1)
                                    dve.tensor_tensor(hidden[s % 2][0:64, :], up_half[:, :], gate_sb[s % 2][0:64, :],
                                                      ALU.mult).then_inc(hid_made, 1)
                                else:
                                    dve.tensor_tensor(hidden[s % 2][:, :], gu_ps[s % 3][:, 1, 0:N],
                                                      gate_sb[s % 2][:, :], ALU.mult).then_inc(hid_made, 1)
                            if s >= 1:
                                low(it, s - 1)
                            done = s + 1 - J - lag
                            if done >= 0 and done % J == 0:
                                evacuate(it, done // J)
                        for n in range(PASSES * NC):
                            if n * J + J + lag - 1 > S:
                                evacuate(it, n)
                    else:
                        n = 0
                        for s in range(S):
                            low(it, s)
                            done = s + 1 - J - lag
                            if done >= 0 and done % J == 0:
                                evacuate(it, done // J)
                                n += 1
                        for m in range(n, PASSES * NC):
                            evacuate(it, m)

                if experts > 1:
                    dve.memset(start[:, :], 0.0).then_inc(evacuated, CREDIT)
                turns(dve, body)


def attention(nc, name, *, q_scr, k_scr, v_scr, o_scr, m_scr, scale, toeplitz, consts):
    NB = 4
    UNITS = 8
    QA = 256
    QB = SP - QA
    QL = SP - 384
    A, BC = 512, QB + QL
    PW = A + 2 * BC + 4
    CREDIT = 2
    with Phase(nc, name) as ph:
        qst = [ph.sb(f"q{i}", [P, HG, SP], F32R) for i in range(NB)]
        kst = [ph.sb(f"k{i}", [P, HG, SP], F32R) for i in range(NB)]
        vst = [ph.sb(f"v{i}", [P, 5, HG, 32]) for i in range(NB)]
        prob = [ph.sb(f"prob{i}", [P, HG, PW]) for i in range(2)]
        mx = [ph.sb(f"mx{i}", [P, 32]) for i in range(2)]
        mneg = [ph.sb(f"mneg{i}", [P, 32], F32R) for i in range(2)]
        mxt = [ph.sb(f"mxt{i}", [P, 32], F32R) for i in range(2)]
        o_sb = [ph.sb(f"osb{i}", [P, SP]) for i in range(2)]
        warm = ph.sb("warm", [P, 3])
        max_ps = ph.ps("max", [P, 3 * 512])
        s_ps = ph.ps("s", [P, 3, 512])
        o_ps = ph.ps("o", [P, 2, 512])
        ident, flip, diag, tail, mask2 = (consts[n] for n in ("ident", "flip", "diag", "tail", "mask2"))
        q_in = [ph.sem(f"qin{i}") for i in range(NB)]
        dve_clear, pool_clear, max_mm, max_read, m_made, m_out, s_mm, exp_done, pv_done, o_copied, own = (
            ph.sem(n) for n in ("dclear", "pclear", "maxmm", "maxrd", "mmade", "mout", "smm", "exp", "pv", "ocp", "own"))
        m_in = [ph.sem(f"min{i}") for i in range(2)]
        o_out = [ph.sem(f"oout{i}") for i in range(2)]
        LOADS = 6
        ML = 2
        NU = B * H // HG

        def unit(u):
            return u // B, u % B

        with nc.Block() as block:
            @block.gpsimd
            def _(pool):
                for i in range(NB // 2, NB):
                    pool.memset(qst[i][:, :, :].bitcast(F32), 0.0).then_inc(pool_clear, 1)
                    pool.memset(kst[i][:, :, :].bitcast(F32), 0.0).then_inc(pool_clear, 1)

            @block.sync
            def _(sp):
                def load(u):
                    hg, b = unit(u)
                    i = u % NB
                    if u < NB // 2:
                        sp.wait_ge(dve_clear, 2 * u + 2)
                    elif u < NB:
                        sp.wait_ge(pool_clear, 2 * (u - NB // 2) + 2)
                    else:
                        sp.wait_ge(pv_done, u - NB + 1)
                    for scr, tiles, n, first in ((q_scr, qst, SEQ, HD), (k_scr, kst, SP, 0)):
                        src = scr[hg * HG:(hg + 1) * HG, :, b * SP:b * SP + n].rearrange("h r t -> r h t")
                        sp.dma_start(tiles[i][0:HD, :, 0:n].bitcast(F32), src[first:first + HD]).then_inc(q_in[i], 16)
                        sp.dma_start(tiles[i][HD:3 * HD + 1, :, 0:n].bitcast(F32), src).then_inc(q_in[i], 16)
                    cols = slice(hg * HG * 32, (hg + 1) * HG * 32)
                    sp.dma_start(vst[i][:, 0:4, :, :].rearrange("p n h c -> p n (h c)"),
                                 v_scr[b * SP:b * SP + 512, cols].rearrange("(n p) c -> p n c", p=P))\
                      .then_inc(q_in[i], 16)
                    sp.dma_start(vst[i][:, 4, :, :].rearrange("p h c -> p (h c)"),
                                 v_scr[(b + 1) * SP - P:(b + 1) * SP, cols]).then_inc(q_in[i], 16)

                def maxima(u):
                    i, scr = u % NB, m_scr[u % 2]
                    sp.wait_ge(m_made, u + 1)
                    sp.dma_start(scr.rearrange("(r k) f -> k r f", k=4), mxt[u % 2][:, :].bitcast(F32)).then_inc(m_out, 16)
                    sp.wait_ge(m_out, 16 * (u + 1))
                    row = qst[i][3 * HD:3 * HD + 1, :, :].bitcast(F32)
                    sp.dma_start(row[:, :, 1:SEQ], scr[0:64].rearrange("(o h n) f -> o h (n f)", o=1, h=HG))\
                      .then_inc(m_in[u % 2], 16)
                    sp.dma_start(row[:, :, 0:1], scr.rearrange("(o r k) f -> o r k f", k=4, o=1)[:, 16:16 + HG, 0, 0:1],
                                 allow_slow_non_contiguous=True).then_inc(m_in[u % 2], 16)

                def store(u):
                    hg, b = unit(u)
                    sp.wait_ge(o_copied, u + 1 + 1)
                    sp.dma_start(o_scr[hg * P:(hg + 1) * P, b * SP:b * SP + SEQ], o_sb[u % 2][:, 0:SEQ])\
                      .then_inc(o_out[u % 2], 16)

                for u in range(min(3, NU)):
                    load(u)
                if toeplitz is not None:
                    toeplitz["load"](sp, 1)
                for u in range(NU + 1):
                    if u % UNITS == 0 and u < NU:
                        if u >= 1:
                            store(u - 1)
                        maxima(u)
                        maxima(u + 1)
                    if u + 3 < NU:
                        load(u + 3)
                    if u % UNITS and u < NU or u == NU:
                        store(u - 1)
                    if toeplitz is not None and u == B + 1:
                        sp.wait_ge(s_mm, 2 * HG * B)
                        sp.wait_ge(max_read, 2 * HG * B + CREDIT)
                        toeplitz["load"](sp, 2)
                    if toeplitz is not None and u == 2 * B:
                        toeplitz["load"](sp, 3)
                    if u < NU and u % UNITS + 2 < UNITS:
                        maxima(u + 2)
                for i in range(2):
                    sp.wait_ge(o_out[i], 16 * (NU // 2))

            @block.tensor
            def _(pe):
                def maxima_mm(it, u, h):
                    i = u % NB
                    if h == 0:
                        pe.wait_ge(q_in[i], it * (UNITS // NB) * 16 * LOADS + (u // NB + 1) * 16 * LOADS)
                    n = it * UNITS * HG + u * HG + h
                    pe.wait_ge(max_read, 2 * n - 1 + CREDIT)
                    pe.matmul(max_ps[:, 0:130], qst[i][:, h, 1:1 + P], kst[i][:, h, 0:130], start=True, stop=True)
                    pe.matmul(max_ps[:, 130:388], qst[i][:, h, 129:129 + P], kst[i][:, h, 0:258],
                              start=True, stop=True)
                    pe.matmul(max_ps[:, 388:390], qst[i][:, h, 0:P], kst[i][:, h, 0:2], start=True, stop=True)
                    pe.matmul(max_ps[:, 508:512], qst[i][:, h, 385:385 + P], kst[i][:, h, 0:4],
                              start=True, stop=True).then_inc(max_mm, 1)
                    pe.matmul(max_ps[:, 512:1024], qst[i][:, h, 385:385 + P], kst[i][:, h, 4:SP],
                              start=True, stop=True).then_inc(max_mm, 1)
                    pe.wait_ge(max_read, 2 * n + CREDIT)
                    pe.matmul(max_ps[:, 1024:1410], qst[i][:, h, 257:257 + P], kst[i][:, h, 0:386],
                              start=True, stop=True).then_inc(max_mm, 1)

                def scores(it, u, h):
                    i = u % NB
                    n = it * UNITS * HG + u * HG + h
                    slot = (u // B) % 2
                    if h == 0:
                        pe.wait_ge(m_in[u % 2], it * (UNITS // 2) * 16 * ML + (u // 2 + 1) * 16 * ML)
                        if toeplitz is not None and u % B == 0:
                            pe.wait_ge(toeplitz["loaded"][slot], 16 * toeplitz["n"] * (it + 1))

                    def products(bank, plan, last):
                        for j, (c, k0, q0, nq) in enumerate(plan):
                            mm = pe.matmul(s_ps[:, bank, c:c + nq], kst[i][:, h, k0:k0 + P], qst[i][:, h, q0:q0 + nq],
                                           start=(j == 0), stop=last, skip_group_check=True)
                        return mm

                    def biased(bank, plan):
                        for c, times, a, nq in plan:
                            for part in ("hi", "lo"):
                                src = toeplitz[part][slot][:, h:h + 1, a:a + nq]
                                mm = pe.matmul(s_ps[:, bank, c:c + times * nq], flip,
                                               src.to_broadcast([P, times, nq]) if times > 1 else src[:, 0, :],
                                               start=False, stop=(part == "lo"), skip_group_check=True)
                        return mm

                    whole = toeplitz is None
                    pe.wait_ge(exp_done, 2 * n - 1 + CREDIT)
                    mm = products(0, ((0, P, P, P), (P, 2 * P, QA, P), (QA, 0, 0, QA)), False)
                    if toeplitz is not None:
                        mm = biased(0, ((0, 3, 0, P), (3 * P, 1, P, P)))
                    else:
                        mm = pe.matmul(s_ps[:, 0, 0:3 * P], ident, diag[:, :].unsqueeze(1).to_broadcast([P, 3, P]),
                                       start=False, stop=True, skip_group_check=True)
                    mm.then_inc(s_mm, 1)
                    pe.wait_ge(exp_done, 2 * n + CREDIT)
                    products(1, ((0, 0, QA, QB), (QB, 3 * P, 384, QL), (BC, SP - P, 512, 4)), False)
                    mm = products(2, ((0, P, QA, QB), (QB, 2 * P, 384, QL)), whole)
                    if toeplitz is not None:
                        biased(1, ((0, 1, QA, QB), (QB, 1, 0, QL)))
                        for part in ("hi", "lo"):
                            pe.matmul(s_ps[:, 1, BC:BC + 4], flip, toeplitz["tail_" + part][slot][:, h, :], start=False,
                                      stop=(part == "lo"), skip_group_check=True)
                        mm = biased(2, ((0, 1, P, QB), (QB, 1, P, QL)))
                    else:
                        pe.matmul(s_ps[:, 1, QB:QB + P], ident, diag, start=False, stop=True, skip_group_check=True)
                        mm = pe.matmul(s_ps[:, 1, BC:BC + 4], ident, tail, start=False, stop=True,
                                       skip_group_check=True)
                    mm.then_inc(s_mm, 1)

                def values(it, u):
                    i = u % NB
                    pr = prob[u % 2]
                    n = it * UNITS + u
                    pe.wait_ge(exp_done, 2 * HG * (n + 1) + CREDIT)
                    pe.wait_ge(o_copied, n + 1)
                    plan = [(0, 0, 0, QA, 2 * P), (0, 1, P, P, 0),
                            (1, 0, 0, QB, A), (1, 1, 0, QB, A + BC), (1, 2, 0, P, P), (1, 2, P, QL, A + BC + QB),
                            (1, 3, P, QL, A + QB), (1, 4, QA, 4, A + 2 * BC)]
                    for bank, t, c0, w, src in plan:
                        for h in range(HG):
                            mm = pe.matmul(o_ps[32 * h:32 * h + 32, bank, c0:c0 + w], vst[i][:, t, h, :],
                                           pr[:, h, src:src + w], start=(t == 0), stop=(t == (1 if bank == 0 else 4)),
                                           skip_group_check=True)
                    mm.then_inc(pv_done, 1)

                with pe.Fori(0, NU // UNITS) as it:
                    for u in range(2):
                        for h in range(HG):
                            maxima_mm(it, u, h)
                    for u in range(UNITS + 1):
                        for h in range(HG):
                            if u < UNITS:
                                scores(it, u, h)
                            if u + 2 < UNITS:
                                maxima_mm(it, u + 2, h)
                            if h == 0 and u >= 1:
                                values(it, u - 1)

            @block.scalar
            def _(act):
                def exps(it, u, h):
                    n = it * UNITS * HG + u * HG + h
                    pr = prob[u % 2]
                    if h == 0 and u >= 2:
                        act.wait_ge(pv_done, it * UNITS + u - 1)
                    act.wait_ge(s_mm, 2 * n + 1)
                    act.activation(pr[:, h, 0:A], s_ps[:, 0, :], ACT.Exp, scale=scale).then_inc(exp_done, 1)
                    act.wait_ge(s_mm, 2 * n + 2)
                    act.activation(pr[:, h, A:A + 2 * BC].rearrange("p (t q) -> p t q", t=2), s_ps[:, 1:3, 0:BC],
                                   ACT.Exp, scale=scale)
                    act.activation(pr[:, h, A + 2 * BC:PW], s_ps[:, 1, BC:BC + 4], ACT.Exp, scale=scale)\
                       .then_inc(exp_done, 1)

                def copy_out(it, u):
                    n = it * UNITS + u
                    act.wait_ge(pv_done, n + 1)
                    if u >= 2:
                        act.wait_ge(o_out[u % 2], it * (UNITS // 2) * 16 + u // 2 * 16)
                    act.activation(o_sb[u % 2][:, 0:QA], o_ps[:, 0, 0:QA], ACT.Copy)
                    act.activation(o_sb[u % 2][:, QA:SP], o_ps[:, 1, 0:QB], ACT.Copy).then_inc(o_copied, 1)

                act.wait_ge(dve_clear, 1)
                act.activation(warm[:, 1:2], warm[:, 0:1], ACT.Exp).then_inc(exp_done, CREDIT)
                act.activation(warm[:, 2:3], warm[:, 0:1], ACT.Copy).then_inc(o_copied, 1)
                with act.Fori(0, NU // UNITS) as it:
                    for u in range(UNITS + 1):
                        for h in range(HG):
                            if u < UNITS:
                                exps(it, u, h)
                            if h == 0 and u >= 1:
                                copy_out(it, u - 1)
                    for i in range(2):
                        act.wait_ge(o_out[i], (it + 1) * (UNITS // 2) * 16)

            @block.vector
            def _(dve):
                def bias2(slot, h):
                    return toeplitz["max"][slot][:, h, :] if toeplitz is not None else mask2

                def maxima(it, u, h):
                    slot = (u // B) % 2
                    m = mx[u % 2]
                    n = it * UNITS * HG + u * HG + h
                    t2 = bias2(slot, h)
                    if toeplitz is not None and u % B == 0 and h == 0:
                        dve.wait_ge(toeplitz["loaded"][slot], 16 * toeplitz["n"] * (it + 1))

                    def piece(i, at):
                        a = 384 - 128 * i
                        w = SP if i == 3 else (i + 1) * P + 2
                        src = max_ps[:, at:at + w]
                        return dve.tensor_tensor_reduce(src, src, t2[:, a:a + w], 1.0, 3.0 * NEG, ALU.add, ALU.max,
                                                        m[:, 4 * h + i:4 * h + i + 1])

                    dve.wait_ge(max_mm, 3 * n + 1)
                    dve.tensor_tensor(m[0:1, 16 + h:17 + h], max_ps[0:1, 388:389], t2[0:1, 385:386], ALU.add)
                    piece(0, 0)
                    piece(1, 130)
                    dve.wait_ge(max_mm, 3 * n + 2)
                    dve.memset(m[:, 20 + 2 * h:21 + 2 * h], 0.0)
                    piece(3, 508).then_inc(max_read, 1)
                    dve.wait_ge(max_mm, 3 * n + 3)
                    dve.memset(m[:, 21 + 2 * h:22 + 2 * h], 0.0)
                    piece(2, 1024).then_inc(max_read, 1)

                def turn_maxima(it, u):
                    dve.wait_ge(max_read, 2 * HG * (it * UNITS + u + 1) + CREDIT)
                    dve.tensor_scalar(mneg[u % 2][:, :], mx[u % 2][:, :], -1.0, None, ALU.mult).then_inc(own, 1)
                    if u >= 2:
                        dve.wait_ge(m_in[u % 2], it * (UNITS // 2) * 16 * ML + u // 2 * 16 * ML)
                    else:
                        dve.wait_ge(exp_done, it * 2 * HG * UNITS + CREDIT)
                    dve.wait_ge(own, it * UNITS + u + 1)
                    dve.transpose(mxt[u % 2][:, :].bitcast(F32), mneg[u % 2][:, :].bitcast(F32)).then_inc(m_made, 1)

                dve.memset(warm[:, :], 0.0)
                for i in range(2):
                    dve.memset(mx[i][:, :], 0.0).then_inc(max_read, 1)
                for i in range(NB // 2):
                    dve.memset(qst[i][:, :, :].bitcast(F32), 0.0).then_inc(dve_clear, 1)
                    dve.memset(kst[i][:, :, :].bitcast(F32), 0.0).then_inc(dve_clear, 1)
                dve.wait_ge(max_read, CREDIT)
                with dve.Fori(0, NU // UNITS) as it:
                    for u in range(UNITS):
                        for h in range(HG):
                            maxima(it, u, h)
                        turn_maxima(it, u)


def project(nc, name, *, x_hi, x_lo, kv_hi, kv_lo, w, w_swap, rope, bias, w_v, q_scr, k_scr, v_scr, before=None):
    STEPS = B * 4 * 2
    with Phase(nc, name) as ph:
        val = [ph.sb(f"val{i}", [P, QC]) for i in range(3)]
        t1 = [ph.sb(f"t1{i}", [P, QC]) for i in range(2)] if rope else None
        t2 = [ph.sb(f"t2{i}", [P, QC]) for i in range(2)] if rope else None
        hi = [ph.sb(f"hi{i}", [P, 2, QC], F32R) for i in range(3)]
        lo = [ph.sb(f"lo{i}", [P, 2, QC], F32R) for i in range(3)]
        v_sb = [ph.sb(f"v{i}", [P, H, 32]) for i in range(2)]
        ps = [ph.ps(f"qk{i}", [P, 2, 512]) for i in range(3)]
        ps_v = [ph.ps(f"vps{i}", [P, 512]) for i in range(2)]
        mm_done, val_done, half_done, hi_done, lo_done, v_mm, v_ready, v_copied, own = (
            ph.sem(n) for n in ("mm", "val", "half", "hi", "lo", "vmm", "vready", "vcopied", "own"))
        out_qk = [ph.sem(f"outqk{i}") for i in range(3)]
        out_v = [ph.sem(f"outv{i}") for i in range(2)]

        def tokens(s):
            return slice(s // 8 * SP + s % 2 * QC, s // 8 * SP + s % 2 * QC + QC)

        with nc.Block() as block:
            @block.tensor
            def _(pe):
                def qk(s):
                    m = s // 2 % 4
                    if s >= 3:
                        pe.wait_ge(val_done if not rope else half_done, s - 2)
                    for g, ww in enumerate((w, w_swap) if rope else (w,)):
                        kt, w_hi, w_lo, xh, xl = ww[m]
                        for k in range(kt):
                            mm = split_product(pe, ps[s % 3][:, g, 0:QC], w_hi(k), w_lo(k), xh[:, k, tokens(s)],
                                               xl[:, k, tokens(s)], k == 0, k == kt - 1)
                    mm.then_inc(mm_done, 1)

                def v(i):
                    kt, w_hi, w_lo, xh, xl = w_v
                    a = tile_start(i)
                    if i >= 2:
                        pe.wait_ge(v_copied, i - 1)
                    for k in range(kt):
                        mm = split_product(pe, ps_v[i % 2][:, 0:D], xh[:, k, a:a + P], xl[:, k, a:a + P], w_hi(k),
                                           w_lo(k), k == 0, k == kt - 1)
                    mm.then_inc(v_mm, 1)

                for s in range(STEPS):
                    qk(s)
                    if s % 2:
                        v(s // 2)
                v(NT - 1)

            @block.scalar
            def _(act):
                for s in range(STEPS):
                    m = s // 2 % 4
                    if not rope:
                        act.wait_ge(mm_done, s + 1)
                        if s >= 3:
                            act.wait_ge(lo_done, s - 2)
                        act.activation(val[s % 3][:, :], ps[s % 3][:, 0, 0:QC], ACT.Identity, bias=bias[:, m:m + 1])\
                           .then_inc(val_done, 1)
                    act.wait_ge(val_done, s + 1)
                    if s >= 6:
                        act.wait_ge(out_qk[s // 2 % 3], 32 * (s // 6))
                    act.activation(hi[s // 2 % 3][:, s % 2, :], val[s % 3][:, :], ACT.Copy).then_inc(hi_done, 1)

            @block.vector
            def _(dve):
                def low(s):
                    dve.wait_ge(hi_done, s + 1)
                    dve.tensor_tensor(lo[s // 2 % 3][:, s % 2, :], val[s % 3][:, :],
                                      hi[s // 2 % 3][:, s % 2, :].bitcast(F32), ALU.subtract).then_inc(lo_done, 1)

                def v(i):
                    dve.wait_ge(v_mm, i + 1)
                    dve.wait_ge(v_ready, 4)
                    if i >= 2:
                        dve.wait_ge(out_v[i % 2], 16 * (i // 2))
                    dve.tensor_copy(v_sb[i % 2][:, :, 0:HD], ps_v[i % 2][:, 0:D].rearrange("p (h d) -> p h d", d=HD))\
                       .then_inc(v_copied, 1)

                for s in range(STEPS + 1):
                    if rope and s < STEPS:
                        cos, sin = (t[:, s % 2 * QC:(s % 2 + 1) * QC] for t in rope)
                        dve.wait_ge(mm_done, s + 1)
                        if s >= 2:
                            dve.wait_ge(val_done, s - 1)
                        dve.tensor_tensor(t1[s % 2][:, :], ps[s % 3][:, 0, 0:QC], cos, ALU.mult)
                        dve.tensor_tensor(t2[s % 2][:, :], ps[s % 3][:, 1, 0:QC], sin, ALU.mult).then_inc(half_done, 1)
                    if s >= 1:
                        low(s - 1)
                        if (s - 1) % 2:
                            v((s - 1) // 2)
                v(NT - 1)

            @block.gpsimd
            def _(pool):
                step = Chain(pool, own)
                for i in range(2):
                    step(pool.memset(v_sb[i][:, :, :], 0.0))
                for i in range(2):
                    pool.memset(v_sb[i][:, :, HD:HD + 1], 1.0).then_inc(v_ready, 2)
                if rope:
                    for s in range(STEPS):
                        pool.wait_ge(half_done, s + 1)
                        if s >= 3:
                            pool.wait_ge(lo_done, s - 2)
                        pool.tensor_tensor(val[s % 3][:, :], t1[s % 2][:, :], t2[s % 2][:, :], ALU.add)\
                            .then_inc(val_done, 1)

            @block.sync
            def _(sp):
                if before is not None:
                    before(sp)
                for n in range(STEPS // 2):
                    b, m = n // 4, n % 4
                    sp.wait_ge(lo_done, 2 * n + 2)
                    heads = slice(m % 2 * 8, m % 2 * 8 + 8)
                    scr, parts = (q_scr, (lo, hi)) if m < 2 else (k_scr, (hi, lo))
                    for r, part in enumerate(parts):
                        sp.dma_start(scr[heads, r * HD:(r + 1) * HD, b * SP:(b + 1) * SP],
                                     part[n % 3][:, :, :].rearrange("p a t -> p (a t)").bitcast(F32))\
                          .then_inc(out_qk[n % 3], 16)
                    for i in ([n] if n < STEPS // 2 - 1 else [n, NT - 1]):
                        sp.wait_ge(v_copied, i + 1)
                        skip = i * P - tile_start(i)
                        sp.dma_start(v_scr[i * P:tile_start(i) + P, :],
                                     v_sb[i % 2][skip:P, :, :].rearrange("p h c -> p (h c)")).then_inc(out_v[i % 2], 16)
                for i in range(3):
                    sp.wait_ge(out_qk[i], 32 * ((STEPS // 2 - i + 2) // 3))
                for i in range(2):
                    sp.wait_ge(out_v[i], 16 * ((NT - i + 1) // 2))


def project_out(nc, name, *, get_weights, o_scr, w, hT, spread, xn=None, xn_scr=None, bias=None, v_bias=None):
    R = H * B
    with Phase(nc, name) as ph:
        o = ph.sb("o", [P, KT, T])
        o_hi = ph.sb("ohi", [P, KT, T], F32R)
        o_lo = ph.sb("olo", [P, KT, T], F32R)
        total, inverse, sel = ph.sb("total", [R, SP]), ph.sb("inverse", [R, SP]), ph.sb("sel", [R, B, D])
        ps = [ph.ps(f"y{i}", [P, 512]) for i in range(4)]
        inv_ps = [ph.ps(f"inv{i}", [P, KT, 512]) for i in range(2)]
        loaded = [ph.sem(f"in{b}") for b in range(B)]
        sums_in, cleared, w_ready, xn_in, inverted, inv_mm, divided, hi_done, lo_done, y_mm, y_done = (
            ph.sem(n) for n in ("sums", "clear", "w", "xn", "inverted", "inv", "divided", "hi", "lo", "mm", "y"))

        def tokens(c):
            return slice(c * QC, (c + 1) * QC)

        with nc.Block() as block:
            @block.sync
            def _(sp):
                heads = o_scr.rearrange("(h r) t -> h r t", r=32)
                sp.dma_start(total[:, 0:SEQ], heads[:, HD, :].rearrange("h (b t) -> h b t", b=B)[:, :, 0:SEQ])\
                  .then_inc(sums_in, 16)
                sp.dma_start(sel[:, :, :], spread).then_inc(sums_in, 16)
                get_weights[0](sp)
                for b in range(B):
                    for k in range(KT):
                        sp.dma_start(o[:, k, b * SP:b * SP + SEQ],
                                     heads[k * 8:(k + 1) * 8, 0:HD, b * SP:b * SP + SEQ]).then_inc(loaded[b], 16)
                    if b == 0 and xn is not None:
                        sp.dma_start(xn[:, :, :], xn_scr).then_inc(xn_in, 16)

            @block.gpsimd
            def _(pool):
                pool.memset(total[:, SEQ:SP], 1.0)
                for b in range(B):
                    ins = pool.memset(o[:, :, b * SP + SEQ:(b + 1) * SP], 0.0)
                ins.then_inc(cleared, 1)
                get_weights[1](pool).then_inc(w_ready, 1)

            @block.tensor
            def _(pe):
                def spread_inverse(c):
                    if c >= 2:
                        pe.wait_ge(divided, c - 1)
                    b, a = c // 2, c % 2 * QC
                    for k in range(KT):
                        mm = pe.matmul(inv_ps[c % 2][:, k, 0:QC], sel[:, b, k * P:(k + 1) * P], inverse[:, a:a + QC],
                                       start=True, stop=True)
                    mm.then_inc(inv_mm, 1)

                pe.wait_ge(inverted, 1)
                for c in range(2):
                    spread_inverse(c)
                pe.wait_ge(w_ready, 1)
                for c in range(NQC):
                    pe.wait_ge(lo_done, c + 1)
                    for m in range(KT):
                        n = c * KT + m
                        if n >= 4:
                            pe.wait_ge(y_done, n - 3)
                        for k in range(KT):
                            mm = split_product(pe, ps[n % 4][:, 0:QC], w[0][:, k, m * P:(m + 1) * P],
                                               w[1][:, k, m * P:(m + 1) * P], o_hi[:, k, tokens(c)],
                                               o_lo[:, k, tokens(c)], k == 0, k == KT - 1)
                        mm.then_inc(y_mm, 1)
                    if c + 2 < NQC:
                        spread_inverse(c + 2)

            @block.scalar
            def _(act):
                act.wait_ge(w_ready, 1)
                for c in range(NQC):
                    act.wait_ge(divided, c + 1)
                    t = tokens(c)
                    if v_bias is None:
                        ins = act.activation(o_hi[:, :, t], o[:, :, t], ACT.Copy)
                    else:
                        for k in range(KT):
                            ins = act.activation(o_hi[:, k, t], o[:, k, t], ACT.Identity, bias=v_bias[:, k:k + 1])
                    ins.then_inc(hi_done, 1)

            @block.vector
            def _(dve):
                def divide(c):
                    if c % 2 == 0:
                        dve.wait_ge(loaded[c // 2], 16 * KT)
                    t = tokens(c)
                    dve.wait_ge(inv_mm, c + 1)
                    dve.tensor_tensor(o[:, :, t], o[:, :, t], inv_ps[c % 2][:, :, 0:QC], ALU.mult).then_inc(divided, 1)

                def low(c):
                    t = tokens(c)
                    dve.wait_ge(hi_done, c + 1)
                    if v_bias is None:
                        ins = dve.tensor_tensor(o_lo[:, :, t], o[:, :, t], o_hi[:, :, t].bitcast(F32), ALU.subtract)
                    else:
                        for k in range(KT):
                            ins = dve.scalar_tensor_tensor(out=o_lo[:, k, t], in0=o[:, k, t], scalar=v_bias[:, k:k + 1],
                                                           in1=o_hi[:, k, t].bitcast(F32), op0=ALU.add,
                                                           op1=ALU.subtract)
                    ins.then_inc(lo_done, 1)

                def add(c):
                    t = tokens(c)
                    for m in range(KT):
                        n = c * KT + m
                        dve.wait_ge(y_mm, n + 1)
                        if xn is not None:
                            ins = dve.scalar_tensor_tensor(out=xn[:, m, t], in0=ps[n % 4][:, 0:QC],
                                                           scalar=bias[:, m:m + 1], in1=xn[:, m, t], op0=ALU.add,
                                                           op1=ALU.add)
                        else:
                            ins = dve.tensor_tensor(hT[:, m, t], ps[n % 4][:, 0:QC], hT[:, m, t], ALU.add)
                        ins.then_inc(y_done, 1)

                dve.wait_ge(sums_in, 32)
                dve.wait_ge(cleared, 1)
                dve.reciprocal(inverse[:, :], total[:, :]).then_inc(inverted, 1)
                divide(0)
                divide(1)
                dve.wait_ge(w_ready, 1)
                low(0)
                if xn is not None:
                    dve.wait_ge(xn_in, 16)
                for c in range(NQC):
                    if c + 2 < NQC:
                        divide(c + 2)
                    if c + 1 < NQC:
                        low(c + 1)
                    add(c)


def latent(nc, name, x_hi, x_lo, w, lat):
    with Phase(nc, name) as ph:
        ps = [ph.ps(f"l{i}", [P, 512]) for i in range(2)]
        mm_done, read = ph.sem("mm"), ph.sem("read")
        with nc.Block() as block:
            @block.tensor
            def _(pe):
                for c in range(NCH):
                    if c >= 2:
                        pe.wait_ge(read, c - 1)
                    t = slice(c * CH, (c + 1) * CH)
                    for k in range(KT):
                        mm = split_product(pe, ps[c % 2][:, 0:CH], w[0][:, k, :], w[1][:, k, :], x_hi[:, k, t],
                                           x_lo[:, k, t], k == 0, k == KT - 1)
                    mm.then_inc(mm_done, 1)

            @block.scalar
            def _(act):
                for c in range(NCH):
                    act.wait_ge(mm_done, c + 1)
                    act.activation(lat[:, 0, c * CH:(c + 1) * CH], ps[c % 2][:, 0:CH], ACT.Copy).then_inc(read, 1)


def router(nc, name, *, xn, w, ne, identity, scr, gain=None, before=None):
    with Phase(nc, name) as ph:
        ps = ph.ps("logits", [P, 512])
        ps_t = ph.ps("turned", [P, 2, 512])
        logit = ph.sb("logit", [P, NT, ne])
        prob = ph.sb("prob", [P, NT, ne])
        beats = ph.sb("beats", [P, NT, ne, ne])
        tied = ph.sb("tied", [P, NT, ne, ne])
        rank = ph.sb("rank", [P, NT, ne])
        one = ph.sb("one", [P, NT])
        two = ph.sb("two", [P, NT])
        best = ph.sb("best", [P, NT, 8])
        fac = ph.sb("fac", [P, 256])
        fac_t = ph.sb("fact", [P, 2, P])
        mm_done, scaled, e_done, own, fac_done, turned, copied, out = (
            ph.sem(n) for n in ("mm", "scaled", "exp", "own", "fac", "turned", "copied", "out"))

        with nc.Block() as block:
            @block.tensor
            def _(pe):
                for i in range(NT):
                    a = tile_start(i)
                    for k in range(KT):
                        mm = pe.matmul(ps[:, i * 8:i * 8 + ne], xn[:, k, a:a + P], w[:, k, :],
                                       start=(k == 0), stop=(k == KT - 1))
                mm.then_inc(mm_done, 1)
                pe.wait_ge(fac_done, 1)
                for g in range(2):
                    mm = pe.transpose(ps_t[:, g, 0:P], fac[:, g * P:(g + 1) * P], identity)
                mm.then_inc(turned, 1)

            @block.scalar
            def _(act):
                act.wait_ge(scaled, 1)
                act.activation(prob[:, :, :], logit[:, :, :], ACT.Exp, scale=(-1.0 if gain is not None else 1.0))\
                   .then_inc(e_done, 1)

            @block.vector
            def _(dve):
                step = Chain(dve, own)
                each = [P, NT, ne]
                step(dve.memset(fac[:, :], 0.0))
                dve.wait_ge(mm_done, 1)
                raw = ps[:, 0:NT * 8].rearrange("p (n e) -> p n e", e=8)[:, :, 0:ne]
                if gain is not None:
                    step(dve.tensor_tensor(rank[:, :, :], raw, gain.unsqueeze(1).to_broadcast(each), ALU.mult))
                    dve.tensor_scalar(logit[:, :, :], rank[:, :, :], -87.0, None, ALU.max).then_inc(scaled, 1)
                    dve.wait_ge(e_done, 1)
                    step(dve.tensor_scalar(rank[:, :, :], prob[:, :, :], 1.0, None, ALU.add))
                    step(dve.reciprocal(prob[:, :, :], rank[:, :, :]))
                    other = prob[:, :, :].unsqueeze(2).to_broadcast([P, NT, ne, ne])
                    this = prob[:, :, :].unsqueeze(3).to_broadcast([P, NT, ne, ne])
                    step(dve.tensor_tensor(tied[:, :, :, :], other, this, ALU.is_equal))
                    for n in range(ne):
                        ins = dve.memset(tied[:, :, n, n:ne], 0.0)
                    step(ins)
                    step(dve.tensor_tensor(beats[:, :, :, :], other, this, ALU.is_gt))
                    step(dve.tensor_tensor(beats[:, :, :, :], beats[:, :, :, :], tied[:, :, :, :], ALU.add))
                    step(dve.tensor_reduce(rank[:, :, :], beats[:, :, :, :], AX.X, ALU.add))
                    step(dve.tensor_scalar(rank[:, :, :], rank[:, :, :], 1.5, None, ALU.is_lt))
                    step(dve.tensor_tensor(rank[:, :, :], rank[:, :, :], prob[:, :, :], ALU.mult))
                    step(dve.tensor_reduce(one[:, :], rank[:, :, :], AX.X, ALU.add))
                    step(dve.reciprocal(two[:, :], one[:, :]))
                    f = fac[:, 0:NT * 8].rearrange("p (n e) -> p n e", e=8)
                    dve.memset(f[:, :, ne:8], 1.0)
                    dve.tensor_tensor(f[:, :, 0:ne], rank[:, :, :], two[:, :].unsqueeze(2).to_broadcast(each), ALU.mult)\
                       .then_inc(fac_done, 1)
                else:
                    step(dve.tensor_reduce(one[:, :], raw, AX.X, ALU.max))
                    dve.tensor_tensor(logit[:, :, :], raw, one[:, :].unsqueeze(2).to_broadcast(each), ALU.subtract)\
                       .then_inc(scaled, 1)
                    dve.wait_ge(e_done, 1)
                    step(dve.tensor_reduce(one[:, :], prob[:, :, :], AX.X, ALU.add))
                    step(dve.reciprocal(two[:, :], one[:, :]))
                    step(dve.tensor_tensor(rank[:, :, :], prob[:, :, :], two[:, :].unsqueeze(2).to_broadcast(each), ALU.mult))
                    for i in range(NT):
                        ins = dve.max(best[:, i, :], rank[:, i, :])
                    step(ins)
                    step(dve.tensor_tensor(one[:, :], best[:, :, 0], best[:, :, 1], ALU.add))
                    step(dve.reciprocal(two[:, :], one[:, :]))
                    step(dve.tensor_tensor(best[:, :, 0:2], best[:, :, 0:2], two[:, :].unsqueeze(2).to_broadcast([P, NT, 2]),
                                           ALU.mult))
                    dve.tensor_tensor(fac[:, 0:NT], best[:, :, 0], best[:, :, 1], ALU.add).then_inc(fac_done, 1)
                dve.wait_ge(turned, 1)
                dve.tensor_copy(fac_t[:, :, :], ps_t[:, :, 0:P]).then_inc(copied, 1)

            @block.sync
            def _(sp):
                if before is not None:
                    before(sp)
                sp.wait_ge(copied, 1)
                whole = T // P * P
                if gain is not None:
                    sp.dma_start(scr[:, 0:whole].rearrange("e (n t) -> n e t", t=P), fac_t[:, 0, :]).then_inc(out, 16)
                    sp.dma_start(scr[:, whole:T], fac_t[0:8, 1, P - (T - whole):P]).then_inc(out, 16)
                else:
                    sp.dma_start(scr[:, 0:whole].rearrange("e (n t) -> (e n) t", t=P), fac_t[0:NT - 1, 0, :]).then_inc(out, 16)
                    sp.dma_start(scr[:, whole:T], fac_t[NT - 1:NT, 0, P - (T - whole):P]).then_inc(out, 16)
                sp.wait_ge(out, 32)


RL = 648
RZ = 4


def bias_rows(nc, name, fwd_in, rev_in, scale, row_scr, fwd_scr, copied, rev_hi_scr, rev_lo_scr, fills):
    with Phase(nc, name) as ph:
        fwd, rev = ph.sb("fwd", [H, RL]), ph.sb("rev", [H, RL])
        hi, lo = ph.sb("hi", [H, RL], F32R), ph.sb("lo", [H, RL], F32R)
        filler = [ph.sb(f"fill{i}", [H, T]) for i in range(len(fills))]
        loaded, cleared, filled, scaled, hi_done, lo_done, out = (
            ph.sem(n) for n in ("in", "clear", "filled", "scaled", "hi", "lo", "out"))
        with nc.Block() as block:
            @block.vector
            def _(dve):
                dve.memset(fwd[:, 0:RZ], 0.0)
                dve.memset(fwd[:, RZ + SEQ:RL], NEG)
                dve.memset(rev[:, 0:RL - RZ - SEQ], NEG)
                dve.memset(rev[:, RL - RZ:RL], 0.0).then_inc(cleared, 1)
                dve.wait_ge(loaded, 32)
                a = RL - RZ - SEQ
                dve.tensor_scalar(fwd[:, RZ:RZ + SEQ], fwd[:, RZ:RZ + SEQ], 1.0 / scale, None, ALU.mult)
                dve.tensor_scalar(rev[:, a:a + SEQ], rev[:, a:a + SEQ], 1.0 / scale, None, ALU.mult).then_inc(scaled, 1)
                dve.wait_ge(scaled, 1)
                dve.tensor_copy(hi[:, :], rev[:, :]).then_inc(hi_done, 1)
                dve.wait_ge(hi_done, 1)
                dve.tensor_tensor(lo[:, :], rev[:, :], hi[:, :].bitcast(F32), ALU.subtract).then_inc(lo_done, 1)

            @block.gpsimd
            def _(pool):
                for tile, (_, value) in zip(filler, fills):
                    pool.memset(tile[:, :], value).then_inc(filled, 1)
                    pool.wait_ge(filled, 1)

            @block.sync
            def _(sp):
                sp.dma_start(fwd[:, RZ:RZ + SEQ], fwd_in[:, 0:SEQ]).then_inc(loaded, 16)
                sp.dma_start(rev[:, RL - RZ - SEQ:RL - RZ], rev_in[:, 2 * SX - 1 - SEQ:2 * SX - 1]).then_inc(loaded, 16)
                sp.wait_ge(lo_done, 1)
                sp.dma_start(row_scr, fwd[:, :]).then_inc(out, 16)
                sp.dma_start(rev_hi_scr, hi[:, :].bitcast(F32)).then_inc(out, 16)
                sp.dma_start(rev_lo_scr, lo[:, :].bitcast(F32)).then_inc(out, 16)
                for n, (tile, (scr, _)) in enumerate(zip(filler, fills)):
                    sp.wait_ge(filled, n + 1)
                    sp.dma_start(scr[:, 2 * HD, :], tile[:, :]).then_inc(out, 16)
                sp.wait_ge(out, 16 * (3 + len(fills)))
                sp.dma_start(fwd_scr.rearrange("p h n -> p (h n)"),
                             bass.AP(tensor=row_scr.tensor, offset=row_scr.offset, ap=[[0, P], [1, H * RL]]))\
                  .then_inc(copied, 16)


def vit_tower(nc, A):
    def scratch(name, shape):
        return nc.dram_tensor(name, shape, F32).ap()

    q_scr, k_scr = scratch("q_scr", [H, 2 * HD + 1, T]), scratch("k_scr", [H, 2 * HD + 1, T])
    v_scr, o_scr = scratch("v_scr", [T, H * 32]), scratch("o_scr", [H * 32, T])
    m_scr = [scratch(f"m_scr{i}", [P, 32]) for i in range(2)]
    xn_scr = scratch("xn_scr", [P, KT, T])
    row_scr, rev_hi_scr, rev_lo_scr = (scratch(n, [H, RL]) for n in ("row_scr", "rev_hi_scr", "rev_lo_scr"))
    fwd_scr = scratch("fwd_scr", [P, H, RL])
    fac0_scr, fac1_scr = scratch("fac0_scr", [8, T]), scratch("fac1_scr", [1, T])

    def rows(ap):
        return ap.rearrange("(k p) n -> p k n", p=P)

    Phase.used.clear()
    with Phase(nc, "all") as top:
        hT = top.sb("hT", [P, KT, T])
        one_c = top.sb("mean", [P, P])
        one64 = top.sb("mean64", [P, P])
        identf = top.sb("identf", [P, P])
        ones = top.sb("ones", [P, P])
        eps = top.sb("eps", [P, 1])
        got, copied = top.sem("got"), top.sem("copied")

        def init_loads(sp):
            sp.dma_start(identf[:, :], A["c_ident"]).then_inc(got, 16)
            for b in range(B):
                sp.dma_start(hT[:, :, b * SP:b * SP + 1], A["cls"].unsqueeze(2), allow_slow_non_contiguous=True)\
                  .then_inc(got, 16)
            sp.wait_ge(got, 16 * (B + 1))

        def init_memsets(dve):
            for b in range(B):
                dve.memset(hT[:, :, b * SP + SEQ:(b + 1) * SP], 0.0)
            dve.memset(one_c[:, :], 1.0 / D)
            dve.memset(ones[:, :], 1.0)
            dve.memset(one64[0:64, :], 1.0 / 64)
            dve.memset(one64[64:P, :], 0.0)
            dve.memset(eps[:, :], EPS)

        with Phase(nc, "tok") as ph:
            raw = ph.sb("raw", [P, KT, B * SX])
            hi, lo = ph.sb("hi", [P, KT, B * SX], F32R), ph.sb("lo", [P, KT, B * SX], F32R)
            x = A["x0"].rearrange("(k p) n -> p k n", p=P)
            weights = FfnWeights(ph, 4, False, True, 1)

            r1, (h1, l1), r2, (h2, l2) = weights.raw1, weights.w1[0], weights.raw2, weights.w2[0]
            part = [slice(b * SX, (b + 1) * SX) for b in range(B)]
            split_loads(nc, "toks", [(r1[:, :, 0:512], rows(A["w0"]), h1[:, :, 0:512], l1[:, :, 0:512]),
                                     (raw[:, :, part[0]], x[:, :, part[0]], hi[:, :, part[0]], lo[:, :, part[0]]),
                                     (r1[:, :, 512:1024], rows(A["w1"]), h1[:, :, 512:1024], l1[:, :, 512:1024]),
                                     (r2[:, :, :], rows(A["wo"]), h2[:, :, :], l2[:, :, :])]
                        + [(raw[:, :, t], x[:, :, t], hi[:, :, t], lo[:, :, t]) for t in part[1:]],
                        (init_loads, init_memsets))
            gated_ffn(nc, "tokf", weights=weights, x_hi=hi, x_lo=lo, chunks=[(b * SX, SX) for b in range(B)], J=4,
                      half=False, gated=True, func=ACT.Relu, experts=1, w_mult=None, lag=2, load=None,
                      finish=lambda c: hT[:, :, c * SP + 1:c * SP + 1 + SX], store=True)

        bias_rows(nc, "rows", A["rpb_fwd"], A["rpb_rev"], 1.0 / 16, row_scr, fwd_scr, copied, rev_hi_scr, rev_lo_scr,
                  ((q_scr, 0.0), (k_scr, 1.0)))

        with Phase(nc, "L0") as l0:
            t_hi, t_lo, t_max = ([l0.sb(f"t{n}{i}", [P, HG, SP], dt) for i in range(2)]
                                 for n, dt in (("hi", F32R), ("lo", F32R), ("mx", F32)))
            tail_hi, tail_lo = ([l0.sb(f"tail{n}{i}", [P, HG, 4], F32R) for i in range(2)] for n in "hl")
            t_sem, tails_clear = [l0.sem(f"t{i}") for i in range(2)], l0.sem("tails")

            def load_bias(sp, hg):
                i = hg % 2

                def window(scr, first, n, step=1, n_rows=P):
                    return bass.AP(tensor=scr.tensor, offset=scr.offset + hg * HG * RL + first,
                                   ap=[[step, n_rows], [RL, HG], [1, n]])

                own = RL - 1 - RZ - SX - (P - 1)
                for dst, src in ((t_hi[i][:, :, :].bitcast(F32), window(rev_hi_scr, own, SP)),
                                 (t_lo[i][:, :, :].bitcast(F32), window(rev_lo_scr, own, SP)),
                                 (t_max[i][:, :, :], window(fwd_scr, RZ + P - 1, SP, H * RL - 1)),
                                 (tail_hi[i][0:4, :, :].bitcast(F32), window(rev_hi_scr, own + P - 4, 4, n_rows=4)),
                                 (tail_lo[i][0:4, :, :].bitcast(F32), window(rev_lo_scr, own + P - 4, 4, n_rows=4))):
                    sp.dma_start(dst, src).then_inc(t_sem[i], 16)

            with Phase(nc, "L0p") as ph:
                xn = ph.sb("xn", [P, KT, T])
                hi, lo = ph.sb("hi", [P, KT, T], F32R), ph.sb("lo", [P, KT, T], F32R)
                wr = ph.sb("wraw", [P, KT, 3 * D])
                wh, wl = ph.sb("wh", [P, KT, 3 * D], F32R), ph.sb("wl", [P, KT, 3 * D], F32R)
                bias = ph.sb("bias", [P, 4])
                with nc.Block() as block:
                    @block.vector
                    def _(dve):
                        for i in range(2):
                            dve.memset(tail_hi[i][:, :, :].bitcast(F32), NEG)
                            ins = dve.memset(tail_lo[i][:, :, :].bitcast(F32), 0.0)
                        ins.then_inc(tails_clear, 1)

                layer_norm(nc, "L0n", hT, (one_c[:, :], ones[:, :], identf[:, :], eps[:, 0:1]), xn=xn, hi=hi, lo=lo, spill=xn_scr,
                           beside=preload(ph, "w", [(wr[:, :, :], rows(A["wqkv"]), wh[:, :, :], wl[:, :, :]),
                                                    (bias[:, :], A["bqk"], None, None)]))

                def part(t, m, n=P):
                    return lambda k: t[:, k, m:m + n]

                def before(sp):
                    sp.wait_ge(copied, 16)
                    sp.wait_ge(tails_clear, 1)
                    load_bias(sp, 0)

                w = [(KT, part(wh, m * P), part(wl, m * P), hi, lo) for m in range(4)]
                project(nc, "L0q", x_hi=hi, x_lo=lo, kv_hi=hi, kv_lo=lo, w=w, w_swap=None, rope=None, bias=bias,
                        w_v=(KT, part(wh, 2 * D, D), part(wl, 2 * D, D), hi, lo), q_scr=q_scr, k_scr=k_scr, v_scr=v_scr,
                        before=before)

            with Phase(nc, "L0a") as ph:
                consts = attention_consts(nc, ph, A, identf, toeplitz=True)
                attention(nc, "L0t", q_scr=q_scr, k_scr=k_scr, v_scr=v_scr, o_scr=o_scr, m_scr=m_scr, scale=1.0 / 16,
                          toeplitz={"hi": t_hi, "lo": t_lo, "max": t_max, "tail_hi": tail_hi, "tail_lo": tail_lo,
                                    "loaded": t_sem, "n": 5, "load": load_bias}, consts=consts)

        with Phase(nc, "L0o") as ph:
            xn = ph.sb("xn", [P, KT, T])
            wr = ph.sb("wraw", [P, KT, D])
            w = [ph.sb(f"w{q}", [P, KT, D], F32R) for q in "hl"]
            vec = ph.sb("vec", [P, 4, KT])
            project_out(nc, "L0oo", get_weights=preload(ph, "w", [(wr[:, :, :], rows(A["wproj"]), w[0][:, :, :], w[1][:, :, :]),
                                                                  (vec[:, :, :], A["vec0"], None, None)]),
                        o_scr=o_scr, w=w, hT=hT, spread=A["c_spread"], xn=xn, xn_scr=xn_scr,
                        bias=vec[:, 0, :], v_bias=vec[:, 3, :])
            layer_norm(nc, "L0on", xn, (one_c[:, :], ones[:, :], identf[:, :], eps[:, 0:1]), xn=xn, gain=vec[:, 1, :], shift=vec[:, 2, :], add_to=hT)

        with Phase(nc, "E") as ph:
            hi, lo = ph.sb("hi", [P, KT, T], F32R), ph.sb("lo", [P, KT, T], F32R)
            weights = FfnWeights(ph, 6, True, True, NEXP0 + 1)

            def load_expert(e, r1, r2):
                return [(r1[:, :, :], rows(A["gu"][e])), (r2[:, 0:5, :], rows(A["down"][e, 0:640, :])),
                        (r2[0:64, 5, :], A["down"][e, 640:HID0, :])]

            with Phase(nc, "E1") as p2:
                xn = p2.sb("xn", [P, KT, T])
                wr = p2.sb("wr", [P, KT, NEXP0])
                gain = p2.sb("gain", [P, NEXP0])
                layer_norm(nc, "E1n", hT, (one_c[:, :], ones[:, :], identf[:, :], eps[:, 0:1]), xn=xn, hi=hi, lo=lo,
                           beside=weights.first(ph, load_expert, half=True, more=[
                               (wr[:, :, :], rows(A["wr0"]), None, None),
                               (gain[:, :], A["rb"].to_broadcast([P, NEXP0]), None, None)]))
                router(nc, "E1r", xn=xn, w=wr, ne=NEXP0, identity=identf[:, :], scr=fac0_scr, gain=gain[:, :])

            gated_ffn(nc, "Ef", weights=weights, x_hi=hi, x_lo=lo, chunks=[(c * CH, CH) for c in range(NCH)], J=6, half=True, gated=True,
                      func=ACT.Silu, experts=NEXP0 + 1, w_mult=lambda e: fac0_scr[e:e + 1, :].to_broadcast([P, T]), lag=3,
                      load=load_expert, finish=lambda c: hT[:, :, c * CH:(c + 1) * CH])

        clear_semaphores(nc)

        with Phase(nc, "L1p") as ph:
            xn = ph.sb("xn", [P, KT, T])
            hi, lo = ph.sb("hi", [P, KT, T], F32R), ph.sb("lo", [P, KT, T], F32R)
            lat, lat_hi, lat_lo = (ph.sb(f"lat{i}", [P, 1, T], dt) for i, dt in enumerate((F32, F32R, F32R)))
            wqr, wq = ph.sb("wqr", [P, KT, 2 * D]), [ph.sb(f"wq{q}", [P, KT, 2 * D], F32R) for q in "hl"]
            wlr, wl = ph.sb("wlr", [P, KT, P]), [ph.sb(f"wl{q}", [P, KT, P], F32R) for q in "hl"]
            wkr, wk = ph.sb("wkr", [P, 1, 3 * D]), [ph.sb(f"wk{q}", [P, 1, 3 * D], F32R) for q in "hl"]
            vec = ph.sb("vec", [P, 2])
            cos, sin = ph.sb("cos", [P, SP]), ph.sb("sin", [P, SP])
            with nc.Block() as block:
                @block.vector
                def _(dve):
                    dve.memset(wlr[:, :, 64:P], 0.0)
                    dve.memset(wkr[64:P, :, :], 0.0)
                    dve.memset(vec[:, :], 0.0)
            layer_norm(nc, "L1n", hT, (one_c[:, :], ones[:, :], identf[:, :], eps[:, 0:1]), xn=xn, hi=hi, lo=lo, beside=preload(ph, "w", [
                (wlr[:, :, 0:64], rows(A["wdkv"]), None, None), (wlr[:, :, :], None, wl[0][:, :, :], wl[1][:, :, :]),
                (wkr[0:64, 0, :], A["wkv1"], None, None), (wkr[:, :, :], None, wk[0][:, :, :], wk[1][:, :, :]),
                (wqr[:, :, :], rows(A["wq1"]), wq[0][:, :, :], wq[1][:, :, :]),
                (vec[0:64, :], A["vec1"], None, None),
                (cos[:, :], A["c_cos"], None, None), (sin[:, :], A["c_sin"], None, None)]))
            latent(nc, "L1l", hi, lo, wl, lat)
            layer_norm(nc, "L1ln", lat, (one64[:, :], ones[:, :], identf[:, :], eps[:, 0:1]), xn=lat, hi=lat_hi, lo=lat_lo, gain=vec[:, 0:1],
                       shift=vec[:, 1:2], width=1)

            def part(t, m, n=P):
                return lambda k: t[:, k, m:m + n]

            def four(q0, k0):
                return ([(KT, part(wq[0], q0 + m * P), part(wq[1], q0 + m * P), hi, lo) for m in range(2)]
                        + [(1, part(wk[0], k0 + m * P), part(wk[1], k0 + m * P), lat_hi, lat_lo) for m in range(2)])

            project(nc, "L1q", x_hi=hi, x_lo=lo, kv_hi=lat_hi, kv_lo=lat_lo, w=four(0, 0), w_swap=four(D, D),
                    rope=(cos, sin), bias=None, w_v=(1, part(wk[0], 2 * D, D), part(wk[1], 2 * D, D), lat_hi, lat_lo),
                    q_scr=q_scr, k_scr=k_scr, v_scr=v_scr)

        with Phase(nc, "L1a") as ph:
            consts = attention_consts(nc, ph, A, identf, toeplitz=False)
            attention(nc, "L1t", q_scr=q_scr, k_scr=k_scr, v_scr=v_scr, o_scr=o_scr, m_scr=m_scr, scale=1.0 / 4,
                      toeplitz=None, consts=consts)

        with Phase(nc, "L1o") as ph:
            wr = ph.sb("wraw", [P, KT, D])
            w = [ph.sb(f"w{q}", [P, KT, D], F32R) for q in "hl"]
            project_out(nc, "L1oo", get_weights=preload(ph, "w", [(wr[:, :, :], rows(A["wo1"]), w[0][:, :, :], w[1][:, :, :])]),
                        o_scr=o_scr, w=w, hT=hT, spread=A["c_spread"])

        with Phase(nc, "F") as ph:
            hi, lo = ph.sb("hi", [P, KT, T], F32R), ph.sb("lo", [P, KT, T], F32R)
            b1, b2 = ph.sb("b1", [P, FF1 // P]), ph.sb("b2", [P, KT])
            weights = FfnWeights(ph, FF1 // P, False, False, 1)

            def load_ffn(e, r1, r2):
                return [(r1[:, :, :], rows(A["ff1"])), (r2[:, :, :], rows(A["ff2"]))]

            with Phase(nc, "F1") as p2:
                xn = p2.sb("xn", [P, KT, T])
                wr = p2.sb("wr", [P, KT, NEXP1])
                layer_norm(nc, "F1n", hT, (one_c[:, :], ones[:, :], identf[:, :], eps[:, 0:1]), xn=xn, hi=hi, lo=lo,
                           beside=weights.first(ph, load_ffn, more=[
                               (wr[:, :, :], rows(A["wr1"]), None, None), (b1[:, :], A["b1"], None, None),
                               (b2[:, :], A["b2"], None, None)]))
                router(nc, "F1r", xn=xn, w=wr, ne=NEXP1, identity=identf[:, :], scr=fac1_scr)
            gated_ffn(nc, "Ff", weights=weights, x_hi=hi, x_lo=lo, chunks=[(c * CH, CH) for c in range(NCH)], J=FF1 // P, half=False,
                      gated=False, func=ACT.Gelu_apprx_tanh, experts=1,
                      w_mult=lambda e: fac1_scr.to_broadcast([P, T]), lag=3, load=None,
                      finish=lambda c: hT[:, :, c * CH:(c + 1) * CH], up_bias=b1, out_bias=b2,
                      output=lambda c: A["out"].rearrange("(k p) t -> p k t", p=P)[:, :, c * CH:(c + 1) * CH])


def attention_consts(nc, ph, A, identf, toeplitz):
    ident, turn, tail = ph.sb("ident", [P, P], F32R), ph.sb("turn", [P, P], F32R), ph.sb("tail", [P, 4], F32R)
    raw = ph.sb("craw", [P, 2 * P + 4])
    mask2 = None if toeplitz else ph.sb("mask2", [P, SP])
    got = ph.sem("cgot")
    loads = [(raw[:, :], A["c_masks"])]
    if mask2 is not None:
        loads.append((mask2[:, :], A["c_mask2"]))
    with nc.Block() as block:
        @block.sync
        def _(sp):
            for dst, src in loads:
                sp.dma_start(dst, src).then_inc(got, 16)

        @block.vector
        def _(dve):
            dve.wait_ge(got, 16 * len(loads))
            dve.tensor_copy(ident[:, :], identf[:, :])
            dve.tensor_copy(turn[:, :], raw[:, P:2 * P] if toeplitz else raw[:, 0:P])
            dve.tensor_copy(tail[:, :], raw[:, 2 * P:])
    return {"ident": ident[:, :], "flip": turn[:, :] if toeplitz else None, "diag": None if toeplitz else turn[:, :],
            "tail": tail[:, :],
            "mask2": None if mask2 is None else mask2[:, :]}


def constants():
    import numpy as np
    p = np.arange(P)
    half = HD // 2
    inv = (1.0 / 10000.0 ** (np.arange(half, dtype=np.float32) / np.float32(half))).astype(np.float32)
    ang = np.arange(SP, dtype=np.float32)[None, :] * inv[:, None]
    row = p % HD
    sign = np.where(row < half, -1.0, 1.0)[:, None]
    diag = np.where(p[:, None] > p[None, :], NEG, 0.0)
    j = np.arange(4)[None, :]
    tail = np.where((p[:, None] < P - 4) | (p[:, None] - (P - 4) > j), NEG, 0.0)
    return {
        "c_ident": np.eye(P, dtype=np.float32),
        "c_cos": np.cos(ang.astype(np.float64))[row % half].astype(np.float32),
        "c_sin": (np.sin(ang.astype(np.float64))[row % half] * sign).astype(np.float32),
        "c_masks": np.concatenate([diag, np.eye(P)[::-1], tail], 1).astype(np.float32),
        "c_mask2": np.where(np.arange(SP)[None, :] > 385 + p[:, None], NEG, 0.0).astype(np.float32),
        "c_spread": (np.arange(H * B)[:, None, None] == (np.arange(D)[None, None] // HD * B
                                                          + np.arange(B)[None, :, None])).astype(np.float32),
    }


def kernel(**inputs):
    import numpy as np
    import concourse.bacc as bacc
    from concourse.bass_utils import run_bass_kernel_spmd as run

    a = {k: np.asarray(v) for k, v in inputs.items()}
    n0, nh = HID0 // P * P, H

    def gate_up(g, u):
        return np.concatenate([g[..., :n0], u[..., :n0], g[..., n0:], u[..., n0:]], -1)

    def swapped(w):
        return w.reshape(-1, nh, 2, HD // 2)[:, :, ::-1].reshape(-1, D)

    qkv, wb = a["L0_attn_W_w"], a["L0_attn_W_b"]
    wq, wuk = a["L1_attn_W_q"], a["L1_attn_W_uk"]
    arrays = {
        "x0": a["x"][..., 0].transpose(2, 0, 1).reshape(D, B * SX),
        "cls": a["cls_tok"].reshape(KT, P).T,
        "w0": a["L0_tok_W0"].T, "w1": a["L0_tok_W1"].T, "wo": a["L0_tok_Wo"].T,
        "wqkv": qkv.T, "bqk": wb[:2 * D].reshape(4, P).T,
        "rpb_fwd": a["L0_attn_rpb"].T, "rpb_rev": a["L0_attn_rpb"][::-1].T,
        "wproj": a["L0_attn_proj_w"].T,
        "vec0": np.stack([v.reshape(KT, P).T for v in (a["L0_attn_proj_b"], a["L0_attn_ln_g"], a["L0_attn_ln_b"],
                                                       wb[2 * D:])], 1),
        "wr0": a["L0_ffn_Wr"], "rb": a["L0_ffn_routing_bias"][None],
        "gu": np.concatenate([gate_up(a["L0_ffn_routed_gate"], a["L0_ffn_routed_up"]),
                              gate_up(a["L0_ffn_shared_gate"], a["L0_ffn_shared_up"])[None]]),
        "down": np.concatenate([a["L0_ffn_routed_down"], a["L0_ffn_shared_down"][None]]),
        "wq1": np.concatenate([wq, swapped(wq)], 1), "wdkv": a["L1_attn_W_dkv"],
        "wkv1": np.concatenate([wuk, swapped(wuk), a["L1_attn_W_uv"]], 1),
        "vec1": np.stack([a["L1_attn_ln_gamma"], a["L1_attn_ln_beta"]], 1),
        "wo1": a["L1_attn_W_o"], "wr1": a["L1_ffn_router_w"], "ff1": a["L1_ffn_w1"], "ff2": a["L1_ffn_w2"],
        "b1": a["L1_ffn_b1"].reshape(FF1 // P, P).T, "b2": a["L1_ffn_b2"].reshape(KT, P).T,
        **constants(),
    }
    arrays = {f"in_{k}": np.ascontiguousarray(v) for k, v in arrays.items()}
    nc = bacc.Bacc("TRN2", target_bir_lowering=False, num_devices=1)
    aps = {k[3:]: nc.dram_tensor(k, v.shape, F32, kind="ExternalInput").ap() for k, v in arrays.items()}
    aps["out"] = nc.dram_tensor("out_dram", [D, T], F32, kind="ExternalOutput").ap()
    vit_tower(nc, aps)
    got = run(nc, [arrays], core_ids=[0]).results[0]["out_dram"]
    return np.ascontiguousarray(got.reshape(D, B, SP)[:, :, :SEQ].transpose(1, 2, 0))
```

```python
import concourse.bass as bass
from concourse import mybir
from contextlib import ExitStack

F32 = mybir.dt.float32
F32R = mybir.dt.float32r
ALU = mybir.AluOpType
ACT = mybir.ActivationFunctionType
AX = mybir.AxisListType

B = 4
SX = 512
SEQ = SX + 1
SP = 516
T = B * SP
D = 256
KT = D // 128
P = 128
CH = 344
NCH = T // CH
QC = SP // 2
NQC = T // QC
H, HD = 16, 16
HG = 4
NT = (T + P - 1) // P
NEG = -1.0e30
EPS = 1e-5
WARM = 14
HID0, NEXP0 = 704, 7
NEXP1 = 8
FF1 = 1024


def tile_start(i):
    return min(i * P, T - P)


def split_product(pe, out, w_hi, w_lo, x_hi, x_lo, start=True, stop=True):
    pe.matmul(out, w_hi, x_hi, start=start, stop=False, skip_group_check=True)
    pe.matmul(out, w_hi, x_lo, start=False, stop=False, skip_group_check=True)
    return pe.matmul(out, w_lo, x_hi, start=False, stop=stop, skip_group_check=True)


class Chain:

    def __init__(self, eng, sem):
        self.eng, self.sem, self.n = eng, sem, 0

    def __call__(self, ins):
        self.n += 1
        ins.then_inc(self.sem, 1)
        self.eng.wait_ge(self.sem, self.n)


class Phase:

    def __init__(self, nc, name):
        self.nc, self.name, self.stack = nc, name, ExitStack()

    def __enter__(self):
        self.stack.__enter__()
        return self

    def __exit__(self, *a):
        return self.stack.__exit__(*a)

    def sb(self, name, shape, dt=F32):
        return self.stack.enter_context(self.nc.sbuf_tensor(f"{self.name}_{name}", shape, dt))

    def ps(self, name, shape):
        return self.stack.enter_context(self.nc.psum_tensor(f"{self.name}_{name}", shape, F32))

    def sem(self, name):
        s = self.stack.enter_context(self.nc.semaphore(f"{self.name}_{name}"))
        self.used.append(s.num)
        return s

    used = []


def clear_semaphores(nc):
    with nc.Block() as block:
        @block.sync
        def _(sp):
            sp.sem_clear(range(min(Phase.used), max(Phase.used) + 1))


def layer_norm(nc, name, x, consts, xn=None, hi=None, lo=None, gain=None, shift=None, add_to=None, spill=None,
               width=KT, beside=None, use=None):
    mean_w, ones, identity, eps = consts
    SUB = CH // 4
    XB, SB = 4, 3
    with Phase(nc, name) as ph:
        xc = [ph.sb(f"xc{i}", [P, width, CH]) for i in range(XB)]
        sq = [ph.sb(f"sq{i}", [P, width, CH]) for i in range(SB)]
        std = [ph.sb(f"std{i}", [SUB, 4]) for i in range(2)]
        rstd = [ph.sb(f"rstd{i}", [SUB, 4]) for i in range(2)]
        diag = [ph.sb(f"diag{i}", [SUB, 4, SUB]) for i in range(2)]
        mean_ps = [ph.ps(f"mean{i}", [P, 512]) for i in range(2)]
        var_ps = [ph.ps(f"var{i}", [SUB, 512]) for i in range(2)]
        rstd_ps = [ph.ps(f"rstdps{i}", [P, 512]) for i in range(2)]
        mean_done, centred, squared, var_done, std_done, inverted, diag_done, spread_done, scaled, normed, hi_done = (
            ph.sem(n) for n in ("mean", "centred", "squared", "var", "stdd", "inv", "diag", "spread", "scaled", "normed",
                                "hid"))
        if gain is None:
            normed = scaled

        def cols(t, c):
            return t[:, :, c * CH:(c + 1) * CH]

        def spread(t):
            return t.unsqueeze(1).to_broadcast([P, width, CH])

        with nc.Block() as block:
            @block.tensor
            def _(pe):
                def mean(c):
                    if c >= 2:
                        pe.wait_ge(centred, c - 1)
                    for k in range(width):
                        mm = pe.matmul(mean_ps[c % 2][:, 0:CH], mean_w, cols(x, c)[:, k, :],
                                       start=(k == 0), stop=(k == width - 1))
                    mm.then_inc(mean_done, 1)

                def var(c):
                    pe.wait_ge(squared, c + 1)
                    if c >= 2:
                        pe.wait_ge(std_done, c - 1)
                    for j in range(4):
                        for k in range(width):
                            mm = pe.matmul(var_ps[c % 2][:, j:j + 1], sq[c % SB][:, k, j * SUB:(j + 1) * SUB],
                                           mean_w[:, 0:1], start=(k == 0), stop=(k == width - 1))
                    mm.then_inc(var_done, 1)

                def spread_inverse(c):
                    pe.wait_ge(diag_done, c + 1)
                    if c >= 2:
                        pe.wait_ge(scaled, c - 1)
                    for j in range(4):
                        mm = pe.matmul(rstd_ps[c % 2][:, j * SUB:(j + 1) * SUB], ones[0:SUB, :], diag[c % 2][:, j, :],
                                       start=True, stop=True)
                    mm.then_inc(spread_done, 1)

                mean(0)
                mean(1)
                for s in range(NCH + 2):
                    if s + 2 < NCH:
                        mean(s + 2)
                    if s < NCH:
                        var(s)
                    if 1 <= s <= NCH:
                        spread_inverse(s - 1)
                    if s >= 2 and use is not None:
                        pe.wait_ge(normed, s - 1)
                        use(pe, s - 2)

            @block.scalar
            def _(act):
                def square(c):
                    act.wait_ge(centred, c + 1)
                    if c >= SB:
                        act.wait_ge(var_done, c - SB + 1)
                    act.activation(sq[c % SB][:, :, :], xc[c % XB][:, :, :], ACT.Square).then_inc(squared, 1)

                square(0)
                square(1)
                for s in range(NCH + 1):
                    if s < NCH:
                        act.wait_ge(var_done, s + 1)
                        if s >= 2:
                            act.wait_ge(inverted, s - 1)
                        act.activation(std[s % 2][:, :], var_ps[s % 2][:, 0:4], ACT.Sqrt, bias=eps[0:SUB, :])\
                           .then_inc(std_done, 1)
                    if s + 2 < NCH:
                        square(s + 2)
                    if s >= 1:
                        c = s - 1
                        if gain is not None:
                            act.wait_ge(scaled, c + 1)
                            for k in range(width):
                                ins = act.activation(cols(xn, c)[:, k, :], xc[c % XB][:, k, :], ACT.Identity,
                                                     bias=shift[:, k:k + 1], scale=gain[:, k:k + 1])
                            ins.then_inc(normed, 1)
                        if hi is not None:
                            act.wait_ge(normed, c + 1)
                            act.activation(cols(hi, c), cols(xn, c), ACT.Copy).then_inc(hi_done, 1)

            @block.vector
            def _(dve):
                def centre(c):
                    dve.wait_ge(mean_done, c + 1)
                    if c >= XB:
                        dve.wait_ge(squared, c - XB + 1)
                        dve.wait_ge(normed, c - XB + 1)
                    dve.tensor_tensor(xc[c % XB][:, :, :], cols(x, c), spread(mean_ps[c % 2][:, 0:CH]),
                                      ALU.subtract).then_inc(centred, 1)

                centre(0)
                centre(1)
                for s in range(NCH + 2):
                    if s < NCH:
                        dve.wait_ge(std_done, s + 1)
                        if s >= 2:
                            dve.wait_ge(diag_done, s - 1)
                        dve.reciprocal(rstd[s % 2][:, :], std[s % 2][:, :]).then_inc(inverted, 1)
                    if s + 2 < NCH:
                        centre(s + 2)
                    if s < NCH:
                        dve.wait_ge(inverted, s + 1)
                        if s >= 2:
                            dve.wait_ge(spread_done, s - 1)
                        dve.tensor_tensor(diag[s % 2][:, :, :],
                                          identity[0:SUB, 0:SUB].unsqueeze(1).to_broadcast([SUB, 4, SUB]),
                                          rstd[s % 2][:, :].unsqueeze(2).to_broadcast([SUB, 4, SUB]), ALU.mult)\
                           .then_inc(diag_done, 1)
                    if 1 <= s <= NCH:
                        c = s - 1
                        dve.wait_ge(spread_done, c + 1)
                        dve.wait_ge(centred, c + 1)
                        dst = cols(xn, c) if gain is None else xc[c % XB][:, :, :]
                        dve.tensor_tensor(dst, xc[c % XB][:, :, :], spread(rstd_ps[c % 2][:, 0:CH]), ALU.mult)\
                           .then_inc(scaled, 1)
                    if s >= 2:
                        c = s - 2
                        dve.wait_ge(normed, c + 1)
                        if add_to is not None:
                            dve.tensor_tensor(cols(add_to, c), cols(add_to, c), cols(xn, c), ALU.add)
                        if hi is not None:
                            dve.wait_ge(hi_done, c + 1)
                            dve.tensor_tensor(cols(lo, c), cols(xn, c), cols(hi, c).bitcast(F32), ALU.subtract)

            if beside is not None:
                @block.gpsimd
                def _(pool):
                    beside[1](pool)

            if spill is not None or beside is not None:
                @block.sync
                def _(sp):
                    if beside is not None:
                        beside[0](sp)
                    if spill is not None:
                        for c in range(NCH):
                            sp.wait_ge(normed, c + 1)
                            sp.dma_start(spill[0][:, :, c * CH:(c + 1) * CH], cols(xn, c)).then_inc(spill[1], 16)


def preload(ph, name, loads, clear=()):
    got, own = ph.sem(name + "got"), ph.sem(name + "own")

    moved = [(raw, src) for raw, src, _, _ in loads if src is not None]

    def start(sp):
        for raw, src in moved:
            sp.dma_start(raw, src).then_inc(got, 16)

    def program(pool):
        step = Chain(pool, own)
        for raw in clear:
            step(pool.memset(raw, 0.0))
        pool.wait_ge(got, 16 * len(moved))
        last = None
        for raw, _, hi, lo in loads:
            if hi is not None:
                step(pool.tensor_copy(hi, raw))
                last = pool.tensor_tensor(lo, raw, hi.bitcast(F32), ALU.subtract)
        return last

    def wait(eng):
        eng.wait_ge(got, 16 * len(moved))

    return start, program, wait


def split_loads(nc, name, loads, init):
    with Phase(nc, name) as ph:
        got = [ph.sem(f"got{i}") for i in range(len(loads))]
        hi_done = ph.sem("hid")
        with nc.Block() as block:
            @block.sync
            def _(sp):
                for s, (raw, src, _, _) in zip(got, loads):
                    sp.dma_start(raw, src).then_inc(s, 16)
                init[0](sp)

            @block.scalar
            def _(act):
                for s, (raw, _, hi, _) in zip(got, loads):
                    act.wait_ge(s, 16)
                    act.activation(hi, raw, ACT.Copy).then_inc(hi_done, 1)

            @block.vector
            def _(dve):
                for n, (raw, _, hi, lo) in enumerate(loads):
                    dve.wait_ge(hi_done, n + 1)
                    dve.tensor_tensor(lo, raw, hi.bitcast(F32), ALU.subtract)
                init[1](dve)


class FfnWeights:

    def __init__(self, ph, J, half, gated, experts):
        GU = 2 * J if gated else J
        if half:
            GU -= 1
        self.GU, self.J = GU, J
        self.passes = 2 if experts > 1 else 1
        self.raw1, self.raw2 = ph.sb("raw1", [P, KT, GU * P]), ph.sb("raw2", [P, J, D])
        self.w1 = [[ph.sb(f"w1{p}{q}", [P, KT, GU * P], F32R) for q in "hl"] for p in range(self.passes)]
        self.w2 = [[ph.sb(f"w2{p}{q}", [P, J, D], F32R) for q in "hl"] for p in range(self.passes)]

    def first(self, ph, load, half=False, more=()):
        clear = [self.raw2[64:P, self.J - 1, :]] if half else []
        start, get, wait = preload(ph, "ffn", [(dst, src, None, None) for dst, src in load(0, self.raw1, self.raw2)]
                      + list(more), clear)
        def split(pool, name, raw, parts):
            step = Chain(pool, ph.sem("ffn" + name))
            step(pool.tensor_copy(parts[0][:, :, :], raw[:, :, :]))
            pool.tensor_tensor(parts[1][:, :, :], raw[:, :, :], parts[0][:, :, :].bitcast(F32), ALU.subtract)

        def program(pool):
            get(pool)
            split(pool, "first", self.raw1, self.w1[0])

        def rest(pool):
            split(pool, "second", self.raw2, self.w2[0])

        return start, program, rest, wait


def gated_ffn(nc, name, *, weights, x_hi, x_lo, chunks, J, half, gated, func, experts, load, w_mult, finish,
              lag, up_bias=None, out_bias=None, add=True, output=None):
    NC = len(chunks)
    N = chunks[0][1]
    GU, PASSES = weights.GU, weights.passes
    FULL = J - 1 if half else J
    S = PASSES * NC * J
    with Phase(nc, name) as ph:
        raw1, raw2, w1, w2 = weights.raw1, weights.raw2, weights.w1, weights.w2
        hid_hi = ph.sb("hidhi", [P, J, N], F32R)
        hid_lo = ph.sb("hidlo", [P, J, N], F32R)
        gate_sb = [ph.sb(f"gate{i}", [P, N]) for i in range(2)]
        up_half = ph.sb("uphalf", [64, N]) if half else None
        hidden = [ph.sb(f"hidden{i}", [P, N]) for i in range(2)]
        out_sb = [ph.sb(f"out{i}", [P, KT, N]) for i in range(2)]
        factor = [ph.sb(f"factor{p}", [P, T]) for p in range(PASSES)] if w_mult is not None else None
        gu_ps = [ph.ps(f"gu{i}", [P, 2 if gated else 1, 512]) for i in range(3)]
        OB = 1 if gated else 2
        out_ps = [ph.ps(f"outps{i}", [P, KT, 512]) for i in range(OB)]
        raw_in, split_done, own = (ph.sem(n) for n in ("raw", "split", "own"))
        gu_done, gate_done, hid_made, hi_done, lo_done, down_done, out_done, evacuated, added, up_done = (
            ph.sem(n) for n in ("gu", "gated", "hid", "hi", "lo", "down", "outd", "evac", "added", "updone"))
        factor_in = [ph.sem(f"factor{p}") for p in range(PASSES)] if factor else None
        stored = ph.sem("stored")
        start = ph.sb("start", [P, 1])
        CREDIT = 1 if experts > 1 else 0

        def turns(eng, body):
            if experts > 1:
                with eng.Fori(0, experts // PASSES) as it:
                    body(it)
            else:
                body(0)

        def where(s):
            return s // (NC * J), s // J % NC, s % J

        def is_half(s):
            return half and s % J == J - 1

        with nc.Block() as block:
            @block.sync
            def _(sp):
                for e in range(experts):
                    if e >= 1:
                        if e >= 2:
                            sp.wait_ge(split_done, e)
                        for dst, src in load(e, raw1, raw2):
                            sp.dma_start(dst, src).then_inc(raw_in, 16)
                    if factor:
                        if e >= PASSES:
                            sp.wait_ge(evacuated, (e - PASSES + 1) * NC + CREDIT)
                        sp.dma_start(factor[e % PASSES][:, :], w_mult(e)).then_inc(factor_in[e % PASSES], 16)
                if output is not None:
                    for c in range(NC):
                        sp.wait_ge(added, c + 1)
                        sp.dma_start(output(c), finish(c)).then_inc(stored, 16)
                    sp.wait_ge(stored, 16 * NC)

            @block.gpsimd
            def _(pool):
                step = Chain(pool, own)
                if half:
                    pool.memset(hid_hi[64:P, J - 1, :].bitcast(F32), 0.0).then_inc(added, CREDIT)
                    pool.wait_ge(added, CREDIT)
                    pool.memset(hid_lo[64:P, J - 1, :].bitcast(F32), 0.0).then_inc(split_done, 1)
                    pool.wait_ge(split_done, 1)

                n_raw = len(load(0, raw1, raw2)) if experts > 1 else 0

                def pieces(e):
                    p = e % PASSES
                    W = GU * P // 4
                    out = [(raw1[:, :, i * W:(i + 1) * W], w1[p][0][:, :, i * W:(i + 1) * W],
                            w1[p][1][:, :, i * W:(i + 1) * W]) for i in range(4)]
                    J2 = J // 2
                    out += [(raw2[:, a:b, :], w2[p][0][:, a:b, :], w2[p][1][:, a:b, :])
                            for a, b in ((0, J2), (J2, J))]
                    return out

                def split(e, i):
                    if i == 0:
                        pool.wait_ge(raw_in, 16 * n_raw * e)
                        if e >= PASSES:
                            pool.wait_ge(out_done, (e - PASSES + 1) * NC)
                    raw, hi, lo = pieces(e)[i]
                    step(pool.tensor_copy(hi, raw))
                    last = pool.tensor_tensor(lo, raw, hi.bitcast(F32), ALU.subtract)
                    if i == 5:
                        last.then_inc(split_done, 1)

                for e in range(experts):
                    for c in range(NC):
                        if e + 1 < experts:
                            split(e + 1, c)
                        pool.wait_ge(evacuated, e * NC + c + 1 + CREDIT)
                        dst = finish(c)
                        if add:
                            ins = pool.tensor_tensor(dst, dst, out_sb[c % 2][:, :, :], ALU.add)
                        else:
                            ins = pool.tensor_copy(dst, out_sb[c % 2][:, :, :])
                        ins.then_inc(added, 1)

            @block.tensor
            def _(pe):
                def first(it, s):
                    p, c, j = where(s)
                    if experts > 1 and c == 0 and j == 0:
                        pe.wait_ge(split_done, it * PASSES + p + 1)
                    if s >= 3:
                        pe.wait_ge(hid_made, it * S + s - 2)
                    a, n = chunks[c]
                    tiles = [(0, j)]
                    if gated and not is_half(s):
                        tiles.append((1, FULL + j))
                    if is_half(s):
                        tiles = [(0, 2 * FULL)]
                    for g, m in tiles:
                        for k in range(KT):
                            w = [w1[p][q][:, k, m * P:(m + 1) * P] for q in range(2)]
                            mm = split_product(pe, gu_ps[s % 3][:, g, 0:N], w[0], w[1], x_hi[:, k, a:a + n],
                                               x_lo[:, k, a:a + n], k == 0, k == KT - 1)
                    mm.then_inc(gu_done, 1)

                def down(it, s):
                    p, c, j = where(s)
                    pe.wait_ge(lo_done, it * S + s + 1)
                    n = s // J
                    if j == 0 and (experts > 1 or n >= OB):
                        pe.wait_ge(evacuated, it * PASSES * NC + n + 1 - OB + CREDIT)
                    for m in range(KT):
                        w = [w2[p][q][:, j, m * P:(m + 1) * P] for q in range(2)]
                        mm = split_product(pe, out_ps[n % OB][:, m, 0:N], w[0], w[1], hid_hi[:, j, :],
                                           hid_lo[:, j, :], j == 0, j == J - 1)
                    if j == J - 1:
                        mm.then_inc(out_done, 1)
                    else:
                        mm.then_inc(down_done, 1)

                def body(it):
                    for s in range(S + lag):
                        if s < S:
                            first(it, s)
                        if s >= lag:
                            down(it, s - lag)

                turns(pe, body)

            def slot_free(eng, it, s):
                if s >= J:
                    q = s - J
                    if q % J == J - 1:
                        eng.wait_ge(out_done, it * (S // J) + q // J + 1)
                    else:
                        eng.wait_ge(down_done, it * (S // J) * (J - 1) + q // J * (J - 1) + q % J + 1)

            @block.scalar
            def _(act):
                def body(it):
                    for s in range(S + 1):
                        if s < S:
                            act.wait_ge(gu_done, it * S + s + 1)
                            r = 64 if is_half(s) else P
                            src = gu_ps[s % 3][0:r, 0, 0:N]
                            if gated:
                                if s >= 2:
                                    act.wait_ge(hid_made, it * S + s - 1)
                                ins = act.activation(gate_sb[s % 2][0:r, :], src, func)
                                ins.then_inc(gate_done, 1)
                                if is_half(s):
                                    act.activation(up_half[:, :], gu_ps[s % 3][64:P, 0, 0:N], ACT.Copy)\
                                       .then_inc(up_done, 1)
                            else:
                                if s >= 2:
                                    act.wait_ge(lo_done, it * S + s - 1)
                                act.activation(hidden[s % 2][:, :], src, func, bias=up_bias[:, s % J:s % J + 1])\
                                   .then_inc(hid_made, 1)
                        if gated and s >= 1:
                            q = s - 1
                            r = 64 if is_half(q) else P
                            act.wait_ge(hid_made, it * S + q + 1)
                            slot_free(act, it, q)
                            act.activation(hid_hi[0:r, q % J, :], hidden[q % 2][0:r, :], ACT.Copy)\
                               .then_inc(hi_done, 1)
                turns(act, body)

            @block.vector
            def _(dve):
                def low(it, q):
                    r = 64 if is_half(q) else P
                    if not gated:
                        dve.wait_ge(hid_made, it * S + q + 1)
                        slot_free(dve, it, q)
                        dve.tensor_copy(hid_hi[:, q % J, :], hidden[q % 2][:, :]).then_inc(hi_done, 1)
                    dve.wait_ge(hi_done, it * S + q + 1)
                    dve.tensor_tensor(hid_lo[0:r, q % J, :], hidden[q % 2][0:r, :],
                                      hid_hi[0:r, q % J, :].bitcast(F32), ALU.subtract).then_inc(lo_done, 1)

                def evacuate(it, n):
                    p, c = n // NC, n % NC
                    a, _ = chunks[c]
                    dve.wait_ge(out_done, it * PASSES * NC + n + 1)
                    if n >= 2:
                        dve.wait_ge(added, it * PASSES * NC + n - 1 + CREDIT)
                    elif experts > 1:
                        dve.wait_ge(added, it * PASSES * NC + CREDIT)
                    if factor and c == 0:
                        dve.wait_ge(factor_in[p], 16 * it + 16)
                    dst = out_sb[n % 2]
                    if out_bias is not None:
                        for m in range(KT):
                            ins = dve.scalar_tensor_tensor(out=dst[:, m, :], in0=out_ps[n % OB][:, m, 0:N],
                                                           scalar=out_bias[:, m:m + 1],
                                                           in1=factor[p][:, a:a + N], op0=ALU.add, op1=ALU.mult)
                    elif factor:
                        f = factor[p][:, a:a + N].unsqueeze(1).to_broadcast([P, KT, N])
                        ins = dve.tensor_tensor(dst[:, :, :], out_ps[n % OB][:, :, 0:N], f, ALU.mult)
                    else:
                        ins = dve.tensor_copy(dst[:, :, :], out_ps[n % OB][:, :, 0:N])
                    ins.then_inc(evacuated, 1)

                def body(it):
                    if gated:
                        for s in range(S + 1):
                            if s < S:
                                dve.wait_ge(gate_done, it * S + s + 1)
                                if s >= 2:
                                    dve.wait_ge(lo_done, it * S + s - 1)
                                    dve.wait_ge(hi_done, it * S + s - 1)
                                if is_half(s):
                                    dve.wait_ge(up_done, it * PASSES * NC + s // J + 1)
                                    dve.tensor_tensor(hidden[s % 2][0:64, :], up_half[:, :], gate_sb[s % 2][0:64, :],
                                                      ALU.mult).then_inc(hid_made, 1)
                                else:
                                    dve.tensor_tensor(hidden[s % 2][:, :], gu_ps[s % 3][:, 1, 0:N],
                                                      gate_sb[s % 2][:, :], ALU.mult).then_inc(hid_made, 1)
                            if s >= 1:
                                low(it, s - 1)
                            done = s + 1 - J - lag
                            if done >= 0 and done % J == 0:
                                evacuate(it, done // J)
                        for n in range(PASSES * NC):
                            if n * J + J + lag - 1 > S:
                                evacuate(it, n)
                    else:
                        n = 0
                        for s in range(S):
                            low(it, s)
                            done = s + 1 - J - lag
                            if done >= 0 and done % J == 0:
                                evacuate(it, done // J)
                                n += 1
                        for m in range(n, PASSES * NC):
                            evacuate(it, m)

                if experts > 1:
                    dve.memset(start[:, :], 0.0).then_inc(evacuated, CREDIT)
                turns(dve, body)


def attention(nc, name, *, q_scr, k_scr, v_scr, o_scr, m_scr, scale, toeplitz, consts):
    NB = 4
    UNITS = 8
    QA = 256
    QB = SP - QA
    QL = SP - 384
    A, BC = 512, QB + QL
    PW = A + 2 * BC + 4
    CREDIT = 2
    with Phase(nc, name) as ph:
        qst = [ph.sb(f"q{i}", [P, HG, SP], F32R) for i in range(NB)]
        kst = [ph.sb(f"k{i}", [P, HG, SP], F32R) for i in range(NB)]
        vst = [ph.sb(f"v{i}", [P, 5, HG, 32]) for i in range(NB)]
        prob = [ph.sb(f"prob{i}", [P, HG, PW]) for i in range(2)]
        mx = [ph.sb(f"mx{i}", [P, 32]) for i in range(2)]
        mneg = [ph.sb(f"mneg{i}", [P, 32], F32R) for i in range(2)]
        mxt = [ph.sb(f"mxt{i}", [P, 32], F32R) for i in range(2)]
        o_sb = [ph.sb(f"osb{i}", [P, SP]) for i in range(2)]
        warm = ph.sb("warm", [P, 3])
        max_ps = ph.ps("max", [P, 3 * 512])
        s_ps = ph.ps("s", [P, 3, 512])
        o_ps = ph.ps("o", [P, 2, 512])
        ident, flip, diag, tail, mask2 = (consts[n] for n in ("ident", "flip", "diag", "tail", "mask2"))
        q_in = [ph.sem(f"qin{i}") for i in range(NB)]
        dve_clear, pool_clear, max_mm, max_read, m_made, m_out, s_mm, exp_done, pv_done, o_copied, own = (
            ph.sem(n) for n in ("dclear", "pclear", "maxmm", "maxrd", "mmade", "mout", "smm", "exp", "pv", "ocp", "own"))
        m_in = [ph.sem(f"min{i}") for i in range(2)]
        o_out = [ph.sem(f"oout{i}") for i in range(2)]
        LOADS = 6
        ML = 2
        NU = B * H // HG

        def unit(u):
            return u // B, u % B

        with nc.Block() as block:
            @block.gpsimd
            def _(pool):
                for tile in [kst[0], kst[1]] + [t[i] for i in range(2, NB) for t in (qst, kst)]:
                    pool.memset(tile[:, :, :].bitcast(F32), 0.0).then_inc(pool_clear, 1)

            @block.sync
            def _(sp):
                def load_v(u):
                    hg, b = unit(u % NU)
                    i = u % NB
                    if u >= NB:
                        sp.wait_ge(pv_done, u - NB + 1)
                    cols = slice(hg * HG * 32, (hg + 1) * HG * 32)
                    sp.dma_start(vst[i][:, 0:4, :, :].rearrange("p n h c -> p n (h c)"),
                                 v_scr[b * SP:b * SP + 512, cols].rearrange("(n p) c -> p n c", p=P))\
                      .then_inc(q_in[i], 16)
                    sp.dma_start(vst[i][:, 4, :, :].rearrange("p h c -> p (h c)"),
                                 v_scr[(b + 1) * SP - P:(b + 1) * SP, cols]).then_inc(q_in[i], 16)

                def load_qk(u):
                    hg, b = unit(u % NU)
                    i = u % NB
                    if u < 2:
                        sp.wait_ge(dve_clear, u + 1)
                        sp.wait_ge(pool_clear, u + 1)
                    elif u < NB:
                        sp.wait_ge(pool_clear, 2 * u)
                    for scr, tiles, n, first in ((q_scr, qst, SEQ, HD), (k_scr, kst, SP, 0)):
                        src = scr[hg * HG:(hg + 1) * HG, :, b * SP:b * SP + n].rearrange("h r t -> r h t")
                        sp.dma_start(tiles[i][0:HD, :, 0:n].bitcast(F32), src[first:first + HD]).then_inc(q_in[i], 16)
                        sp.dma_start(tiles[i][HD:3 * HD + 1, :, 0:n].bitcast(F32), src).then_inc(q_in[i], 16)

                def maxima(u):
                    i, scr = u % NB, m_scr[u % 2]
                    sp.wait_ge(m_made, u + 1)
                    sp.dma_start(scr.rearrange("(r k) f -> k r f", k=4), mxt[u % 2][:, :].bitcast(F32)).then_inc(m_out, 16)
                    sp.wait_ge(m_out, 16 * (u + 1))
                    row = qst[i][3 * HD:3 * HD + 1, :, :].bitcast(F32)
                    sp.dma_start(row[:, :, 1:SEQ], scr[0:64].rearrange("(o h n) f -> o h (n f)", o=1, h=HG))\
                      .then_inc(m_in[u % 2], 16)
                    sp.dma_start(row[:, :, 0:1], scr.rearrange("(o r k) f -> o r k f", k=4, o=1)[:, 16:16 + HG, 0, 0:1],
                                 allow_slow_non_contiguous=True).then_inc(m_in[u % 2], 16)

                def store(u):
                    hg, b = unit(u)
                    sp.wait_ge(o_copied, u + 1 + 1)
                    sp.dma_start(o_scr[hg * P:(hg + 1) * P, b * SP:b * SP + SEQ], o_sb[u % 2][:, 0:SEQ])\
                      .then_inc(o_out[u % 2], 16)

                for u in range(3):
                    load_v(u)
                for u in range(3):
                    load_qk(u)
                maxima(0)
                maxima(1)
                for u in range(NU + 1):
                    if u >= 1:
                        store(u - 1)
                    if u + 3 < NU + 2:
                        load_v(u + 3)
                        load_qk(u + 3)
                    if toeplitz is not None and u % B == 0 and u < NU:
                        if u > 0:
                            sp.wait_ge(s_mm, 2 * HG * u)
                            sp.wait_ge(max_read, 2 * HG * u + CREDIT)
                        toeplitz["load"](sp, u // B + 1)
                    if u + 2 < NU:
                        if u >= 1:
                            sp.wait_ge(o_out[(u - 1) % 2], 16 * ((u - 1) // 2 + 1))
                        maxima(u + 2)
                for i in range(2):
                    sp.wait_ge(o_out[i], 16 * (NU // 2))

            @block.tensor
            def _(pe):
                def maxima_mm(it, u, h):
                    i = u % NB
                    if h == 0:
                        pe.wait_ge(q_in[i], it * (UNITS // NB) * 16 * LOADS + (u // NB + 1) * 16 * LOADS)
                    n = it * UNITS * HG + u * HG + h
                    pe.wait_ge(max_read, 2 * n - 1 + CREDIT)
                    pe.matmul(max_ps[:, 0:130], qst[i][:, h, 1:1 + P], kst[i][:, h, 0:130], start=True, stop=True)
                    pe.matmul(max_ps[:, 130:388], qst[i][:, h, 129:129 + P], kst[i][:, h, 0:258],
                              start=True, stop=True)
                    pe.matmul(max_ps[:, 388:390], qst[i][:, h, 0:P], kst[i][:, h, 0:2], start=True, stop=True)
                    pe.matmul(max_ps[:, 508:512], qst[i][:, h, 385:385 + P], kst[i][:, h, 0:4],
                              start=True, stop=True).then_inc(max_mm, 1)
                    pe.matmul(max_ps[:, 512:1024], qst[i][:, h, 385:385 + P], kst[i][:, h, 4:SP],
                              start=True, stop=True).then_inc(max_mm, 1)
                    pe.wait_ge(max_read, 2 * n + CREDIT)
                    pe.matmul(max_ps[:, 1024:1410], qst[i][:, h, 257:257 + P], kst[i][:, h, 0:386],
                              start=True, stop=True).then_inc(max_mm, 1)

                def scores(it, u, h):
                    i = u % NB
                    n = it * UNITS * HG + u * HG + h
                    slot = (u // B) % 2
                    if h == 0:
                        pe.wait_ge(m_in[u % 2], it * (UNITS // 2) * 16 * ML + (u // 2 + 1) * 16 * ML)
                        if toeplitz is not None and u % B == 0:
                            pe.wait_ge(toeplitz["loaded"][slot], 16 * toeplitz["n"] * (it + 1))

                    def products(bank, plan, last):
                        for j, (c, k0, q0, nq) in enumerate(plan):
                            mm = pe.matmul(s_ps[:, bank, c:c + nq], kst[i][:, h, k0:k0 + P], qst[i][:, h, q0:q0 + nq],
                                           start=(j == 0), stop=last, skip_group_check=True)
                        return mm

                    def biased(bank, plan):
                        for c, times, a, nq in plan:
                            for part in ("hi", "lo"):
                                src = toeplitz[part][slot][:, h:h + 1, a:a + nq]
                                mm = pe.matmul(s_ps[:, bank, c:c + times * nq], flip,
                                               src.to_broadcast([P, times, nq]) if times > 1 else src[:, 0, :],
                                               start=False, stop=(part == "lo"), skip_group_check=True)
                        return mm

                    whole = toeplitz is None
                    pe.wait_ge(exp_done, 2 * n - 1 + CREDIT)
                    mm = products(0, ((0, P, P, P), (P, 2 * P, QA, P), (QA, 0, 0, QA)), False)
                    if toeplitz is not None:
                        mm = biased(0, ((0, 3, 0, P), (3 * P, 1, P, P)))
                    else:
                        mm = pe.matmul(s_ps[:, 0, 0:3 * P], ident, diag[:, :].unsqueeze(1).to_broadcast([P, 3, P]),
                                       start=False, stop=True, skip_group_check=True)
                    mm.then_inc(s_mm, 1)
                    pe.wait_ge(exp_done, 2 * n + CREDIT)
                    products(1, ((0, 0, QA, QB), (QB, 3 * P, 384, QL), (BC, SP - P, 512, 4)), False)
                    mm = products(2, ((0, P, QA, QB), (QB, 2 * P, 384, QL)), whole)
                    if toeplitz is not None:
                        biased(1, ((0, 1, QA, QB), (QB, 1, 0, QL)))
                        for part in ("hi", "lo"):
                            pe.matmul(s_ps[:, 1, BC:BC + 4], flip, toeplitz["tail_" + part][slot][:, h, :], start=False,
                                      stop=(part == "lo"), skip_group_check=True)
                        mm = biased(2, ((0, 1, P, QB), (QB, 1, P, QL)))
                    else:
                        pe.matmul(s_ps[:, 1, QB:QB + P], ident, diag, start=False, stop=True, skip_group_check=True)
                        mm = pe.matmul(s_ps[:, 1, BC:BC + 4], ident, tail, start=False, stop=True,
                                       skip_group_check=True)
                    mm.then_inc(s_mm, 1)

                def values(it, u):
                    i = u % NB
                    pr = prob[u % 2]
                    n = it * UNITS + u
                    pe.wait_ge(exp_done, 2 * HG * (n + 1) + CREDIT)
                    pe.wait_ge(o_copied, n + 1)
                    plan = [(0, 0, 0, QA, 2 * P), (0, 1, P, P, 0),
                            (1, 0, 0, QB, A), (1, 1, 0, QB, A + BC), (1, 2, 0, P, P), (1, 2, P, QL, A + BC + QB),
                            (1, 3, P, QL, A + QB), (1, 4, QA, 4, A + 2 * BC)]
                    for bank, t, c0, w, src in plan:
                        for h in range(HG):
                            mm = pe.matmul(o_ps[32 * h:32 * h + 32, bank, c0:c0 + w], vst[i][:, t, h, :],
                                           pr[:, h, src:src + w], start=(t == 0), stop=(t == (1 if bank == 0 else 4)),
                                           skip_group_check=True)
                    mm.then_inc(pv_done, 1)

                for u in range(2):
                    for h in range(HG):
                        maxima_mm(0, u, h)
                for _ in range(WARM):
                    pe.matmul(s_ps[:, 0, :], ident, kst[0][:, 0, 0:512], start=True, stop=True)
                with pe.Fori(0, NU // UNITS) as it:
                    for u in range(UNITS + 1):
                        for h in range(HG):
                            if u < UNITS:
                                scores(it, u, h)
                                maxima_mm(it, u + 2, h)
                            if h == 0 and u >= 1:
                                values(it, u - 1)

            @block.scalar
            def _(act):
                def exps(it, u, h):
                    n = it * UNITS * HG + u * HG + h
                    pr = prob[u % 2]
                    if h == 0 and u >= 2:
                        act.wait_ge(pv_done, it * UNITS + u - 1)
                    act.wait_ge(s_mm, 2 * n + 1)
                    act.activation(pr[:, h, 0:A], s_ps[:, 0, :], ACT.Exp, scale=scale).then_inc(exp_done, 1)
                    act.wait_ge(s_mm, 2 * n + 2)
                    act.activation(pr[:, h, A:A + 2 * BC].rearrange("p (t q) -> p t q", t=2), s_ps[:, 1:3, 0:BC],
                                   ACT.Exp, scale=scale)
                    act.activation(pr[:, h, A + 2 * BC:PW], s_ps[:, 1, BC:BC + 4], ACT.Exp, scale=scale)\
                       .then_inc(exp_done, 1)

                def copy_out(it, u):
                    n = it * UNITS + u
                    act.wait_ge(pv_done, n + 1)
                    if u >= 2:
                        act.wait_ge(o_out[u % 2], it * (UNITS // 2) * 16 + u // 2 * 16)
                    act.activation(o_sb[u % 2][:, 0:QA], o_ps[:, 0, 0:QA], ACT.Copy)
                    act.activation(o_sb[u % 2][:, QA:SP], o_ps[:, 1, 0:QB], ACT.Copy).then_inc(o_copied, 1)

                act.wait_ge(dve_clear, 1)
                act.activation(warm[:, 1:2], warm[:, 0:1], ACT.Exp).then_inc(exp_done, CREDIT)
                act.activation(warm[:, 2:3], warm[:, 0:1], ACT.Copy).then_inc(o_copied, 1)
                with act.Fori(0, NU // UNITS) as it:
                    for u in range(UNITS + 1):
                        for h in range(HG):
                            if u < UNITS:
                                exps(it, u, h)
                            if h == 0 and u >= 1:
                                copy_out(it, u - 1)

            @block.vector
            def _(dve):
                def bias2(slot, h):
                    return toeplitz["max"][slot][:, h, :] if toeplitz is not None else mask2

                def maxima(it, u, h):
                    slot = (u // B) % 2
                    m = mx[u % 2]
                    n = it * UNITS * HG + u * HG + h
                    t2 = bias2(slot, h)
                    if toeplitz is not None and u % B == 0 and h == 0:
                        dve.wait_ge(toeplitz["loaded"][slot], 16 * toeplitz["n"] * (it + 1 + u // UNITS))

                    def piece(i, at):
                        a = 384 - 128 * i
                        w = SP if i == 3 else (i + 1) * P + 2
                        src = max_ps[:, at:at + w]
                        return dve.tensor_tensor_reduce(src, src, t2[:, a:a + w], 1.0, 3.0 * NEG, ALU.add, ALU.max,
                                                        m[:, 4 * h + i:4 * h + i + 1])

                    dve.wait_ge(max_mm, 3 * n + 1)
                    dve.tensor_tensor(m[0:1, 16 + h:17 + h], max_ps[0:1, 388:389], t2[0:1, 385:386], ALU.add)
                    piece(0, 0)
                    piece(1, 130)
                    dve.wait_ge(max_mm, 3 * n + 2)
                    dve.memset(m[:, 20 + 2 * h:21 + 2 * h], 0.0)
                    piece(3, 508).then_inc(max_read, 1)
                    dve.wait_ge(max_mm, 3 * n + 3)
                    dve.memset(m[:, 21 + 2 * h:22 + 2 * h], 0.0)
                    piece(2, 1024).then_inc(max_read, 1)

                def turn_maxima(it, u):
                    dve.wait_ge(max_read, 2 * HG * (it * UNITS + u + 1) + CREDIT)
                    dve.tensor_scalar(mneg[u % 2][:, :], mx[u % 2][:, :], -1.0, None, ALU.mult).then_inc(own, 1)
                    if u >= 2:
                        dve.wait_ge(m_in[u % 2], it * (UNITS // 2) * 16 * ML + u // 2 * 16 * ML)
                    dve.wait_ge(own, it * UNITS + u + 1)
                    dve.transpose(mxt[u % 2][:, :].bitcast(F32), mneg[u % 2][:, :].bitcast(F32)).then_inc(m_made, 1)

                dve.memset(warm[:, :], 0.0)
                for i in range(2):
                    dve.memset(mx[i][:, :], 0.0).then_inc(max_read, 1)
                dve.memset(qst[0][:, :, :].bitcast(F32), 0.0).then_inc(dve_clear, 1)
                dve.memset(qst[1][:, :, :].bitcast(F32), 0.0).then_inc(dve_clear, 1)
                dve.wait_ge(max_read, CREDIT)
                for u in range(2):
                    for h in range(HG):
                        maxima(0, u, h)
                    turn_maxima(0, u)
                with dve.Fori(0, NU // UNITS) as it:
                    for u in range(2, UNITS + 2):
                        for h in range(HG):
                            maxima(it, u, h)
                        turn_maxima(it, u)


def project(nc, name, *, w, w_swap, rope, bias, w_v, q_scr, k_scr, v_scr, before=None):
    STEPS = B * 4 * 2
    with Phase(nc, name) as ph:
        val = [ph.sb(f"val{i}", [P, QC]) for i in range(3)]
        t1 = [ph.sb(f"t1{i}", [P, QC]) for i in range(2)] if rope else None
        t2 = [ph.sb(f"t2{i}", [P, QC]) for i in range(2)] if rope else None
        hi = [ph.sb(f"hi{i}", [P, 2, QC], F32R) for i in range(3)]
        lo = [ph.sb(f"lo{i}", [P, 2, QC], F32R) for i in range(3)]
        v_sb = [ph.sb(f"v{i}", [P, H, 32]) for i in range(2)]
        ps = [ph.ps(f"qk{i}", [P, 2, 512]) for i in range(3)]
        ps_v = [ph.ps(f"vps{i}", [P, 512]) for i in range(2)]
        mm_done, val_done, half_done, hi_done, lo_done, v_mm, v_ready, v_copied, own = (
            ph.sem(n) for n in ("mm", "val", "half", "hi", "lo", "vmm", "vready", "vcopied", "own"))
        out_qk = [ph.sem(f"outqk{i}") for i in range(3)]
        out_v = [ph.sem(f"outv{i}") for i in range(2)]

        def tokens(s):
            return slice(s // 8 * SP + s % 2 * QC, s // 8 * SP + s % 2 * QC + QC)

        with nc.Block() as block:
            @block.tensor
            def _(pe):
                def qk(s):
                    m = s // 2 % 4
                    if s >= 3:
                        pe.wait_ge(val_done if not rope else half_done, s - 2)
                    for g, ww in enumerate((w, w_swap) if rope else (w,)):
                        kt, w_hi, w_lo, xh, xl = ww[m]
                        for k in range(kt):
                            mm = split_product(pe, ps[s % 3][:, g, 0:QC], w_hi(k), w_lo(k), xh[:, k, tokens(s)],
                                               xl[:, k, tokens(s)], k == 0, k == kt - 1)
                    mm.then_inc(mm_done, 1)

                def v(i):
                    kt, w_hi, w_lo, xh, xl = w_v
                    a = tile_start(i)
                    if i >= 2:
                        pe.wait_ge(v_copied, i - 1)
                    for k in range(kt):
                        mm = split_product(pe, ps_v[i % 2][:, 0:D], xh[:, k, a:a + P], xl[:, k, a:a + P], w_hi(k),
                                           w_lo(k), k == 0, k == kt - 1)
                    mm.then_inc(v_mm, 1)

                for s in range(STEPS):
                    qk(s)
                    if s % 2:
                        v(s // 2)
                v(NT - 1)

            @block.scalar
            def _(act):
                for s in range(STEPS):
                    m = s // 2 % 4
                    if not rope:
                        act.wait_ge(mm_done, s + 1)
                        if s >= 3:
                            act.wait_ge(lo_done, s - 2)
                        act.activation(val[s % 3][:, :], ps[s % 3][:, 0, 0:QC], ACT.Identity, bias=bias[:, m:m + 1])\
                           .then_inc(val_done, 1)
                    act.wait_ge(val_done, s + 1)
                    if s >= 6:
                        act.wait_ge(out_qk[s // 2 % 3], 32 * (s // 6))
                    act.activation(hi[s // 2 % 3][:, s % 2, :], val[s % 3][:, :], ACT.Copy).then_inc(hi_done, 1)

            @block.vector
            def _(dve):
                def low(s):
                    dve.wait_ge(hi_done, s + 1)
                    dve.tensor_tensor(lo[s // 2 % 3][:, s % 2, :], val[s % 3][:, :],
                                      hi[s // 2 % 3][:, s % 2, :].bitcast(F32), ALU.subtract).then_inc(lo_done, 1)

                def v(i):
                    dve.wait_ge(v_mm, i + 1)
                    dve.wait_ge(v_ready, 4)
                    if i >= 2:
                        dve.wait_ge(out_v[i % 2], 16 * (i // 2))
                    dve.tensor_copy(v_sb[i % 2][:, :, 0:HD], ps_v[i % 2][:, 0:D].rearrange("p (h d) -> p h d", d=HD))\
                       .then_inc(v_copied, 1)

                for s in range(STEPS + 1):
                    if rope and s < STEPS:
                        cos, sin = (t[:, s % 2 * QC:(s % 2 + 1) * QC] for t in rope)
                        dve.wait_ge(mm_done, s + 1)
                        if s >= 2:
                            dve.wait_ge(val_done, s - 1)
                        dve.tensor_tensor(t1[s % 2][:, :], ps[s % 3][:, 0, 0:QC], cos, ALU.mult)
                        dve.tensor_tensor(t2[s % 2][:, :], ps[s % 3][:, 1, 0:QC], sin, ALU.mult).then_inc(half_done, 1)
                    if s >= 1:
                        low(s - 1)
                        if (s - 1) % 2:
                            v((s - 1) // 2)
                v(NT - 1)

            @block.gpsimd
            def _(pool):
                step = Chain(pool, own)
                for i in range(2):
                    step(pool.memset(v_sb[i][:, :, :], 0.0))
                for i in range(2):
                    pool.memset(v_sb[i][:, :, HD:HD + 1], 1.0).then_inc(v_ready, 2)
                if rope:
                    for s in range(STEPS):
                        pool.wait_ge(half_done, s + 1)
                        if s >= 3:
                            pool.wait_ge(lo_done, s - 2)
                        pool.tensor_tensor(val[s % 3][:, :], t1[s % 2][:, :], t2[s % 2][:, :], ALU.add)\
                            .then_inc(val_done, 1)

            @block.sync
            def _(sp):
                if before is not None:
                    before(sp)
                for n in range(STEPS // 2):
                    b, m = n // 4, n % 4
                    sp.wait_ge(lo_done, 2 * n + 2)
                    heads = slice(m % 2 * 8, m % 2 * 8 + 8)
                    scr, parts = (q_scr, (lo, hi)) if m < 2 else (k_scr, (hi, lo))
                    for r, part in enumerate(parts):
                        sp.dma_start(scr[heads, r * HD:(r + 1) * HD, b * SP:(b + 1) * SP],
                                     part[n % 3][:, :, :].rearrange("p a t -> p (a t)").bitcast(F32))\
                          .then_inc(out_qk[n % 3], 16)
                    for i in ([n] if n < STEPS // 2 - 1 else [n, NT - 1]):
                        sp.wait_ge(v_copied, i + 1)
                        skip = i * P - tile_start(i)
                        sp.dma_start(v_scr[i * P:tile_start(i) + P, :],
                                     v_sb[i % 2][skip:P, :, :].rearrange("p h c -> p (h c)")).then_inc(out_v[i % 2], 16)
                for i in range(3):
                    sp.wait_ge(out_qk[i], 32 * ((STEPS // 2 - i + 2) // 3))
                for i in range(2):
                    sp.wait_ge(out_v[i], 16 * ((NT - i + 1) // 2))


def project_out(nc, name, *, warm, get_weights, o_scr, w, hT, spread, xn=None, xn_src=None, bias=None, v_bias=None):
    R = H * B
    with Phase(nc, name) as ph:
        o = ph.sb("o", [P, KT, T])
        o_hi = ph.sb("ohi", [P, KT, T], F32R)
        o_lo = ph.sb("olo", [P, KT, T], F32R)
        total, inverse, sel = ph.sb("total", [R, SP]), ph.sb("inverse", [R, SP]), ph.sb("sel", [R, B, D])
        ps = [ph.ps(f"y{i}", [P, 512]) for i in range(4)]
        inv_ps = [ph.ps(f"inv{i}", [P, KT, 512]) for i in range(2)]
        loaded = [ph.sem(f"in{b}") for b in range(B)]
        sums_in, cleared, w_ready, xn_in, inverted, inv_mm, divided, hi_done, lo_done, y_mm, y_done = (
            ph.sem(n) for n in ("sums", "clear", "w", "xn", "inverted", "inv", "divided", "hi", "lo", "mm", "y"))

        def tokens(c):
            return slice(c * QC, (c + 1) * QC)

        with nc.Block() as block:
            @block.sync
            def _(sp):
                heads = o_scr.rearrange("(h r) t -> h r t", r=32)
                sp.dma_start(total[:, 0:SEQ], heads[:, HD, :].rearrange("h (b t) -> h b t", b=B)[:, :, 0:SEQ])\
                  .then_inc(sums_in, 16)
                sp.dma_start(sel[:, :, :], spread).then_inc(sums_in, 16)
                get_weights[0](sp)
                for b in range(B):
                    for k in range(KT):
                        sp.dma_start(o[:, k, b * SP:b * SP + SEQ],
                                     heads[k * 8:(k + 1) * 8, 0:HD, b * SP:b * SP + SEQ]).then_inc(loaded[b], 16)
                    if b == 1 and xn is not None:
                        sp.wait_ge(xn_src[1], 16 * NCH)
                        sp.dma_start(xn[:, :, :], xn_src[0]).then_inc(xn_in, 16)

            @block.gpsimd
            def _(pool):
                pool.memset(total[:, SEQ:SP], 1.0)
                for b in range(B):
                    ins = pool.memset(o[:, :, b * SP + SEQ:(b + 1) * SP], 0.0)
                ins.then_inc(cleared, 1)
                get_weights[1](pool).then_inc(w_ready, 1)

            @block.tensor
            def _(pe):
                def spread_inverse(c):
                    if c >= 2:
                        pe.wait_ge(divided, c - 1)
                    b, a = c // 2, c % 2 * QC
                    for k in range(KT):
                        mm = pe.matmul(inv_ps[c % 2][:, k, 0:QC], sel[:, b, k * P:(k + 1) * P], inverse[:, a:a + QC],
                                       start=True, stop=True)
                    mm.then_inc(inv_mm, 1)

                for _ in range(WARM):
                    pe.matmul(ps[0][:, :], warm, warm.unsqueeze(1).to_broadcast([P, 4, P]), start=True, stop=True)
                pe.wait_ge(inverted, 1)
                for c in range(2):
                    spread_inverse(c)
                pe.wait_ge(w_ready, 1)
                for c in range(NQC):
                    pe.wait_ge(lo_done, c + 1)
                    for m in range(KT):
                        n = c * KT + m
                        if n >= 4:
                            pe.wait_ge(y_done, n - 3)
                        for k in range(KT):
                            mm = split_product(pe, ps[n % 4][:, 0:QC], w[0][:, k, m * P:(m + 1) * P],
                                               w[1][:, k, m * P:(m + 1) * P], o_hi[:, k, tokens(c)],
                                               o_lo[:, k, tokens(c)], k == 0, k == KT - 1)
                        mm.then_inc(y_mm, 1)
                    if c + 2 < NQC:
                        spread_inverse(c + 2)

            @block.scalar
            def _(act):
                act.wait_ge(w_ready, 1)
                for c in range(NQC):
                    act.wait_ge(divided, c + 1)
                    t = tokens(c)
                    if v_bias is None:
                        ins = act.activation(o_hi[:, :, t], o[:, :, t], ACT.Copy)
                    else:
                        for k in range(KT):
                            ins = act.activation(o_hi[:, k, t], o[:, k, t], ACT.Identity, bias=v_bias[:, k:k + 1])
                    ins.then_inc(hi_done, 1)

            @block.vector
            def _(dve):
                def divide(c):
                    if c % 2 == 0:
                        dve.wait_ge(loaded[c // 2], 16 * KT)
                    t = tokens(c)
                    dve.wait_ge(inv_mm, c + 1)
                    dve.tensor_tensor(o[:, :, t], o[:, :, t], inv_ps[c % 2][:, :, 0:QC], ALU.mult).then_inc(divided, 1)

                def low(c):
                    t = tokens(c)
                    dve.wait_ge(hi_done, c + 1)
                    if v_bias is None:
                        ins = dve.tensor_tensor(o_lo[:, :, t], o[:, :, t], o_hi[:, :, t].bitcast(F32), ALU.subtract)
                    else:
                        for k in range(KT):
                            ins = dve.scalar_tensor_tensor(out=o_lo[:, k, t], in0=o[:, k, t], scalar=v_bias[:, k:k + 1],
                                                           in1=o_hi[:, k, t].bitcast(F32), op0=ALU.add,
                                                           op1=ALU.subtract)
                    ins.then_inc(lo_done, 1)

                def add(c):
                    t = tokens(c)
                    for m in range(KT):
                        n = c * KT + m
                        dve.wait_ge(y_mm, n + 1)
                        if xn is not None:
                            ins = dve.scalar_tensor_tensor(out=xn[:, m, t], in0=ps[n % 4][:, 0:QC],
                                                           scalar=bias[:, m:m + 1], in1=xn[:, m, t], op0=ALU.add,
                                                           op1=ALU.add)
                        else:
                            ins = dve.tensor_tensor(hT[:, m, t], ps[n % 4][:, 0:QC], hT[:, m, t], ALU.add)
                        ins.then_inc(y_done, 1)

                dve.wait_ge(sums_in, 32)
                dve.wait_ge(cleared, 1)
                dve.reciprocal(inverse[:, :], total[:, :]).then_inc(inverted, 1)
                divide(0)
                divide(1)
                dve.wait_ge(w_ready, 1)
                low(0)
                if xn is not None:
                    dve.wait_ge(xn_in, 16)
                for c in range(NQC):
                    if c + 2 < NQC:
                        divide(c + 2)
                    if c + 1 < NQC:
                        low(c + 1)
                    add(c)


def latent(nc, name, x_hi, x_lo, w, lat):
    with Phase(nc, name) as ph:
        ps = [ph.ps(f"l{i}", [P, 512]) for i in range(2)]
        mm_done, read = ph.sem("mm"), ph.sem("read")
        with nc.Block() as block:
            @block.tensor
            def _(pe):
                for c in range(NCH):
                    if c >= 2:
                        pe.wait_ge(read, c - 1)
                    t = slice(c * CH, (c + 1) * CH)
                    for k in range(KT):
                        mm = split_product(pe, ps[c % 2][:, 0:CH], w[0][:, k, :], w[1][:, k, :], x_hi[:, k, t],
                                           x_lo[:, k, t], k == 0, k == KT - 1)
                    mm.then_inc(mm_done, 1)

            @block.scalar
            def _(act):
                for c in range(NCH):
                    act.wait_ge(mm_done, c + 1)
                    act.activation(lat[:, 0, c * CH:(c + 1) * CH], ps[c % 2][:, 0:CH], ACT.Copy).then_inc(read, 1)


def router_logits(pe, c, *, ps, xn, w, ne):
    for i in range(NT):
        a = tile_start(i)
        if c * CH < a + P <= (c + 1) * CH:
            for k in range(KT):
                pe.matmul(ps[:, i * 8:i * 8 + ne], xn[:, k, a:a + P], w[:, k, :], start=(k == 0), stop=(k == KT - 1))


def router(nc, name, *, ps, ne, identity, scr, gain=None, beside=None):
    with Phase(nc, name) as ph:
        ps_t = ph.ps("turned", [P, 2, 512])
        logit = ph.sb("logit", [P, NT, ne])
        prob = ph.sb("prob", [P, NT, ne])
        beats = ph.sb("beats", [P, NT, ne, ne])
        tied = ph.sb("tied", [P, NT, ne, ne])
        rank = ph.sb("rank", [P, NT, ne])
        one = ph.sb("one", [P, NT])
        two = ph.sb("two", [P, NT])
        best = ph.sb("best", [P, NT, 8])
        fac = ph.sb("fac", [P, 256])
        fac_t = ph.sb("fact", [P, 2, P])
        scaled, e_done, own, fac_done, turned, copied, out = (
            ph.sem(n) for n in ("scaled", "exp", "own", "fac", "turned", "copied", "out"))

        with nc.Block() as block:
            @block.tensor
            def _(pe):
                pe.wait_ge(fac_done, 1)
                for g in range(2):
                    mm = pe.transpose(ps_t[:, g, 0:P], fac[:, g * P:(g + 1) * P], identity)
                mm.then_inc(turned, 1)

            @block.scalar
            def _(act):
                act.wait_ge(scaled, 1)
                act.activation(prob[:, :, :], logit[:, :, :], ACT.Exp, scale=(-1.0 if gain is not None else 1.0))\
                   .then_inc(e_done, 1)

            @block.vector
            def _(dve):
                step = Chain(dve, own)
                each = [P, NT, ne]
                step(dve.memset(fac[:, :], 0.0))
                raw = ps[:, 0:NT * 8].rearrange("p (n e) -> p n e", e=8)[:, :, 0:ne]
                if gain is not None:
                    step(dve.tensor_tensor(rank[:, :, :], raw, gain.unsqueeze(1).to_broadcast(each), ALU.mult))
                    dve.tensor_scalar(logit[:, :, :], rank[:, :, :], -87.0, None, ALU.max).then_inc(scaled, 1)
                    dve.wait_ge(e_done, 1)
                    step(dve.tensor_scalar(rank[:, :, :], prob[:, :, :], 1.0, None, ALU.add))
                    step(dve.reciprocal(prob[:, :, :], rank[:, :, :]))
                    other = prob[:, :, :].unsqueeze(2).to_broadcast([P, NT, ne, ne])
                    this = prob[:, :, :].unsqueeze(3).to_broadcast([P, NT, ne, ne])
                    step(dve.tensor_tensor(tied[:, :, :, :], other, this, ALU.is_equal))
                    for n in range(ne):
                        ins = dve.memset(tied[:, :, n, n:ne], 0.0)
                    step(ins)
                    step(dve.tensor_tensor(beats[:, :, :, :], other, this, ALU.is_gt))
                    step(dve.tensor_tensor(beats[:, :, :, :], beats[:, :, :, :], tied[:, :, :, :], ALU.add))
                    step(dve.tensor_reduce(rank[:, :, :], beats[:, :, :, :], AX.X, ALU.add))
                    step(dve.tensor_scalar(rank[:, :, :], rank[:, :, :], 1.5, None, ALU.is_lt))
                    step(dve.tensor_tensor(rank[:, :, :], rank[:, :, :], prob[:, :, :], ALU.mult))
                    step(dve.tensor_reduce(one[:, :], rank[:, :, :], AX.X, ALU.add))
                    step(dve.reciprocal(two[:, :], one[:, :]))
                    f = fac[:, 0:NT * 8].rearrange("p (n e) -> p n e", e=8)
                    dve.memset(f[:, :, ne:8], 1.0)
                    dve.tensor_tensor(f[:, :, 0:ne], rank[:, :, :], two[:, :].unsqueeze(2).to_broadcast(each), ALU.mult)\
                       .then_inc(fac_done, 1)
                else:
                    step(dve.tensor_reduce(one[:, :], raw, AX.X, ALU.max))
                    dve.tensor_tensor(logit[:, :, :], raw, one[:, :].unsqueeze(2).to_broadcast(each), ALU.subtract)\
                       .then_inc(scaled, 1)
                    dve.wait_ge(e_done, 1)
                    step(dve.tensor_reduce(one[:, :], prob[:, :, :], AX.X, ALU.add))
                    step(dve.reciprocal(two[:, :], one[:, :]))
                    step(dve.tensor_tensor(rank[:, :, :], prob[:, :, :], two[:, :].unsqueeze(2).to_broadcast(each), ALU.mult))
                    for i in range(NT):
                        ins = dve.max(best[:, i, :], rank[:, i, :])
                    step(ins)
                    step(dve.tensor_tensor(one[:, :], best[:, :, 0], best[:, :, 1], ALU.add))
                    step(dve.reciprocal(two[:, :], one[:, :]))
                    step(dve.tensor_tensor(best[:, :, 0:2], best[:, :, 0:2], two[:, :].unsqueeze(2).to_broadcast([P, NT, 2]),
                                           ALU.mult))
                    dve.tensor_tensor(fac[:, 0:NT], best[:, :, 0], best[:, :, 1], ALU.add).then_inc(fac_done, 1)
                dve.wait_ge(turned, 1)
                dve.tensor_copy(fac_t[:, :, :], ps_t[:, :, 0:P]).then_inc(copied, 1)

            @block.gpsimd
            def _(pool):
                beside(pool)

            @block.sync
            def _(sp):
                sp.wait_ge(copied, 1)
                whole = T // P * P
                if gain is not None:
                    sp.dma_start(scr[:, 0:whole].rearrange("e (n t) -> n e t", t=P), fac_t[:, 0, :]).then_inc(out, 16)
                    sp.dma_start(scr[:, whole:T], fac_t[0:8, 1, P - (T - whole):P]).then_inc(out, 16)
                else:
                    sp.dma_start(scr[:, 0:whole].rearrange("e (n t) -> (e n) t", t=P), fac_t[0:NT - 1, 0, :]).then_inc(out, 16)
                    sp.dma_start(scr[:, whole:T], fac_t[NT - 1:NT, 0, P - (T - whole):P]).then_inc(out, 16)
                sp.wait_ge(out, 32)


COPIES = 32
RL = 648
RZ = 4


def bias_rows(ph, fwd_in, rev_in, scale, row_scr, fwd_scr, copied, rev_hi_scr, rev_lo_scr, fills):
    fwd, rev = ph.sb("fwd", [H, RL]), ph.sb("rev", [H, RL])
    hi, lo = ph.sb("rhi", [H, RL], F32R), ph.sb("rlo", [H, RL], F32R)
    filler = [ph.sb(f"fill{i}", [P, T * H // P]) for i in range(len(fills))]
    loaded, filled, hi_done, lo_done, out, own = (ph.sem("row" + n) for n in ("in", "filled", "hi", "lo", "out", "own"))

    def program(pool):
        step = Chain(pool, own)
        for tile, (_, value) in zip(filler, fills):
            pool.memset(tile[:, :], value).then_inc(filled, 1)
        pool.wait_ge(filled, len(fills))
        step(pool.memset(fwd[:, 0:RZ], 0.0))
        step(pool.memset(fwd[:, RZ + SEQ:RL], NEG))
        step(pool.memset(rev[:, 0:RL - RZ - SEQ], NEG))
        step(pool.memset(rev[:, RL - RZ:RL], 0.0))
        pool.wait_ge(loaded, 32)
        a = RL - RZ - SEQ
        step(pool.tensor_scalar(fwd[:, RZ:RZ + SEQ], fwd[:, RZ:RZ + SEQ], 1.0 / scale, None, ALU.mult))
        step(pool.tensor_scalar(rev[:, a:a + SEQ], rev[:, a:a + SEQ], 1.0 / scale, None, ALU.mult))
        pool.tensor_copy(hi[:, :], rev[:, :]).then_inc(hi_done, 1)
        pool.wait_ge(hi_done, 1)
        pool.tensor_tensor(lo[:, :], rev[:, :], hi[:, :].bitcast(F32), ALU.subtract).then_inc(lo_done, 1)
        pool.wait_ge(lo_done, 1)

    def start(sp):
        sp.dma_start(fwd[:, RZ:RZ + SEQ], fwd_in[:, 0:SEQ]).then_inc(loaded, 16)
        sp.dma_start(rev[:, RL - RZ - SEQ:RL - RZ], rev_in[:, 2 * SX - 1 - SEQ:2 * SX - 1]).then_inc(loaded, 16)

    def store(sp):
        sp.wait_ge(filled, len(fills))
        for tile, (scr, _) in zip(filler, fills):
            sp.dma_start(scr[:, 2 * HD, :].rearrange("h (c t) -> h c t", c=P // H), tile[:, :]).then_inc(out, 16)
        sp.wait_ge(lo_done, 1)
        sp.dma_start(row_scr, fwd[:, :]).then_inc(out, 16)
        sp.dma_start(rev_hi_scr, hi[:, :].bitcast(F32)).then_inc(out, 16)
        sp.dma_start(rev_lo_scr, lo[:, :].bitcast(F32)).then_inc(out, 16)
        sp.wait_ge(out, 16 * (3 + len(fills)))
        sp.dma_start(fwd_scr.rearrange("p h n -> p (h n)"),
                     bass.AP(tensor=row_scr.tensor, offset=row_scr.offset, ap=[[0, COPIES], [1, H * RL]])).then_inc(copied, 16)

    return start, program, store


def vit_tower(nc, A):
    def scratch(name, shape):
        return nc.dram_tensor(name, shape, F32).ap()

    q_scr, k_scr = scratch("q_scr", [H, 2 * HD + 1, T]), scratch("k_scr", [H, 2 * HD + 1, T])
    v_scr, o_scr = scratch("v_scr", [T, H * 32]), scratch("o_scr", [H * 32, T])
    m_scr = [scratch(f"m_scr{i}", [P, 32]) for i in range(2)]
    xn_scr = scratch("xn_scr", [P, KT, T])
    row_scr, rev_hi_scr, rev_lo_scr = (scratch(n, [H, RL]) for n in ("row_scr", "rev_hi_scr", "rev_lo_scr"))
    fwd_scr = scratch("fwd_scr", [COPIES, H, RL])
    fac0_scr, fac1_scr = scratch("fac0_scr", [8, T]), scratch("fac1_scr", [1, T])

    def rows(ap):
        return ap.rearrange("(k p) n -> p k n", p=P)

    Phase.used.clear()
    with Phase(nc, "all") as top:
        hT = top.sb("hT", [P, KT, T])
        one_c = top.sb("mean", [P, P])
        one64 = top.sb("mean64", [P, P])
        identf = top.sb("identf", [P, P])
        ones = top.sb("ones", [P, P])
        eps = top.sb("eps", [P, 1])
        masks_raw = top.sb("masks_raw", [P, 2 * P + 4])
        masks = {name: top.sb(name, [P, n], F32R)[:, :] for name, n in
                 (("ident", P), ("diag", P), ("flip", P), ("tail", 4))}
        norm = (one_c[:, :], ones[:, :], identf[:, :], eps[:, 0:1])
        norm64 = (one64[:, :], ones[:, :], identf[:, :], eps[:, 0:1])
        masks["mask2"] = top.sb("mask2", [P, SP])[:, :]
        got, copied, spilled = top.sem("got"), top.sem("copied"), top.sem("spilled")

        def init_loads(sp):
            sp.dma_start(identf[:, :], A["c_ident"]).then_inc(got, 16)
            sp.dma_start(masks_raw[:, :], A["c_masks"]).then_inc(got, 16)
            sp.dma_start(masks["mask2"], A["c_mask2"]).then_inc(got, 16)
            for b in range(B):
                sp.dma_start(hT[:, :, b * SP:b * SP + 1], A["cls"].unsqueeze(2), allow_slow_non_contiguous=True)\
                  .then_inc(got, 16)
            sp.wait_ge(got, 16 * (B + 3))

        def init_memsets(dve):
            for b in range(B):
                dve.memset(hT[:, :, b * SP + SEQ:(b + 1) * SP], 0.0)
            dve.memset(one_c[:, :], 1.0 / D)
            dve.memset(ones[:, :], 1.0)
            dve.memset(one64[0:64, :], 1.0 / 64)
            dve.memset(one64[64:P, :], 0.0)
            dve.memset(eps[:, :], EPS)
            dve.wait_ge(got, 16 * (B + 3))
            dve.tensor_copy(masks["ident"], identf[:, :])
            for n, name in enumerate(("diag", "flip")):
                dve.tensor_copy(masks[name], masks_raw[:, n * P:(n + 1) * P])
            dve.tensor_copy(masks["tail"], masks_raw[:, 2 * P:])

        with Phase(nc, "tok") as ph:
            raw = ph.sb("raw", [P, KT, B * SX])
            hi, lo = ph.sb("hi", [P, KT, B * SX], F32R), ph.sb("lo", [P, KT, B * SX], F32R)
            x = A["x0"].rearrange("(k p) n -> p k n", p=P)
            weights = FfnWeights(ph, 4, False, True, 1)

            r1, (h1, l1), r2, (h2, l2) = weights.raw1, weights.w1[0], weights.raw2, weights.w2[0]
            part = [slice(b * SX, (b + 1) * SX) for b in range(B)]
            split_loads(nc, "toks", [(r1[:, :, 0:512], rows(A["w0"]), h1[:, :, 0:512], l1[:, :, 0:512]),
                                     (raw[:, :, part[0]], x[:, :, part[0]], hi[:, :, part[0]], lo[:, :, part[0]]),
                                     (r1[:, :, 512:1024], rows(A["w1"]), h1[:, :, 512:1024], l1[:, :, 512:1024]),
                                     (r2[:, :, :], rows(A["wo"]), h2[:, :, :], l2[:, :, :])]
                        + [(raw[:, :, t], x[:, :, t], hi[:, :, t], lo[:, :, t]) for t in part[1:]],
                        (init_loads, init_memsets))
            gated_ffn(nc, "tokf", weights=weights, x_hi=hi, x_lo=lo, chunks=[(b * SX, SX) for b in range(B)], J=4,
                      half=False, gated=True, func=ACT.Relu, experts=1, w_mult=None, lag=2, load=None,
                      finish=lambda c: hT[:, :, c * SP + 1:c * SP + 1 + SX], add=False)

        with Phase(nc, "L0") as l0:
            t_hi, t_lo, t_max = ([l0.sb(f"t{n}{i}", [P, HG, SP], dt) for i in range(2)]
                                 for n, dt in (("hi", F32R), ("lo", F32R), ("mx", F32)))
            tail_hi, tail_lo = ([l0.sb(f"tail{n}{i}", [P, HG, 4], F32R) for i in range(2)] for n in "hl")
            t_sem, tails_clear = [l0.sem(f"t{i}") for i in range(2)], l0.sem("tails")

            def load_bias(sp, hg):
                i, hg = hg % 2, hg % (H // HG)

                def window(scr, first, n, step=1, n_rows=P):
                    return bass.AP(tensor=scr.tensor, offset=scr.offset + hg * HG * RL + first,
                                   ap=[[step, n_rows], [RL, HG], [1, n]])

                own = RL - 1 - RZ - SX - (P - 1)
                for dst, src in ((t_hi[i][:, :, :].bitcast(F32), window(rev_hi_scr, own, SP)),
                                 (t_lo[i][:, :, :].bitcast(F32), window(rev_lo_scr, own, SP)),
                                 *((t_max[i][r:r + COPIES, :, :], window(fwd_scr, RZ + P - 1 - r, SP, H * RL - 1, COPIES))
                                   for r in range(0, P, COPIES)),
                                 (tail_hi[i][0:4, :, :].bitcast(F32), window(rev_hi_scr, own + P - 4, 4, n_rows=4)),
                                 (tail_lo[i][0:4, :, :].bitcast(F32), window(rev_lo_scr, own + P - 4, 4, n_rows=4))):
                    sp.dma_start(dst, src).then_inc(t_sem[i], 16)

            with Phase(nc, "L0p") as ph:
                xn = ph.sb("xn", [P, KT, T])
                hi, lo = ph.sb("hi", [P, KT, T], F32R), ph.sb("lo", [P, KT, T], F32R)
                wr = ph.sb("wraw", [P, KT, 3 * D])
                wh, wl = ph.sb("wh", [P, KT, 3 * D], F32R), ph.sb("wl", [P, KT, 3 * D], F32R)
                bias = ph.sb("bias", [P, 4])
                bias_load, bias_program, bias_store = bias_rows(
                    ph, A["rpb_fwd"], A["rpb_rev"], 1.0 / 16, row_scr, fwd_scr, copied, rev_hi_scr, rev_lo_scr,
                    ((q_scr, 0.0), (k_scr, 1.0)))
                w_load, w_program, _ = preload(ph, "w", [(wr[:, :, :], rows(A["wqkv"]), wh[:, :, :], wl[:, :, :]),
                                                         (bias[:, :], A["bqk"], None, None)])

                def loads(sp):
                    bias_load(sp)
                    w_load(sp)
                    bias_store(sp)

                def splits(pool):
                    for i in range(2):
                        pool.memset(tail_hi[i][:, :, :].bitcast(F32), NEG).then_inc(tails_clear, 1)
                        pool.memset(tail_lo[i][:, :, :].bitcast(F32), 0.0).then_inc(tails_clear, 1)
                    bias_program(pool)
                    w_program(pool)

                layer_norm(nc, "L0n", hT, norm, xn=xn, hi=hi, lo=lo, spill=(xn_scr, spilled), beside=(loads, splits))

                def part(t, m, n=P):
                    return lambda k: t[:, k, m:m + n]

                def before(sp):
                    sp.wait_ge(spilled, 16 * NCH)
                    sp.wait_ge(copied, 16)
                    sp.wait_ge(tails_clear, 4)
                    load_bias(sp, 0)

                w = [(KT, part(wh, m * P), part(wl, m * P), hi, lo) for m in range(4)]
                project(nc, "L0q", w=w, w_swap=None, rope=None, bias=bias,
                        w_v=(KT, part(wh, 2 * D, D), part(wl, 2 * D, D), hi, lo), q_scr=q_scr, k_scr=k_scr, v_scr=v_scr,
                        before=before)

            attention(nc, "L0t", q_scr=q_scr, k_scr=k_scr, v_scr=v_scr, o_scr=o_scr, m_scr=m_scr, scale=1.0 / 16,
                      toeplitz={"hi": t_hi, "lo": t_lo, "max": t_max, "tail_hi": tail_hi, "tail_lo": tail_lo,
                                "loaded": t_sem, "n": 4 + P // COPIES, "load": load_bias}, consts=masks)

        with Phase(nc, "L0o") as ph:
            xn = ph.sb("xn", [P, KT, T])
            wr = ph.sb("wraw", [P, KT, D])
            w = [ph.sb(f"w{q}", [P, KT, D], F32R) for q in "hl"]
            vec = ph.sb("vec", [P, 4, KT])
            get_weights = preload(ph, "w", [(wr[:, :, :], rows(A["wproj"]), w[0][:, :, :], w[1][:, :, :]),
                                            (vec[:, :, :], A["vec0"], None, None)])
            project_out(nc, "L0oo", warm=masks["ident"], get_weights=get_weights,
                        o_scr=o_scr, w=w, hT=hT, spread=A["c_spread"], xn=xn, xn_src=(xn_scr, spilled),
                        bias=vec[:, 0, :], v_bias=vec[:, 3, :])
            layer_norm(nc, "L0on", xn, norm, xn=xn, gain=vec[:, 1, :], shift=vec[:, 2, :], add_to=hT)

        with Phase(nc, "E") as ph:
            hi, lo = ph.sb("hi", [P, KT, T], F32R), ph.sb("lo", [P, KT, T], F32R)
            weights = FfnWeights(ph, 6, True, True, NEXP0 + 1)

            def load_expert(e, r1, r2):
                return [(r1[:, :, :], rows(A["gu"][e])), (r2[:, 0:5, :], rows(A["down"][e, 0:640, :])),
                        (r2[0:64, 5, :], A["down"][e, 640:HID0, :])]

            with Phase(nc, "E1") as p2:
                xn = p2.sb("xn", [P, KT, T])
                wr = p2.sb("wr", [P, KT, NEXP0])
                gain = p2.sb("gain", [P, NEXP0])
                load, split, split_rest, loaded = weights.first(ph, load_expert, half=True, more=[
                    (wr[:, :, :], rows(A["wr0"]), None, None), (gain[:, :], A["rb"].to_broadcast([P, NEXP0]), None, None)])
                logits = p2.ps("logits", [P, 512])

                def use(pe, c):
                    if c == 0:
                        loaded(pe)
                    router_logits(pe, c, ps=logits, xn=xn, w=wr, ne=NEXP0)

                layer_norm(nc, "E1n", hT, norm, xn=xn, hi=hi, lo=lo,
                           beside=(load, split), use=use)
                router(nc, "E1r", ps=logits, ne=NEXP0, identity=identf[:, :], scr=fac0_scr, gain=gain[:, :],
                       beside=split_rest)

            gated_ffn(nc, "Ef", weights=weights, x_hi=hi, x_lo=lo,
                      chunks=[(c * CH, CH) for c in range(NCH)], J=6, half=True, gated=True,
                      func=ACT.Silu, experts=NEXP0 + 1, w_mult=lambda e: fac0_scr[e:e + 1, :].to_broadcast([P, T]), lag=3,
                      load=load_expert, finish=lambda c: hT[:, :, c * CH:(c + 1) * CH])

        clear_semaphores(nc)

        with Phase(nc, "L1p") as ph:
            xn = ph.sb("xn", [P, KT, T])
            hi, lo = ph.sb("hi", [P, KT, T], F32R), ph.sb("lo", [P, KT, T], F32R)
            lat, lat_hi, lat_lo = (ph.sb(f"lat{i}", [P, 1, T], dt) for i, dt in enumerate((F32, F32R, F32R)))
            wqr, wq = ph.sb("wqr", [P, KT, 2 * D]), [ph.sb(f"wq{q}", [P, KT, 2 * D], F32R) for q in "hl"]
            wlr, wl = ph.sb("wlr", [P, KT, P]), [ph.sb(f"wl{q}", [P, KT, P], F32R) for q in "hl"]
            wkr, wk = ph.sb("wkr", [P, 1, 3 * D]), [ph.sb(f"wk{q}", [P, 1, 3 * D], F32R) for q in "hl"]
            vec = ph.sb("vec", [P, 2])
            cos, sin = ph.sb("cos", [P, SP]), ph.sb("sin", [P, SP])
            layer_norm(nc, "L1n", hT, norm, xn=xn, hi=hi, lo=lo, beside=preload(ph, "w", [
                (wlr[:, :, 0:64], rows(A["wdkv"]), None, None), (wlr[:, :, :], None, wl[0][:, :, :], wl[1][:, :, :]),
                (wkr[0:64, 0, :], A["wkv1"], None, None), (wkr[:, :, :], None, wk[0][:, :, :], wk[1][:, :, :]),
                (wqr[:, :, :], rows(A["wq1"]), wq[0][:, :, :], wq[1][:, :, :]),
                (vec[0:64, :], A["vec1"], None, None),
                (cos[:, :], A["c_cos"], None, None), (sin[:, :], A["c_sin"], None, None)],
                clear=(wlr[:, :, 64:P], wkr[64:P, :, :], vec[64:P, :])))
            latent(nc, "L1l", hi, lo, wl, lat)
            layer_norm(nc, "L1ln", lat, norm64, xn=lat, hi=lat_hi, lo=lat_lo, gain=vec[:, 0:1],
                       shift=vec[:, 1:2], width=1)

            def part(t, m, n=P):
                return lambda k: t[:, k, m:m + n]

            def four(q0, k0):
                return ([(KT, part(wq[0], q0 + m * P), part(wq[1], q0 + m * P), hi, lo) for m in range(2)]
                        + [(1, part(wk[0], k0 + m * P), part(wk[1], k0 + m * P), lat_hi, lat_lo) for m in range(2)])

            project(nc, "L1q", w=four(0, 0), w_swap=four(D, D),
                    rope=(cos, sin), bias=None, w_v=(1, part(wk[0], 2 * D, D), part(wk[1], 2 * D, D), lat_hi, lat_lo),
                    q_scr=q_scr, k_scr=k_scr, v_scr=v_scr)

        attention(nc, "L1t", q_scr=q_scr, k_scr=k_scr, v_scr=v_scr, o_scr=o_scr, m_scr=m_scr, scale=1.0 / 4,
                  toeplitz=None, consts=masks)

        with Phase(nc, "L1o") as ph:
            wr = ph.sb("wraw", [P, KT, D])
            w = [ph.sb(f"w{q}", [P, KT, D], F32R) for q in "hl"]
            get_weights = preload(ph, "w", [(wr[:, :, :], rows(A["wo1"]), w[0][:, :, :], w[1][:, :, :])])
            project_out(nc, "L1oo", warm=masks["ident"], get_weights=get_weights,
                        o_scr=o_scr, w=w, hT=hT, spread=A["c_spread"])

        with Phase(nc, "F") as ph:
            hi, lo = ph.sb("hi", [P, KT, T], F32R), ph.sb("lo", [P, KT, T], F32R)
            b1, b2 = ph.sb("b1", [P, FF1 // P]), ph.sb("b2", [P, KT])
            weights = FfnWeights(ph, FF1 // P, False, False, 1)

            def load_ffn(e, r1, r2):
                return [(r1[:, :, :], rows(A["ff1"])), (r2[:, :, :], rows(A["ff2"]))]

            with Phase(nc, "F1") as p2:
                xn = p2.sb("xn", [P, KT, T])
                wr = p2.sb("wr", [P, KT, NEXP1])
                load, split, split_rest, loaded = weights.first(ph, load_ffn, more=[
                    (wr[:, :, :], rows(A["wr1"]), None, None), (b1[:, :], A["b1"], None, None),
                    (b2[:, :], A["b2"], None, None)])
                logits = p2.ps("logits", [P, 512])

                def use(pe, c):
                    if c == 0:
                        loaded(pe)
                    router_logits(pe, c, ps=logits, xn=xn, w=wr, ne=NEXP1)

                layer_norm(nc, "F1n", hT, norm, xn=xn, hi=hi, lo=lo,
                           beside=(load, split), use=use)
                router(nc, "F1r", ps=logits, ne=NEXP1, identity=identf[:, :], scr=fac1_scr,
                       beside=split_rest)
            gated_ffn(nc, "Ff", weights=weights, x_hi=hi, x_lo=lo,
                      chunks=[(c * CH, CH) for c in range(NCH)], J=FF1 // P, half=False,
                      gated=False, func=ACT.Gelu_apprx_tanh, experts=1,
                      w_mult=lambda e: fac1_scr.to_broadcast([P, T]), lag=3, load=None,
                      finish=lambda c: hT[:, :, c * CH:(c + 1) * CH], up_bias=b1, out_bias=b2,
                      output=lambda c: A["out"].rearrange("(k p) t -> p k t", p=P)[:, :, c * CH:(c + 1) * CH])


def constants():
    import numpy as np
    p = np.arange(P)
    half = HD // 2
    inv = (1.0 / 10000.0 ** (np.arange(half, dtype=np.float32) / np.float32(half))).astype(np.float32)
    ang = np.arange(SP, dtype=np.float32)[None, :] * inv[:, None]
    row = p % HD
    sign = np.where(row < half, -1.0, 1.0)[:, None]
    diag = np.where(p[:, None] > p[None, :], NEG, 0.0)
    j = np.arange(4)[None, :]
    tail = np.where((p[:, None] < P - 4) | (p[:, None] - (P - 4) > j), NEG, 0.0)
    return {
        "c_ident": np.eye(P, dtype=np.float32),
        "c_cos": np.cos(ang.astype(np.float64))[row % half].astype(np.float32),
        "c_sin": (np.sin(ang.astype(np.float64))[row % half] * sign).astype(np.float32),
        "c_masks": np.concatenate([diag, np.eye(P)[::-1], tail], 1).astype(np.float32),
        "c_mask2": np.where(np.arange(SP)[None, :] > 385 + p[:, None], NEG, 0.0).astype(np.float32),
        "c_spread": (np.arange(H * B)[:, None, None] == (np.arange(D)[None, None] // HD * B
                                                          + np.arange(B)[None, :, None])).astype(np.float32),
    }


def kernel(**inputs):
    import numpy as np
    import concourse.bacc as bacc
    from concourse.bass_utils import run_bass_kernel_spmd as run

    a = {k: np.asarray(v) for k, v in inputs.items()}
    n0, nh = HID0 // P * P, H

    def gate_up(g, u):
        return np.concatenate([g[..., :n0], u[..., :n0], g[..., n0:], u[..., n0:]], -1)

    def swapped(w):
        return w.reshape(-1, nh, 2, HD // 2)[:, :, ::-1].reshape(-1, D)

    qkv, wb = a["L0_attn_W_w"], a["L0_attn_W_b"]
    wq, wuk = a["L1_attn_W_q"], a["L1_attn_W_uk"]
    arrays = {
        "x0": a["x"][..., 0].transpose(2, 0, 1).reshape(D, B * SX),
        "cls": a["cls_tok"].reshape(KT, P).T,
        "w0": a["L0_tok_W0"].T, "w1": a["L0_tok_W1"].T, "wo": a["L0_tok_Wo"].T,
        "wqkv": qkv.T, "bqk": wb[:2 * D].reshape(4, P).T,
        "rpb_fwd": a["L0_attn_rpb"].T, "rpb_rev": a["L0_attn_rpb"][::-1].T,
        "wproj": a["L0_attn_proj_w"].T,
        "vec0": np.stack([v.reshape(KT, P).T for v in (a["L0_attn_proj_b"], a["L0_attn_ln_g"], a["L0_attn_ln_b"],
                                                       wb[2 * D:])], 1),
        "wr0": a["L0_ffn_Wr"], "rb": a["L0_ffn_routing_bias"][None],
        "gu": np.concatenate([gate_up(a["L0_ffn_routed_gate"], a["L0_ffn_routed_up"]),
                              gate_up(a["L0_ffn_shared_gate"], a["L0_ffn_shared_up"])[None]]),
        "down": np.concatenate([a["L0_ffn_routed_down"], a["L0_ffn_shared_down"][None]]),
        "wq1": np.concatenate([wq, swapped(wq)], 1), "wdkv": a["L1_attn_W_dkv"],
        "wkv1": np.concatenate([wuk, swapped(wuk), a["L1_attn_W_uv"]], 1),
        "vec1": np.stack([a["L1_attn_ln_gamma"], a["L1_attn_ln_beta"]], 1),
        "wo1": a["L1_attn_W_o"], "wr1": a["L1_ffn_router_w"], "ff1": a["L1_ffn_w1"], "ff2": a["L1_ffn_w2"],
        "b1": a["L1_ffn_b1"].reshape(FF1 // P, P).T, "b2": a["L1_ffn_b2"].reshape(KT, P).T,
        **constants(),
    }
    arrays = {f"in_{k}": np.ascontiguousarray(v) for k, v in arrays.items()}
    nc = bacc.Bacc("TRN2", target_bir_lowering=False, num_devices=1)
    aps = {k[3:]: nc.dram_tensor(k, v.shape, F32, kind="ExternalInput").ap() for k, v in arrays.items()}
    aps["out"] = nc.dram_tensor("out_dram", [D, T], F32, kind="ExternalOutput").ap()
    vit_tower(nc, aps)
    got = run(nc, [arrays], core_ids=[0]).results[0]["out_dram"]
    return np.ascontiguousarray(got.reshape(D, B, SP)[:, :, :SEQ].transpose(1, 2, 0))
```
